# Optimizing a Trainium2 kernel written in Bass

```python
import numpy as np
import jax
import jax.numpy as jnp

def _softmax(x, axis=-1):
    return jax.nn.softmax(x, axis=axis)

def _gelu(x):
    return jax.nn.gelu(x, approximate=True)

def _silu(x):
    return jax.nn.silu(x)

def _sigmoid(x):
    return jax.nn.sigmoid(x)

def _layernorm(x, axis=-1, eps=1e-05):
    m = jnp.mean(x, axis=axis, keepdims=True)
    v = jnp.var(x, axis=axis, keepdims=True)
    return (x - m) / jnp.sqrt(v + eps)

def _scatter_add(tgt, idx, src, axis=0):
    return tgt.at[idx].add(src)

def _segment_sum(src, seg, n):
    return jax.ops.segment_sum(src, seg, n)
kernel_name = 'mk_flamingo_gated_d2_seqx_r4_f5c8e8'

def setup_inputs(seed: int=0):
    np.random.seed(seed)
    _w = jnp.asarray

    def _rec_inputs():
        import jax
        import jax.numpy as jnp
        _rk = jax.random.key(seed)
        x = -0.0002928 + 1 * jax.random.normal(jax.random.fold_in(_rk, 1), (4, 512, 256), jnp.float32)
        _lenS = 512 - jax.random.randint(jax.random.fold_in(_rk, 7), (4,), 0, max(1, 512 // 4) + 1, jnp.int32)
        _lenS2 = 512 - jax.random.randint(jax.random.fold_in(_rk, 8), (4,), 0, max(1, 512 // 4) + 1, jnp.int32)
        _ctx_1024P = jax.random.normal(jax.random.fold_in(_rk, 11), (4, 16, 256), jnp.float32)
        _ctx_1024c = jax.random.dirichlet(jax.random.fold_in(_rk, 511), 0.3 * jnp.ones((16,), jnp.float32), (4, 512))
        _ctx_1024t = jnp.einsum('bsk,bkd->bsd', _ctx_1024c, _ctx_1024P)
        _ctx_1024t = _ctx_1024t * jax.lax.rsqrt(jnp.mean(jnp.square(_ctx_1024t)) + 1e-12) * 0.953939
        ctx_1024 = -1.39393e-06 + 0.999914 * (_ctx_1024t + 0.3 * jax.random.normal(jax.random.fold_in(_rk, 611), (4, 512, 256), jnp.float32))
        _validS = jnp.arange(512)[None, :] < _lenS[:, None]
        _validS2 = jnp.arange(512)[None, :] < _lenS2[:, None]
        _causal = jnp.tril(jnp.ones((512, 512), dtype=bool))
        mask_BxS2_bk1 = jnp.broadcast_to(_validS2[:, :], (4, 512))
        mask_SxS2_fk1 = jnp.where(jnp.broadcast_to(_validS2[0:1, :], (512, 512)), 1.0, 0.0).astype(jnp.float32)
        _g = jax.random.normal(jax.random.fold_in(_rk, 9001), (2, 2), jnp.float32)
        _g = jnp.sign(_g) * jnp.maximum(jnp.abs(_g), 1.0) + (_g == 0) * 1.0
        g_xattn = _g[0]
        g_ffn = _g[1]
        return (x, ctx_1024, mask_BxS2_bk1, mask_SxS2_fk1, g_xattn, g_ffn)
    x, ctx_1024, mask_BxS2_bk1, mask_SxS2_fk1, g_xattn, g_ffn = _rec_inputs()

    def _L0_xattn_setup():
        import jax, jax.numpy as jnp
        import numpy as np
        B, S, D, H = (2, 512, 256, 16)
        DH = D // H
        key = jax.random.key(seed)
        ks = jax.random.split(key, 16)
        inp = {'query': jax.random.normal(ks[0], (B, S, D), jnp.float32), 'key': jax.random.normal(ks[1], (B, S, D), jnp.float32), 'value': jax.random.normal(ks[2], (B, S, D), jnp.float32), 'key_padding_mask': jnp.arange(S)[None, :] < jnp.array([S, S - 64])[:, None], 'relative_bias': jax.random.normal(ks[3], (1, H, S, S), jnp.float32) * 0.1}
        sc = 1.0 / np.sqrt(D)
        for i, n in enumerate(['q', 'k', 'v', 'o']):
            inp[f'W{n}'] = jax.random.normal(ks[4 + 2 * i], (D, D), jnp.float32) * sc
            inp[f'b{n}'] = jnp.zeros((D,), jnp.float32)
        return inp
    _L0_xattn_all = _L0_xattn_setup()
    _L0_xattn_in = {k: v for k, v in _L0_xattn_all.items() if k in ('relative_bias', 'Wq', 'bq', 'Wk', 'bk', 'Wv', 'bv', 'Wo', 'bo')}
    del _L0_xattn_all

    def _L0_ffn_setup():
        import jax, jax.numpy as jnp
        import numpy as np
        B, S, H = (8, 1024, 256)
        NAV = 128
        E = 8
        F = 2 * H
        key = jax.random.key(seed)
        ks = jax.random.split(key, 12)

        def w(k, shape, fan_in):
            return jax.random.normal(k, shape, dtype=jnp.float32) / np.sqrt(fan_in)
        return {'hidden_states': jax.random.normal(ks[0], (B, S, H), dtype=jnp.float32), 'Wp1': w(ks[1], (H, NAV), H), 'bp1': jnp.zeros((NAV,), jnp.float32), 'Wp2': w(ks[2], (NAV, E), NAV), 'bp2': jnp.zeros((E,), jnp.float32), 'W1': w(ks[3], (E, H, F), H), 'b1': jnp.zeros((E, F), jnp.float32), 'W2': w(ks[4], (E, F, H), F), 'b2': jnp.zeros((E, H), jnp.float32), 'Wo': w(ks[5], (H, H), H), 'bo': jnp.zeros((H,), jnp.float32)}
    _L0_ffn_all = _L0_ffn_setup()
    _L0_ffn_in = {k: v for k, v in _L0_ffn_all.items() if k in ('Wp1', 'bp1', 'Wp2', 'bp2', 'W1', 'b1', 'W2', 'b2', 'Wo', 'bo')}
    del _L0_ffn_all

    def _L1_xattn_setup():
        import jax, jax.numpy as jnp
        import numpy as np
        B, S, D, H = (2, 512, 256, 16)
        DEPTH = D // H

        def _split_heads(x):
            b, s, _ = x.shape
            return x.reshape(b, s, H, DEPTH).transpose(0, 2, 1, 3)
        key = jax.random.key(seed)
        ks = jax.random.split(key, 12)
        inp = {'xq': jax.random.normal(ks[0], (B, S, D), jnp.float32), 'xk': jax.random.normal(ks[1], (B, S, D), jnp.float32), 'xv': jax.random.normal(ks[2], (B, S, D), jnp.float32), 'mask': jnp.triu(jnp.ones((S, S), jnp.float32), k=1)}
        scale = 1.0 / np.sqrt(D)
        inp['Wq'] = jax.random.normal(ks[3], (D, D), jnp.float32) * scale
        inp['bq'] = jnp.zeros((D,), jnp.float32)
        inp['Wk'] = jax.random.normal(ks[4], (D, D), jnp.float32) * scale
        inp['bk'] = jnp.zeros((D,), jnp.float32)
        inp['Wv'] = jax.random.normal(ks[5], (D, D), jnp.float32) * scale
        inp['bv'] = jnp.zeros((D,), jnp.float32)
        inp['Wo'] = jax.random.normal(ks[6], (D, D), jnp.float32) * scale
        inp['bo'] = jnp.zeros((D,), jnp.float32)
        return inp
    _L1_xattn_all = _L1_xattn_setup()
    _L1_xattn_in = {k: v for k, v in _L1_xattn_all.items() if k in ('Wq', 'bq', 'Wk', 'bk', 'Wv', 'bv', 'Wo', 'bo')}
    del _L1_xattn_all

    def _L1_ffn_setup():
        import jax, jax.numpy as jnp
        import numpy as np
        HIDDEN_SIZE = 256
        NUM_EXPERTS = 8
        MOE_INTERMEDIATE_SIZE = 352
        NUM_EXPERTS_PER_TOK = 2
        SHARED_EXPERT_INTERMEDIATE_SIZE = 704
        B, T = (2, 256)
        W_SCALE = 0.02
        key = jax.random.key(seed)
        ks = jax.random.split(key, 8)
        H, E, I, SI = (HIDDEN_SIZE, NUM_EXPERTS, MOE_INTERMEDIATE_SIZE, SHARED_EXPERT_INTERMEDIATE_SIZE)
        return {'x': jax.random.normal(ks[0], (B, T, H), jnp.float32), 'gate_w': jax.random.normal(ks[1], (E, H), jnp.float32) * W_SCALE, 'experts_gate_up': jax.random.normal(ks[2], (E, 2 * I, H), jnp.float32) * W_SCALE, 'experts_down': jax.random.normal(ks[3], (E, H, I), jnp.float32) * W_SCALE, 'shared_gate_w': jax.random.normal(ks[4], (SI, H), jnp.float32) * W_SCALE, 'shared_up_w': jax.random.normal(ks[5], (SI, H), jnp.float32) * W_SCALE, 'shared_down_w': jax.random.normal(ks[6], (H, SI), jnp.float32) * W_SCALE, 'shared_expert_gate_w': jax.random.normal(ks[7], (1, H), jnp.float32) * W_SCALE}
    _L1_ffn_all = _L1_ffn_setup()
    _L1_ffn_in = {k: v for k, v in _L1_ffn_all.items() if k in ('gate_w', 'experts_gate_up', 'experts_down', 'shared_gate_w', 'shared_up_w', 'shared_down_w', 'shared_expert_gate_w')}
    del _L1_ffn_all
    return {'x': x, 'ctx_1024': ctx_1024, 'mask_BxS2_bk1': mask_BxS2_bk1, 'mask_SxS2_fk1': mask_SxS2_fk1, 'g_xattn': g_xattn, 'g_ffn': g_ffn, 'L0_xattn_relative_bias': _L0_xattn_in['relative_bias'], 'L0_xattn_Wq': _L0_xattn_in['Wq'], 'L0_xattn_bq': _L0_xattn_in['bq'], 'L0_xattn_Wk': _L0_xattn_in['Wk'], 'L0_xattn_bk': _L0_xattn_in['bk'], 'L0_xattn_Wv': _L0_xattn_in['Wv'], 'L0_xattn_bv': _L0_xattn_in['bv'], 'L0_xattn_Wo': _L0_xattn_in['Wo'], 'L0_xattn_bo': _L0_xattn_in['bo'], 'L0_ffn_Wp1': _L0_ffn_in['Wp1'], 'L0_ffn_bp1': _L0_ffn_in['bp1'], 'L0_ffn_Wp2': _L0_ffn_in['Wp2'], 'L0_ffn_bp2': _L0_ffn_in['bp2'], 'L0_ffn_W1': _L0_ffn_in['W1'], 'L0_ffn_b1': _L0_ffn_in['b1'], 'L0_ffn_W2': _L0_ffn_in['W2'], 'L0_ffn_b2': _L0_ffn_in['b2'], 'L0_ffn_Wo': _L0_ffn_in['Wo'], 'L0_ffn_bo': _L0_ffn_in['bo'], 'L1_xattn_Wq': _L1_xattn_in['Wq'], 'L1_xattn_bq': _L1_xattn_in['bq'], 'L1_xattn_Wk': _L1_xattn_in['Wk'], 'L1_xattn_bk': _L1_xattn_in['bk'], 'L1_xattn_Wv': _L1_xattn_in['Wv'], 'L1_xattn_bv': _L1_xattn_in['bv'], 'L1_xattn_Wo': _L1_xattn_in['Wo'], 'L1_xattn_bo': _L1_xattn_in['bo'], 'L1_ffn_gate_w': _L1_ffn_in['gate_w'], 'L1_ffn_experts_gate_up': _L1_ffn_in['experts_gate_up'], 'L1_ffn_experts_down': _L1_ffn_in['experts_down'], 'L1_ffn_shared_gate_w': _L1_ffn_in['shared_gate_w'], 'L1_ffn_shared_up_w': _L1_ffn_in['shared_up_w'], 'L1_ffn_shared_down_w': _L1_ffn_in['shared_down_w'], 'L1_ffn_shared_expert_gate_w': _L1_ffn_in['shared_expert_gate_w']}

def reference(x, ctx_1024, mask_BxS2_bk1, mask_SxS2_fk1, g_xattn, g_ffn, L0_xattn_relative_bias, L0_xattn_Wq, L0_xattn_bq, L0_xattn_Wk, L0_xattn_bk, L0_xattn_Wv, L0_xattn_bv, L0_xattn_Wo, L0_xattn_bo, L0_ffn_Wp1, L0_ffn_bp1, L0_ffn_Wp2, L0_ffn_bp2, L0_ffn_W1, L0_ffn_b1, L0_ffn_W2, L0_ffn_b2, L0_ffn_Wo, L0_ffn_bo, L1_xattn_Wq, L1_xattn_bq, L1_xattn_Wk, L1_xattn_bk, L1_xattn_Wv, L1_xattn_bv, L1_xattn_Wo, L1_xattn_bo, L1_ffn_gate_w, L1_ffn_experts_gate_up, L1_ffn_experts_down, L1_ffn_shared_gate_w, L1_ffn_shared_up_w, L1_ffn_shared_down_w, L1_ffn_shared_expert_gate_w):
    import jax
    import jax.numpy as jnp

    def _L0_xattn_ref(query, key, value, key_padding_mask, relative_bias, Wq, bq, Wk, bk, Wv, bv, Wo, bo):
        import jax, jax.numpy as jnp
        import numpy as np
        B, S, D, H = (2, 512, 256, 16)
        DH = D // H

        def split_heads(x):
            b, s, _ = x.shape
            return x.reshape(b, s, H, DH).transpose(0, 2, 1, 3)
        q = split_heads(query @ Wq.T + bq)
        k = split_heads(key @ Wk.T + bk)
        v = split_heads(value @ Wv.T + bv)
        scores = jnp.einsum('bhqd,bhkd->bhqk', q, k) / jnp.sqrt(jnp.asarray(DH, q.dtype))
        scores = scores + relative_bias
        scores = jnp.where(key_padding_mask[:, None, None, :], scores, -jnp.inf)
        attn = jax.nn.softmax(scores, axis=-1)
        out = jnp.einsum('bhqk,bhkd->bhqd', attn, v)
        out = out.transpose(0, 2, 1, 3).reshape(query.shape[0], query.shape[1], D)
        return out @ Wo.T + bo

    def _L0_ffn_ref(hidden_states, Wp1, bp1, Wp2, bp2, W1, b1, W2, b2, Wo, bo):
        import jax, jax.numpy as jnp
        import numpy as np
        B, S, H = (8, 1024, 256)
        NAV = 128
        E = 8
        F = 2 * H
        last = hidden_states[:, -1, :]
        logits = jax.nn.gelu(last @ Wp1 + bp1, approximate=False) @ Wp2 + bp2
        action_probs = jax.nn.softmax(logits, axis=-1)
        sel = jnp.argmax(action_probs, axis=-1)
        w1 = W1[sel]
        w2 = W2[sel]
        h = jax.nn.gelu(jnp.einsum('bsh,bhf->bsf', hidden_states, w1) + b1[sel][:, None, :], approximate=False)
        reasoned = jnp.einsum('bsf,bfh->bsh', h, w2) + b2[sel][:, None, :]
        out = reasoned @ Wo + bo
        return hidden_states + 0.3 * out

    def _L1_xattn_ref(xq, xk, xv, mask, Wq, bq, Wk, bk, Wv, bv, Wo, bo):
        import jax, jax.numpy as jnp
        import numpy as np
        B, S, D, H = (2, 512, 256, 16)
        DEPTH = D // H

        def _split_heads(x):
            b, s, _ = x.shape
            return x.reshape(b, s, H, DEPTH).transpose(0, 2, 1, 3)
        q = _split_heads(xq @ Wq + bq)
        k = _split_heads(xk @ Wk + bk)
        v = _split_heads(xv @ Wv + bv)
        logits = jnp.einsum('bhqd,bhkd->bhqk', q, k) / jnp.sqrt(jnp.float32(DEPTH))
        logits = logits + mask[None, None, :, :] * -1000000000.0
        weights = jax.nn.softmax(logits, axis=-1)
        attn = jnp.einsum('bhqk,bhkd->bhqd', weights, v)
        concat = attn.transpose(0, 2, 1, 3).reshape(xq.shape[0], -1, D)
        return concat @ Wo + bo

    def _L1_ffn_ref(x, gate_w, experts_gate_up, experts_down, shared_gate_w, shared_up_w, shared_down_w, shared_expert_gate_w):
        import jax, jax.numpy as jnp
        import numpy as np
        HIDDEN_SIZE = 256
        NUM_EXPERTS = 8
        MOE_INTERMEDIATE_SIZE = 352
        NUM_EXPERTS_PER_TOK = 2
        SHARED_EXPERT_INTERMEDIATE_SIZE = 704
        B, T = (2, 256)
        W_SCALE = 0.02
        Bx, Tx, H = x.shape
        E = gate_w.shape[0]
        I = experts_down.shape[2]
        x_flat = x.reshape(Bx * Tx, H)
        logits = x_flat @ gate_w.T
        scores = jax.nn.softmax(logits, axis=-1)
        _, topk_ids = jax.lax.top_k(scores, NUM_EXPERTS_PER_TOK)
        in_topk = jax.nn.one_hot(topk_ids, E, dtype=x.dtype).sum(axis=1)
        w = scores * in_topk
        gu = jnp.einsum('nh,eih->nei', x_flat, experts_gate_up)
        g, u = (gu[..., :I], gu[..., I:])
        h = jax.nn.silu(g) * u
        expert_out = jnp.einsum('nei,ehi->neh', h, experts_down)
        out = jnp.einsum('neh,ne->nh', expert_out, w)
        shared = jax.nn.silu(x_flat @ shared_gate_w.T) * (x_flat @ shared_up_w.T) @ shared_down_w.T
        shared_weight = jax.nn.sigmoid(x_flat @ shared_expert_gate_w.T)
        out = out + shared_weight * shared
        return out.reshape(Bx, Tx, H)
    x = x + jnp.tanh(g_xattn[0]) * _L0_xattn_ref(_layernorm(x, axis=-1), ctx_1024, ctx_1024, mask_BxS2_bk1, L0_xattn_relative_bias, L0_xattn_Wq, L0_xattn_bq, L0_xattn_Wk, L0_xattn_bk, L0_xattn_Wv, L0_xattn_bv, L0_xattn_Wo, L0_xattn_bo)
    x = x + jnp.tanh(g_ffn[0]) * _L0_ffn_ref(_layernorm(x, axis=-1), L0_ffn_Wp1, L0_ffn_bp1, L0_ffn_Wp2, L0_ffn_bp2, L0_ffn_W1, L0_ffn_b1, L0_ffn_W2, L0_ffn_b2, L0_ffn_Wo, L0_ffn_bo)
    x = x + jnp.tanh(g_xattn[1]) * _L1_xattn_ref(_layernorm(x, axis=-1), ctx_1024, ctx_1024, mask_SxS2_fk1, L1_xattn_Wq, L1_xattn_bq, L1_xattn_Wk, L1_xattn_bk, L1_xattn_Wv, L1_xattn_bv, L1_xattn_Wo, L1_xattn_bo)
    x = x + jnp.tanh(g_ffn[1]) * _L1_ffn_ref(_layernorm(x, axis=-1), L1_ffn_gate_w, L1_ffn_experts_gate_up, L1_ffn_experts_down, L1_ffn_shared_gate_w, L1_ffn_shared_up_w, L1_ffn_shared_down_w, L1_ffn_shared_expert_gate_w)
    return x

_drawn_inputs = setup_inputs


def setup_inputs(seed=0):
    import zlib

    import numpy as np

    out = dict(_drawn_inputs(seed))
    spreads = {'g_ffn': (-1.0, 0.6),
     'L0_xattn_bq': (0.0, 0.744),
     'L0_xattn_bk': (0.0, 0.8),
     'L0_xattn_bv': (0.0, 0.1),
     'L0_xattn_bo': (0.0, 0.1),
     'L0_ffn_bp1': (0.0, 0.1),
     'L0_ffn_bp2': (0.0, 0.1),
     'L0_ffn_b1': (0.0, 0.28),
     'L0_ffn_b2': (0.0, 0.1),
     'L0_ffn_bo': (0.0, 0.1),
     'L1_xattn_bq': (0.0, 0.1),
     'L1_xattn_bk': (0.0, 0.8),
     'L1_xattn_bv': (0.0, 0.1),
     'L1_xattn_bo': (0.0, 0.1)}
    factors = {'L0_xattn_relative_bias': 8.0,
     'L1_ffn_gate_w': 8.0,
     'L1_ffn_experts_gate_up': 8.0,
     'L1_ffn_experts_down': 8.0,
     'L1_ffn_shared_gate_w': 3.242,
     'L1_ffn_shared_up_w': 3.384,
     'L1_ffn_shared_down_w': 3.268,
     'L1_ffn_shared_expert_gate_w': 8.0}
    for name, (base, spread) in spreads.items():
        noise = np.random.default_rng([zlib.crc32(name.encode()), seed]).standard_normal(out[name].shape)
        drawn = base * np.exp(spread * noise) if base else spread * noise
        out[name] = jnp.asarray(drawn.astype(out[name].dtype))
    for name, factor in factors.items():
        out[name] = (out[name] * factor).astype(out[name].dtype)
    return out
```

```python
from contextlib import ExitStack

import concourse.bass as bass
from concourse import mybir

ALU = mybir.AluOpType
ACT = mybir.ActivationFunctionType
F32 = mybir.dt.float32
BF16 = mybir.dt.bfloat16
U32 = mybir.dt.uint32
U8 = mybir.dt.uint8

P = 128
B, S, D = 4, 512, 256
H, DH = 16, 16
N = B * S
DC = D // P
TT = N // P
QT = S // P
E0, F0, NAV = 8, 512, 128
E1, I1, SI = 8, 352, 704
HG = 4
VW = 32
SCALE = 1.0 / DH ** 0.5
EPS = 1e-5
NEG = -1.0e30
MASK_C = -1000000000.0
Q_PARTS = [0, 1, 2, 0, 1, 0]
K_PARTS = [0, 0, 0, 1, 1, 2]
KS = DH * len(Q_PARTS)


def chunks(n):
    return [(a, min(P, n - a)) for a in range(0, n, P)]


def layernorm_phase(nc, sem, sb, x_loaded, tag):
    stats_done, mv_done, var_ready = sem(tag + "stats_done"), sem(tag + "mv_done"), sem(tag + "var_ready")
    std_ready, rstd_ready = sem(tag + "std_ready"), sem(tag + "rstd_ready")
    norm_done, turned, copied = sem(tag + "norm_done"), sem(tag + "turned"), sem(tag + "copied")
    copied_act = sem(tag + "copied_act")
    G = TT // 4

    with nc.Block() as block:
        @block.vector
        def _(dve):
            for t in range(TT):
                if x_loaded is not None and t % 4 == 0:
                    dve.wait_ge(x_loaded[t // 4], 16)
                nc.vector.bn_stats(sb.stats[:, t, :], sb.x[:, t, :]).then_inc(stats_done, 1)
            for t in range(TT):
                dve.wait_ge(stats_done, t + 1)
                nc.vector.bn_aggr(sb.mv[:, t, :], sb.stats[:, t, :]).then_inc(mv_done, 1)
            dve.wait_ge(mv_done, TT)
            nc.vector.tensor_scalar(sb.rstd[:, :], sb.mv[:, :, 1], EPS, None, ALU.add).then_inc(var_ready, 1)
            dve.wait_ge(std_ready, 1)
            nc.vector.reciprocal(sb.rstd[:, :], sb.std[:, :]).then_inc(rstd_ready, 1)
            dve.wait_ge(rstd_ready, 1)
            for t in range(TT):
                nc.vector.tensor_scalar(sb.tok[:, t, :], sb.x[:, t, :], sb.mv[:, t, 0:1], sb.rstd[:, t:t + 1],
                                        ALU.subtract, ALU.mult).then_inc(norm_done, 1)
                if t % 4 == 3:
                    g = t // 4
                    dve.wait_ge(turned, 2 * g + 1)
                    nc.vector.tensor_copy(sb.xT[:, 0, g * S:(g + 1) * S], sb.ps[:, (2 * g) % 8, :]).then_inc(copied, 1)

        @block.scalar
        def _(act):
            act.wait_ge(var_ready, 1)
            nc.scalar.activation(sb.std[:, :], sb.rstd[:, :], ACT.Sqrt).then_inc(std_ready, 1)
            for g in range(G):
                act.wait_ge(turned, 2 * g + 2)
                nc.scalar.activation(sb.xT[:, 1, g * S:(g + 1) * S], sb.ps[:, (2 * g + 1) % 8, :],
                                     ACT.Copy).then_inc(copied_act, 1)

        @block.tensor
        def _(pe):
            for g in range(G):
                for c in range(DC):
                    for i in range(4):
                        t = 4 * g + i
                        pe.wait_ge(norm_done, t + 1)
                        last = nc.tensor.transpose(sb.ps[:, (2 * g + c) % 8, i * P:(i + 1) * P],
                                                   sb.tok[:, t, c * P:(c + 1) * P], sb.ident[:, :])
                    last.then_inc(turned, 1)


def projection_phase(nc, sem, sb, w, dram, tag):
    proj_done, plain_done, head_done = sem(tag + "proj_done"), sem(tag + "plain_done"), sem(tag + "head_done")
    rest_done, mid_done, low_done = sem(tag + "rest_done"), sem(tag + "mid_done"), sem(tag + "low_done")
    stored = [sem(tag + f"stored{i}") for i in range(2)]
    v_done, v_copied = sem(tag + "v_done"), sem(tag + "v_copied")
    NT = 2 * DC * B

    def place(n):
        return n // (DC * B), n // B % DC, n % B

    with nc.Block() as block:
        @block.tensor
        def _(pe):
            for n in range(NT):
                which, mo, b = place(n)
                src = sb.cT if which else sb.xT
                if n >= 4:
                    pe.wait_ge(plain_done, n - 3)
                for c in range(DC):
                    last = nc.tensor.matmul(sb.ps[:, n % 4, :], w.qk[:, which, c, mo * P:(mo + 1) * P],
                                            src[:, c, b * S:(b + 1) * S], start=(c == 0), stop=(c == DC - 1))
                last.then_inc(proj_done, 1)
            for v in range(TT // 2):
                if v >= 4:
                    pe.wait_ge(v_copied, v - 3)
                for i in range(2):
                    t = 2 * v + i
                    for c in range(DC):
                        last = nc.tensor.matmul(sb.ps[:, 4 + v % 4, i * D:(i + 1) * D],
                                                sb.cT[:, c, t * P:(t + 1) * P], w.v[:, c, :],
                                                start=(c == 0), stop=(c == DC - 1))
                last.then_inc(v_done, 1)

        @block.scalar
        def _(act):
            for n in range(NT):
                which, mo, b = place(n)
                act.wait_ge(proj_done, n + 1)
                if n >= 2:
                    act.wait_ge(rest_done, n - 1)
                nc.scalar.activation(sb.plain[:, n % 2, :], sb.ps[:, n % 4, :], ACT.Identity,
                                     bias=w.bqk[:, which, mo:mo + 1],
                                     scale=1.0 if which else SCALE).then_inc(plain_done, 1)

        @block.vector
        def _(dve):
            for n in range(NT):
                dve.wait_ge(plain_done, n + 1)
                if n >= 2:
                    dve.wait_ge(stored[n % 2], 16 * (n // 2))
                nc.vector.tensor_copy(sb.parts[:, n % 2, 0, :], sb.plain[:, n % 2, :]).then_inc(head_done, 1)
                dve.wait_ge(head_done, n + 1)
                if n >= 2:
                    dve.wait_ge(low_done, n - 1)
                nc.vector.tensor_tensor(sb.rest[:, n % 2, :], sb.plain[:, n % 2, :], sb.parts[:, n % 2, 0, :],
                                        ALU.subtract).then_inc(rest_done, 1)
                dve.wait_ge(rest_done, n + 1)
                nc.vector.tensor_copy(sb.parts[:, n % 2, 1, :], sb.rest[:, n % 2, :]).then_inc(mid_done, 1)
            for v in range(TT // 2):
                dve.wait_ge(v_done, v + 1)
                nc.vector.tensor_tensor(
                    sb.v[:, 2 * v:2 * v + 2, :], sb.ps[:, 4 + v % 4, :].rearrange("p (a d) -> p a d", a=2),
                    w.bv[:, :].unsqueeze(1).to_broadcast([P, 2, D]), ALU.add).then_inc(v_copied, 1)

        @block.gpsimd
        def _(pool):
            for n in range(NT):
                pool.wait_ge(mid_done, n + 1)
                nc.gpsimd.tensor_tensor(sb.parts[:, n % 2, 2, :], sb.rest[:, n % 2, :], sb.parts[:, n % 2, 1, :],
                                        ALU.subtract).then_inc(low_done, 1)

        @block.sync
        def _(sp):
            for n in range(NT):
                which, mo, b = place(n)
                sp.wait_ge(low_done, n + 1)
                sp.dma_start(dram.qk[which, :, mo * P:(mo + 1) * P, b * S:(b + 1) * S].rearrange("s p t -> p s t"),
                             sb.parts[:, n % 2, :, :]).then_inc(stored[n % 2], 16)
            for i in range(2):
                sp.wait_ge(stored[i], 16 * (NT // 2))


def attention_phase(nc, sem, sb, at, dram, bias_dram, tag):
    per_head_bias = bias_dram is not None
    K = KS + 1 if per_head_bias else KS
    LOADS = 2 * len(Q_PARTS) + (1 if per_head_bias else 0)
    qk_loaded = [sem(tag + f"qk_loaded{i}") for i in range(2)]
    bias_loaded = [sem(tag + f"bias_loaded{j}") for j in range(HG)]
    scores_done = sem(tag + "scores_done")
    biased = sem(tag + "biased")
    exp_done = sem(tag + "exp_done")
    turned = sem(tag + "turned")
    kept0, kept1 = sem(tag + "kept0"), sem(tag + "kept1")
    v_ready = sem(tag + "v_ready")
    av_done = sem(tag + "av_done")
    out_kept = sem(tag + "out_kept")
    out_turned = sem(tag + "out_turned")
    sums_ready = sem(tag + "sums_ready")
    out_done = sem(tag + "out_done")
    granted = sem(tag + "granted")
    GROUPS = H // HG
    M = HG * B

    def groups(eng, body):
        body(0, True, False)
        with eng.Fori(1, GROUPS - 1) as hg:
            body(hg, False, False)
        body(GROUPS - 1, False, True)

    def before(hg, b):
        return (hg, b - 1) if b else (hg - 1, B - 1)

    def slot(b, j):
        return j + HG * (b % 2) if j < 2 else j

    with nc.Block() as block:
        @block.sync
        def _(sp):
            def load_qk(hg, b):
                sp.wait_ge(scores_done, (hg * 4 + b) * 16 + 16)
                for s in range(len(Q_PARTS)):
                    for which, part, dst in ((0, Q_PARTS[s], at.qs), (1, K_PARTS[s], at.ks)):
                        src = dram.qk[which, part, :, b * S:(b + 1) * S].rearrange("(g j d) t -> g d j t", j=HG, d=DH)
                        sp.dma_start(dst[s * DH:(s + 1) * DH, b % 2, :, :],
                                     src[bass.ds(hg, 1), :, :, :].rearrange("g d j t -> (g d) j t")
                                     ).then_inc(qk_loaded[b % 2], 16)
                if per_head_bias:
                    sp.dma_start(at.ks[KS:KS + 1, b % 2, :, :],
                                 dram.keymask[b:b + 1, :].unsqueeze(1).to_broadcast([1, HG, S])
                                 ).then_inc(qk_loaded[b % 2], 16)

            def load_bias(hg, j):
                src = bias_dram.rearrange("(g j) (t p) k -> g j p t k", j=HG, p=P)
                sp.dma_start(at.bias[:, j, :, :], src[bass.ds(hg, 1), j, :, :, :].rearrange("g p t k -> (g p) t k")
                             ).then_inc(bias_loaded[j], 16)

            load_qk(0, 0)
            if per_head_bias:
                for j in range(HG):
                    load_bias(0, j)

            def body(hg, first, last):
                for b in range(1, B):
                    load_qk(hg, b)
                if not last:
                    load_qk(hg + 1, 0)
                    for j in range(HG if per_head_bias else 0):
                        sp.wait_ge(biased, hg * 64 + 4 * (M - HG + j) + 4 + 2)
                        load_bias(hg + 1, j)
            groups(sp, body)

        @block.tensor
        def _(pe):
            pe.nop().then_inc(scores_done, 32)

            def scores(hg, m, qts):
                b, j = m % M // HG, m % HG
                for qt in qts:
                    if j == 0 and qt == 0:
                        pe.wait_ge(qk_loaded[b % 2], (hg * 2 + (m // HG) // 2 + 1) * (16 * LOADS))
                    pe.wait_ge(biased, hg * 64 + 4 * m + qt + 1)
                    nc.tensor.matmul(sb.ps[:, qt % 2, :], at.qs[0:K, b % 2, j, qt * P:(qt + 1) * P],
                                     at.ks[0:K, b % 2, j, :], start=True, stop=True).then_inc(scores_done, 1)

            def turn(hg, m, kt):
                if kt == 0:
                    pe.wait_ge(exp_done, hg * 64 + 4 * m + 4 + 4)
                if kt % 2 == 0:
                    pe.wait_ge(kept1 if kt else kept0, hg * M + m + 1)
                for qt in range(QT):
                    last = nc.tensor.transpose(sb.ps[:, 2 + kt, qt * P:(qt + 1) * P],
                                               at.p[m % 4][:, qt, kt * P:(kt + 1) * P], sb.ident[:, :])
                if kt % 2 == 1:
                    last.then_inc(turned, 1)

            def values(hg, b, kt):
                pe.wait_ge(kept1 if kt >= 2 else kept0, hg * M + HG * b + HG + 1)
                if kt == 0:
                    pe.wait_ge(v_ready, hg * B + b + 1)
                    pe.wait_ge(out_kept, hg * B + b + 1)
                for j in range(HG):
                    last = nc.tensor.matmul(sb.ps[VW * j:VW * (j + 1), 6, :], at.vq[:, b % 2, kt, j, :],
                                            at.pT[:, slot(b, j), kt, :], start=(kt == 0), stop=(kt == QT - 1))
                if kt == QT - 1:
                    last.then_inc(av_done, 1)

            def turn_out(hg, b):
                pe.wait_ge(out_kept, hg * B + b + 2)
                pe.wait_ge(out_done, hg * B + b + 1)
                for qt in range(QT):
                    last = nc.tensor.transpose(sb.ps[:, 7, qt * P:(qt + 1) * P], at.oT[:, qt * P:(qt + 1) * P],
                                               sb.ident[:, :])
                last.then_inc(out_turned, 1)

            scores(0, 0, range(QT))
            scores(0, 1, (0, 1))

            def body(hg, first, last):
                for m in range(M):
                    b, j = m // HG, m % HG
                    earlier = not (first and b == 0)
                    next1, next2 = not (last and m + 1 >= M), not (last and m + 2 >= M)
                    if next1:
                        scores(hg, m + 1, (2,))
                    if earlier and j < 3:
                        values(*before(hg, b), (0, 2, 3)[j])
                    turn(hg, m, 0)
                    if next1:
                        scores(hg, m + 1, (3,))
                    turn(hg, m, 1)
                    if next2:
                        scores(hg, m + 2, (0,))
                    if earlier and j == 0:
                        values(*before(hg, b), 1)
                    if earlier and j == 3:
                        turn_out(*before(hg, b))
                    turn(hg, m, 2)
                    if next2:
                        scores(hg, m + 2, (1,))
                    turn(hg, m, 3)
                if last:
                    for kt in range(QT):
                        values(hg, B - 1, kt)
                    turn_out(hg, B - 1)
            groups(pe, body)

        @block.vector
        def _(dve):
            dve.nop().then_inc(biased, 2)
            dve.nop().then_inc(kept1, 1)
            dve.nop().then_inc(out_done, 1)

            def add_bias(hg, m, qts):
                b, j = m % M // HG, m % HG
                for qt in qts:
                    u = 4 * m + qt + 1
                    if per_head_bias and b == 0 and qt == 0:
                        dve.wait_ge(bias_loaded[j], (hg + (m // M + 1)) * 16)
                    dve.wait_ge(scores_done, hg * 64 + (u + 32))
                    dve.wait_ge(exp_done, hg * 64 + u)
                    dve.sem_inc(granted, 1)
                    nc.vector.tensor_tensor_reduce(
                        at.s[:, qt, :], sb.ps[:, qt % 2, :], at.bias[:, j if per_head_bias else 0, qt, :],
                        -1.0, 3.0e38, ALU.add, ALU.min, at.nmax[:, m % 4, qt:qt + 1]).then_inc(biased, 1)

            def keep(hg, m):
                dve.wait_ge(turned, (hg * M + m) * 2 + 2 + 8)
                nc.vector.tensor_copy(at.pT[:, slot(m // HG, m % HG), 2:4, :], sb.ps[:, 4:6, :]).then_inc(kept1, 1)

            def normalise(hg, b):
                dve.wait_ge(out_turned, hg * B + b + 2)
                o = sb.ps[:, 7, :].rearrange("p (t j w) -> p t j w", t=QT, j=HG)
                nc.vector.reciprocal(at.rsum[:, :, :], o[:, :, :, DH]).then_inc(sums_ready, 1)
                dve.wait_ge(sums_ready, hg * B + b + 1)
                dst = sb.tok[:, b * QT:(b + 1) * QT, :].rearrange("p t (g f) -> p g t f", g=GROUPS)
                nc.vector.tensor_tensor(
                    dst[:, bass.ds(hg, 1), :, :].rearrange("p g t (j d) -> p (g t) j d", j=HG),
                    o[:, :, :, 0:DH], at.rsum[:, :, :].unsqueeze(3).to_broadcast([P, QT, HG, DH]),
                    ALU.mult).then_inc(out_done, 1)

            add_bias(0, 0, range(QT))
            add_bias(0, 1, (0, 1))

            def body(hg, first, last):
                for m in range(M):
                    b, j = m // HG, m % HG
                    if not (last and m + 1 >= M):
                        add_bias(hg, m + 1, (2,))
                    if not (first and m == 0):
                        keep(hg, m - 1)
                    if not (last and m + 1 >= M):
                        add_bias(hg, m + 1, (3,))
                    if not (last and m + 2 >= M):
                        add_bias(hg, m + 2, (0, 1))
                    if j == 3 and not (first and b == 0):
                        normalise(*before(hg, b))
                if last:
                    keep(hg, M - 1)
                    normalise(hg, B - 1)
            groups(dve, body)

        @block.scalar
        def _(act):
            act.nop().then_inc(exp_done, 4)
            act.nop().then_inc(kept0, 1)
            act.nop().then_inc(out_kept, 1)

            def exps(hg, m, qts):
                for qt in qts:
                    if qt == 0:
                        act.wait_ge(turned, (hg * M + m) * 2 + 2)
                    act.wait_ge(biased, hg * 64 + 4 * m + qt + 1 + 2)
                    nc.scalar.activation(at.p[m % 4][:, qt, :], at.s[:, qt, :], ACT.Exp,
                                         bias=at.nmax[:, m % 4, qt:qt + 1], scale=-1.0).then_inc(exp_done, 1)

            def keep(hg, m):
                act.wait_ge(turned, (hg * M + m) * 2 + 1 + 8)
                nc.scalar.activation(at.pT[:, slot(m // HG, m % HG), 0:2, :], sb.ps[:, 2:4, :], ACT.Copy).then_inc(kept0, 1)

            def keep_out(hg, b):
                act.wait_ge(av_done, hg * B + b + 1 + 2)
                act.wait_ge(out_turned, hg * B + b + 1)
                nc.scalar.activation(at.oT[:, :], sb.ps[:, 6, :], ACT.Copy).then_inc(out_kept, 1)

            exps(0, 0, range(QT))
            exps(0, 1, (0, 1))

            def body(hg, first, last):
                for m in range(M):
                    b, j = m // HG, m % HG
                    if not (last and m + 1 >= M):
                        exps(hg, m + 1, (2, 3))
                    keep(hg, m)
                    if j == 2 and not (first and b == 0):
                        keep_out(*before(hg, b))
                    if not (last and m + 2 >= M):
                        exps(hg, m + 2, (0, 1))
                if last:
                    keep_out(hg, B - 1)
            groups(act, body)

        @block.gpsimd
        def _(pool):
            pool.nop().then_inc(turned, 8)
            pool.nop().then_inc(av_done, 2)
            pool.nop().then_inc(out_turned, 1)

            def body(hg, first, last):
                for b in range(B):
                    pool.wait_ge(av_done, hg * B + b + 1)
                    src = sb.v[:, b * QT:(b + 1) * QT, :].rearrange("p t (g f) -> p g t f", g=GROUPS)
                    nc.gpsimd.tensor_copy(
                        at.vq[:, b % 2, :, :, 0:DH],
                        src[:, bass.ds(hg, 1), :, :].rearrange("p g t (j d) -> p (g t) j d", j=HG)).then_inc(v_ready, 1)
            groups(pool, body)


def output_phase(nc, sem, sb, w, tag):
    turned, copied, copied_act = sem(tag + "turned"), sem(tag + "copied"), sem(tag + "copied_act")
    bias_added, proj_done, added = sem(tag + "bias_added"), sem(tag + "proj_done"), sem(tag + "added")
    G = TT // 4

    with nc.Block() as block:
        @block.tensor
        def _(pe):
            for g in range(G):
                for c in range(DC):
                    if g >= 2:
                        pe.wait_ge(copied_act if c else copied, g - 1)
                    for i in range(4):
                        last = nc.tensor.transpose(sb.ps[:, 2 * (g % 2) + c, i * P:(i + 1) * P],
                                                   sb.tok[:, 4 * g + i, c * P:(c + 1) * P], sb.ident[:, :])
                    last.then_inc(turned, 1)
            for v in range(TT // 2):
                if v % 2 == 0:
                    pe.wait_ge(copied, v // 2 + 1)
                    pe.wait_ge(copied_act, v // 2 + 1)
                if v >= 4:
                    pe.wait_ge(added, v - 3)
                for i in range(2):
                    t = 2 * v + i
                    for c in range(DC):
                        last = nc.tensor.matmul(sb.ps[:, 4 + v % 4, i * D:(i + 1) * D],
                                                sb.xT[:, c, t * P:(t + 1) * P], w.o[:, c, :],
                                                start=(c == 0), stop=(c == DC - 1))
                last.then_inc(proj_done, 1)

        @block.scalar
        def _(act):
            for g in range(G):
                act.wait_ge(turned, 2 * g + 2)
                nc.scalar.activation(sb.xT[:, 1, g * S:(g + 1) * S], sb.ps[:, 2 * (g % 2) + 1, :],
                                     ACT.Copy).then_inc(copied_act, 1)

        @block.gpsimd
        def _(pool):
            for v in range(TT // 2):
                nc.gpsimd.tensor_tensor(sb.x[:, 2 * v:2 * v + 2, :], sb.x[:, 2 * v:2 * v + 2, :],
                                        w.bo[:, :].unsqueeze(1).to_broadcast([P, 2, D]),
                                        ALU.add).then_inc(bias_added, 1)

        @block.vector
        def _(dve):
            for g in range(G):
                dve.wait_ge(turned, 2 * g + 1)
                nc.vector.tensor_copy(sb.xT[:, 0, g * S:(g + 1) * S], sb.ps[:, 2 * (g % 2), :]).then_inc(copied, 1)
            for v in range(TT // 2):
                dve.wait_ge(bias_added, v + 1)
                dve.wait_ge(proj_done, v + 1)
                xs = sb.x[:, 2 * v:2 * v + 2, :].rearrange("p a d -> p (a d)")
                nc.vector.scalar_tensor_tensor(xs, sb.ps[:, 4 + v % 4, :], w.gate, xs,
                                               ALU.mult, ALU.add).then_inc(added, 1)


def routed_ffn_phase(nc, sem, sb, f, args, tag):
    r1_done, r1_kept, r2_done = sem(tag + "r1_done"), sem(tag + "r1_kept"), sem(tag + "r2_done")
    logits_kept, top_done, idx_done = sem(tag + "logits_kept"), sem(tag + "top_done"), sem(tag + "idx_done")
    loaded = [sem(tag + f"loaded{i}") for i in range(2)]
    up_done, gelu_done, down_done = sem(tag + "up_done"), sem(tag + "gelu_done"), sem(tag + "down_done")
    down_kept, out_done, added = sem(tag + "down_kept"), sem(tag + "out_done"), sem(tag + "added")
    hid_added = sem(tag + "hid_added")
    FC = F0 // P

    with nc.Block() as block:
        @block.tensor
        def _(pe):
            last_tokens = sb.xT[:, :, :].rearrange("p c (b s) -> p c b s", b=B)[:, :, :, S - 1]
            for c in range(DC):
                last = nc.tensor.matmul(sb.ps[:, 0, 0:B], f.wp1[:, c, :], last_tokens[:, c, :],
                                        start=(c == 0), stop=(c == DC - 1))
            last.then_inc(r1_done, 1)
            pe.wait_ge(r1_kept, 1)
            nc.tensor.matmul(sb.ps[0:B, 1, 0:E0], f.r1[:, :], f.wp2[:, :], start=True, stop=True).then_inc(r2_done, 1)
            for b in range(B):
                pe.wait_ge(loaded[b % 2], 64 * (b // 2 + 1))
                for mo in range(FC):
                    n = b * FC + mo
                    if n >= 4:
                        pe.wait_ge(gelu_done, n - 3)
                    elif n < 2:
                        pe.wait_ge(logits_kept, 1)
                    for c in range(DC):
                        last = nc.tensor.matmul(sb.ps[:, n % 4, :], f.w1[:, b % 2, c, mo * P:(mo + 1) * P],
                                                sb.xT[:, c, b * S:(b + 1) * S], start=(c == 0), stop=(c == DC - 1))
                    last.then_inc(up_done, 1)
                pe.wait_ge(gelu_done, FC * (b + 1))
                for mo in range(DC):
                    if b >= 1:
                        pe.wait_ge(down_kept, DC * (b - 1) + mo + 1)
                    for c in range(FC):
                        last = nc.tensor.matmul(sb.ps[:, 4 + mo, :], f.w2[:, b % 2, c, mo * P:(mo + 1) * P],
                                                f.h[:, b % 2, c, :], start=(c == 0), stop=(c == FC - 1))
                    last.then_inc(down_done, 1)
                pe.wait_ge(down_kept, DC * (b + 1))
                for v in range(2):
                    if b >= 1:
                        pe.wait_ge(added, 2 * (b - 1) + v + 1)
                    for i in range(2):
                        t = 2 * v + i
                        for c in range(DC):
                            last = nc.tensor.matmul(sb.ps[:, 6 + v, i * D:(i + 1) * D],
                                                    f.rT[:, c, t * P:(t + 1) * P], f.wo[:, c, :],
                                                    start=(c == 0), stop=(c == DC - 1))
                    last.then_inc(out_done, 1)

        @block.scalar
        def _(act):
            act.wait_ge(r1_done, 1)
            nc.scalar.activation(f.r1[:, :], sb.ps[:, 0, 0:B], ACT.Gelu, bias=f.bp1[:, 0:1]).then_inc(r1_kept, 1)
            for b in range(B):
                act.wait_ge(loaded[b % 2], 64 * (b // 2 + 1))
                for mo in range(FC):
                    n = b * FC + mo
                    act.wait_ge(up_done, n + 1)
                    if b >= 2 and mo == 0:
                        act.wait_ge(down_done, DC * (b - 1))
                    nc.scalar.activation(f.h[:, b % 2, mo, :], sb.ps[:, n % 4, :], ACT.Gelu,
                                         bias=f.b1[:, b % 2, mo:mo + 1]).then_inc(gelu_done, 1)

        @block.vector
        def _(dve):
            dve.wait_ge(r2_done, 1)
            nc.vector.tensor_tensor(f.logits[:, :], sb.ps[0:B, 1, 0:E0], f.bp2[:, :], ALU.add).then_inc(logits_kept, 1)
            dve.wait_ge(logits_kept, 1)
            nc.vector.max(f.top[:, :], f.logits[:, :]).then_inc(top_done, 1)
            dve.wait_ge(top_done, 1)
            nc.vector.max_index(f.idx[:, :], f.top[:, :], f.logits[:, :]).then_inc(idx_done, 1)
            for b in range(B):
                for mo in range(DC):
                    dve.wait_ge(down_done, DC * b + mo + 1)
                    if b >= 1 and mo == 0:
                        dve.wait_ge(out_done, 2 * b)
                    nc.vector.tensor_scalar(f.rT[:, mo, :], sb.ps[:, 4 + mo, :], f.b2[:, b % 2, mo:mo + 1], None,
                                            ALU.add).then_inc(down_kept, 1)
                for v in range(2):
                    t = QT * b + 2 * v
                    dve.wait_ge(out_done, 2 * b + v + 1)
                    dve.wait_ge(hid_added, 2 * (2 * b + v + 1))
                    xs = sb.x[:, t:t + 2, :].rearrange("p a d -> p (a d)")
                    nc.vector.scalar_tensor_tensor(xs, sb.ps[:, 6 + v, :], f.gate03, xs,
                                                   ALU.mult, ALU.add).then_inc(added, 1)

        @block.gpsimd
        def _(pool):
            for v in range(TT // 2):
                xs, hs = sb.x[:, 2 * v:2 * v + 2, :], f.gh[:, v % 2, :, :]
                nc.gpsimd.tensor_tensor(xs, xs, f.bo[:, :].unsqueeze(1).to_broadcast([P, 2, D]),
                                        ALU.add).then_inc(hid_added, 1)
                if v >= 2:
                    pool.wait_ge(hid_added, 2 * (v - 1))
                nc.gpsimd.tensor_scalar(hs, sb.tok[:, 2 * v:2 * v + 2, :], f.gate, None, ALU.mult).then_inc(f.scaled, 1)
                pool.wait_ge(f.scaled, v + 1)
                pool.wait_ge(hid_added, 2 * v + 1)
                nc.gpsimd.tensor_tensor(xs, xs, hs, ALU.add).then_inc(hid_added, 1)

        @block.sync
        def _(sp):
            sp.wait_ge(idx_done, 1)
            for b in range(B):
                e = sp.value_load(f.idx[b:b + 1, 0:1], min_val=0, max_val=E0 - 1)
                if b >= 2:
                    sp.wait_ge(down_done, DC * (b - 1))
                    sp.wait_ge(down_kept, DC * (b - 1))
                s = loaded[b % 2]
                sp.dma_start(f.w1[:, b % 2, :, :], args["L0_ffn_W1"][bass.ds(e, 1), :, :].rearrange(
                    "e (c p) f -> (e p) c f", p=P)).then_inc(s, 16)
                sp.dma_start(f.w2[:, b % 2, :, :], args["L0_ffn_W2"][bass.ds(e, 1), :, :].rearrange(
                    "e (c p) f -> (e p) c f", p=P)).then_inc(s, 16)
                sp.dma_start(f.b1[:, b % 2, :], args["L0_ffn_b1"][bass.ds(e, 1), :, :].rearrange(
                    "e p c -> (e p) c")).then_inc(s, 16)
                sp.dma_start(f.b2[:, b % 2, :], args["L0_ffn_b2"][bass.ds(e, 1), :, :].rearrange(
                    "e p c -> (e p) c")).then_inc(s, 16)


def gating_phase(nc, sem, sb, m, tag):
    logits_done, top_done, idx_done, idxf_done = (sem(tag + n) for n in ("logits_done", "top_done", "idx_done", "idxf_done"))
    exp_done, chain, shared_done = sem(tag + "exp_done"), sem(tag + "chain"), sem(tag + "shared_done")
    E = E1

    with nc.Block() as block:
        @block.tensor
        def _(pe):
            for t in range(TT):
                for c in range(DC):
                    last = nc.tensor.matmul(sb.ps[:, 0, t * 16:t * 16 + E + 1], sb.xT[:, c, t * P:(t + 1) * P],
                                            m.gw[:, c, :], start=(c == 0), stop=(c == DC - 1))
            last.then_inc(logits_done, 1)

        @block.vector
        def _(dve):
            steps = [0]

            def link(ins):
                steps[0] += 1
                ins.then_inc(chain, 1)
                dve.wait_ge(chain, steps[0])

            lg = sb.ps[:, 0, 0:TT * 16].rearrange("p (t w) -> p t w", w=16)
            dve.wait_ge(logits_done, 1)
            for t in range(TT):
                last = nc.vector.max(m.top[:, t, :], lg[:, t, 0:E])
            last.then_inc(top_done, 1)
            dve.wait_ge(top_done, 1)
            link(nc.vector.tensor_tensor(m.e[:, :, :], lg[:, :, 0:E], m.top[:, :, 0:1].to_broadcast([P, TT, E]),
                                         ALU.subtract))
            dve.wait_ge(exp_done, 1)
            link(nc.vector.tensor_reduce(m.sum[:, :], m.e[:, :, :], mybir.AxisListType.X, ALU.add))
            link(nc.vector.reciprocal(m.rsum[:, :], m.sum[:, :]))
            link(nc.vector.tensor_tensor(m.e[:, :, :], m.e[:, :, :], m.rsum[:, :].unsqueeze(2).to_broadcast([P, TT, E]),
                                         ALU.mult))
            for t in range(TT):
                last = nc.vector.max(m.top[:, t, :], m.e[:, t, :])
            link(last)
            for t in range(TT):
                last = nc.vector.max_index(m.idx[:, t, :], m.top[:, t, :], m.e[:, t, :])
            link(last)
            link(nc.vector.tensor_copy(m.idxf[:, :, :], m.idx[:, :, :]))
            iota = m.iota[:, :].unsqueeze(1).to_broadcast([P, TT, E])
            link(nc.vector.tensor_tensor(m.hot[:, 0, :, :], iota, m.idxf[:, :, 0:1].to_broadcast([P, TT, E]), ALU.is_equal))
            link(nc.vector.tensor_tensor(m.hot[:, 1, :, :], iota, m.idxf[:, :, 1:2].to_broadcast([P, TT, E]), ALU.is_equal))
            link(nc.vector.tensor_tensor(m.hot[:, 0, :, :], m.hot[:, 0, :, :], m.hot[:, 1, :, :], ALU.add))
            link(nc.vector.tensor_tensor(m.e[:, :, :], m.e[:, :, :], m.hot[:, 0, :, :], ALU.mult))
            link(nc.vector.tensor_scalar(m.w[:, :, 0:E], m.e[:, :, :], m.gate, None, ALU.mult))
            dve.wait_ge(shared_done, 1)
            link(nc.vector.tensor_scalar(m.w[:, :, E], m.sw[:, :], m.gate, None, ALU.mult))

        @block.scalar
        def _(act):
            lg = sb.ps[:, 0, 0:TT * 16].rearrange("p (t w) -> p t w", w=16)
            act.wait_ge(chain, 1)
            nc.scalar.activation(m.e[:, :, :], m.e[:, :, :], ACT.Exp).then_inc(exp_done, 1)
            nc.scalar.activation(m.sw[:, :], lg[:, :, E], ACT.Sigmoid).then_inc(shared_done, 1)

        @block.gpsimd
        def _(pool):
            pool.nop().then_inc(idxf_done, 1)
            pool.nop().then_inc(idx_done, 1)


def expert_phase(nc, sem, sb, m, args, out, tag):
    loaded = [sem(tag + f"loaded{i}") for i in range(2)]
    up_done, silu_done, prod_done = sem(tag + "up_done"), sem(tag + "silu_done"), sem(tag + "prod_done")
    down_done, added = sem(tag + "down_done"), sem(tag + "added")
    out_done = sem(tag + "out_done")
    IC = chunks(I1)
    NE = E1 + SI // I1
    UN = len(IC) * B

    with nc.Block() as block:
        @block.sync
        def _(sp):
            def load(e, par):
                s = loaded[par]
                sp.dma_start(m.gu[:, par, :, :], args["gate_up"][bass.ds(e, 1), :, :].rearrange(
                    "e (c p) f -> (e p) c f", p=P)).then_inc(s, 16)
                d = args["down"][bass.ds(e, 1), :, :]
                for i, (a, n) in enumerate(IC):
                    sp.dma_start(m.dn[0:n, par, i, :], d[:, a:a + n, :].rearrange("e p f -> (e p) f")).then_inc(s, 16)
            load(0, 0)
            load(1, 1)
            with sp.Fori(0, NE // 2 - 1) as ee:
                for par in range(2):
                    sp.wait_ge(down_done, ee * (2 * TT) + (par + 1) * TT + 2 * QT)
                    load(ee * 2 + (par + 2), par)
            for g in range(4):
                sp.wait_ge(added, NE * TT - TT + 4 * (g + 1) + 4)
                sp.dma_start(out.rearrange("b (t p) d -> p (b t) d", p=P)[:, 4 * g:4 * g + 4, :],
                             sb.x[:, 4 * g:4 * g + 4, :]).then_inc(out_done, 16)
            sp.wait_ge(out_done, 64)

        LOADS = 1 + len(IC)

        def experts(eng, body):
            with eng.Fori(0, NE // 2) as ee:
                for par in range(2):
                    body(ee, par)

        @block.tensor
        def _(pe):
            pe.nop().then_inc(down_done, 2 * QT)

            def up(ee, par, b, i):
                a, n = IC[i]
                k = par * UN + b * len(IC) + i
                pe.wait_ge(prod_done, ee * (2 * UN) + k + 1)
                for half in range(2):
                    for c in range(DC):
                        last = nc.tensor.matmul(sb.ps[0:n, 2 * (k % 2) + half, :],
                                                m.gu[:, par, c, half * I1 + a:half * I1 + a + n],
                                                sb.xT[:, c, b * S:(b + 1) * S], start=(c == 0), stop=(c == DC - 1))
                last.then_inc(up_done, 1)

            def down(ee, par, b):
                pe.wait_ge(prod_done, ee * (2 * UN) + par * UN + (b + 1) * len(IC) + 2)
                for q in range(QT):
                    k = par * TT + b * QT + q
                    pe.wait_ge(added, ee * (2 * TT) + k + 1)
                    for i, (a, n) in enumerate(IC):
                        last = nc.tensor.matmul(sb.ps[:, 4 + q, 0:D], m.h[0:n, b % 2, i, q * P:(q + 1) * P],
                                                m.dn[0:n, par, i, :], start=(i == 0), stop=(i == len(IC) - 1))
                    last.then_inc(down_done, 1)

            def body(ee, par):
                pe.wait_ge(loaded[par], (ee + 1) * (16 * LOADS))
                for b in range(B):
                    for i in range(len(IC)):
                        up(ee, par, b, i)
                    if b >= 1:
                        down(ee, par, b - 1)
                down(ee, par, B - 1)
            experts(pe, body)

        @block.scalar
        def _(act):
            act.nop().then_inc(silu_done, 2)

            def body(ee, par):
                for b in range(B):
                    for i, (a, n) in enumerate(IC):
                        k = par * UN + b * len(IC) + i
                        act.wait_ge(up_done, ee * (2 * UN) + k + 1)
                        act.wait_ge(prod_done, ee * (2 * UN) + k + 1)
                        nc.scalar.activation(m.g[0:n, k % 2, :], sb.ps[0:n, 2 * (k % 2), :],
                                             ACT.Silu).then_inc(silu_done, 1)
            experts(act, body)

        @block.vector
        def _(dve):
            dve.nop().then_inc(prod_done, 2)
            dve.nop().then_inc(added, 4)

            def add(ee, par, b):
                for q in range(QT):
                    k = par * TT + b * QT + q
                    t = b * QT + q
                    dve.wait_ge(down_done, ee * (2 * TT) + k + 1 + 2 * QT)
                    wcol = m.w[:, t, :].rearrange("p (u v) -> p u v", v=2)[:, bass.ds(ee, 1), par:par + 1]
                    nc.vector.scalar_tensor_tensor(sb.x[:, t, :], sb.ps[:, 4 + q, 0:D],
                                                   wcol.rearrange("p u v -> p (u v)"), sb.x[:, t, :],
                                                   ALU.mult, ALU.add).then_inc(added, 1)

            def body(ee, par):
                for b in range(B):
                    for i, (a, n) in enumerate(IC):
                        k = par * UN + b * len(IC) + i
                        dve.wait_ge(silu_done, ee * (2 * UN) + k + 1 + 2)
                        if i == 0:
                            dve.wait_ge(down_done, ee * (2 * TT) + par * TT + (b + 1) * QT)
                        nc.vector.tensor_tensor(m.h[0:n, b % 2, i, :], m.g[0:n, k % 2, :],
                                                sb.ps[0:n, 2 * (k % 2) + 1, :], ALU.mult).then_inc(prod_done, 1)
                    if b >= 1:
                        add(ee, par, b - 1)
                add(ee, par, B - 1)
            experts(dve, body)


class Names:
    pass


def build(nc, a, out):
    ctx = ExitStack()
    with ctx:
        names = [0]
        layer_sems, used = [ctx.enter_context(ExitStack())], []

        def sem(name):
            used.append(layer_sems[0].enter_context(nc.semaphore(name)))
            return used[-1]

        def buffers(stack):
            def made(name, shape, dt):
                names[0] += 1
                return stack.enter_context(nc.sbuf_tensor(f"{name}_{names[0]}", shape, dt))
            return made

        def dram(name, shape, dt):
            return nc.dram_tensor(name, shape, dt, kind="Internal").ap()

        sb, buf = Names(), buffers(ctx)
        sb.x = buf("x", [P, TT, D], F32)
        sb.tok = buf("tok", [P, TT, D], F32)
        sb.xT = buf("xT", [P, DC, N], F32)
        sb.ident = buf("ident", [P, P], F32)
        sb.stats = buf("stats", [P, TT, 6], F32)
        sb.mv = buf("mv", [P, TT, 2], F32)
        sb.std = buf("std", [P, TT], F32)
        sb.rstd = buf("rstd", [P, TT], F32)
        sb.gates = buf("gates", [P, 4], F32)
        sb.rawg = buf("rawg", [P, 4], F32)
        sb.gate03 = buf("gate03", [P, 1], F32)
        sb.iota = buf("iota", [P, E1], F32)
        sb.ps = ctx.enter_context(nc.psum_tensor("ps", [P, 8, 512], F32))
        x_loaded = [sem(f"x_loaded{i}") for i in range(4)]
        scratch = Names()
        scratch.keymask = dram("keymask_scratch", [B, S], BF16)
        scratch.qk = [dram(f"qk_scratch{i}", [2, 3, D, N], BF16) for i in range(2)]

        for layer in range(2):
            L = f"L{layer}_"
            with ExitStack() as mem:
                aw, buf = Names(), buffers(mem)
                aw.o = buf("o", [P, DC, D], F32)
                aw.bo = buf("bo", [P, D], F32)
                sb.v = buf("v", [P, TT, D], F32)
                with ExitStack() as pm:
                    t, buf = Names(), buffers(pm)
                    aw.qk = buf("qk", [P, 2, DC, D], F32)
                    aw.v = buf("v", [P, DC, D], F32)
                    aw.bqk = buf("bqk", [P, 2, DC], F32)
                    aw.bv = buf("bv", [P, D], F32)
                    t.cT = buf("cT", [P, DC, N], F32)
                    t.plain = buf("plain", [P, 2, S], F32)
                    t.rest = buf("rest", [P, 2, S], F32)
                    t.parts = buf("parts", [P, 2, 3, S], BF16)
                    t.m8 = buf("m8", [B, S // 4], U32)
                    t.mf = buf("mf", [B, S], BF16)
                    sb.cT, sb.plain, sb.rest, sb.parts = t.cT, t.plain, t.rest, t.parts
                    loads_phase(nc, sem, sb, aw, a, layer, x_loaded, scratch, t)
                    layernorm_phase(nc, sem, sb, x_loaded if layer == 0 else None, f"n{layer}_")
                    s2 = Names()
                    s2.qk = scratch.qk[layer]
                    projection_phase(nc, sem, sb, aw, s2, f"p{layer}_")
                with ExitStack() as am:
                    t, buf = Names(), buffers(am)
                    t.bias = buf("bias", [P, HG if layer == 0 else 1, QT, S], F32)
                    t.qs = buf("qs", [P, 2, HG, S], BF16)
                    t.ks = buf("ks", [P, 2, HG, S], BF16)
                    t.s = buf("s", [P, QT, S], F32)
                    p01 = buf("p", [P, 2, QT, S], F32)
                    t.p = [p01[:, i, :, :] for i in range(2)] + [
                        sb.xT[:, i, :].rearrange("p (t k) -> p t k", t=QT) for i in range(2)]
                    t.pT = buf("pT", [P, HG + 2, QT, S], F32)
                    t.vq = buf("vq", [P, 2, QT, HG, VW], F32)
                    t.oT = buf("oT", [P, S], F32)
                    t.nmax = buf("nmax", [P, 4, QT], F32)
                    t.rsum = buf("rsum", [P, QT, HG], F32)
                    s2.keymask = scratch.keymask
                    attention_setup(nc, sem, sb, t, a, layer, f"s{layer}_")
                    attention_phase(nc, sem, sb, t, s2, a["bias"] if layer == 0 else None, f"a{layer}_")
                aw.gate = sb.gates[:, layer:layer + 1]
                output_phase(nc, sem, sb, aw, f"o{layer}_")
            with ExitStack() as fm:
                if layer == 0:
                    f, buf = Names(), buffers(fm)
                    f.wp1 = buf("wp1", [P, DC, NAV], F32)
                    f.wp2 = buf("wp2", [P, E0], F32)
                    f.bp1 = buf("bp1", [P, 1], F32)
                    f.bp2 = buf("bp2", [B, E0], F32)
                    f.wo = buf("wo", [P, DC, D], F32)
                    f.bo = buf("bo", [P, D], F32)
                    f.r1 = buf("r1", [P, B], F32)
                    f.logits = buf("logits", [B, E0], F32)
                    f.top = buf("top", [B, E0], F32)
                    f.idx = buf("idx", [B, E0], U32)
                    f.w1 = buf("w1", [P, 2, DC, F0], F32)
                    f.w2 = buf("w2", [P, 2, F0 // P, D], F32)
                    f.b1 = buf("b1", [P, 2, F0 // P], F32)
                    f.b2 = buf("b2", [P, 2, DC], F32)
                    f.h = buf("h", [P, 2, F0 // P, S], F32)
                    f.rT = buf("rT", [P, DC, S], F32)
                    f.gh = buf("gh", [P, 2, 2, D], F32)
                    f.gate, f.gate03, f.scaled = sb.gates[:, 2:3], sb.gate03[:, 0:1], sem("hid_scaled")
                    routed_loads(nc, sem, sb, f, a)
                    layernorm_phase(nc, sem, sb, None, "n2_")
                    routed_ffn_phase(nc, sem, sb, f, a, "f_")
                    with nc.Block() as block:
                        @block.sync
                        def _(sp):
                            for s in used:
                                sp.sem_clear(s)
                    layer_sems[0].close()
                    layer_sems[0] = ctx.enter_context(ExitStack())
                else:
                    m, buf = Names(), buffers(fm)
                    m.gw = buf("gw", [P, DC, E1 + 1], F32)
                    m.top = buf("top", [P, TT, 8], F32)
                    m.e = buf("e", [P, TT, E1], F32)
                    m.sum = buf("sum", [P, TT], F32)
                    m.rsum = buf("rsum", [P, TT], F32)
                    m.idx = buf("idx", [P, TT, 8], U32)
                    m.idxf = buf("idxf", [P, TT, 8], F32)
                    m.hot = buf("hot", [P, 2, TT, E1], F32)
                    m.w = buf("w", [P, TT, E1 + 2], F32)
                    m.sw = buf("sw", [P, TT], F32)
                    m.gu = buf("gu", [P, 2, DC, 2 * I1], F32)
                    m.dn = buf("dn", [P, 2, 3, D], F32)
                    m.g = buf("g", [P, 2, S], F32)
                    m.h = buf("h", [P, 2, 3, S], F32)
                    m.gate, m.iota = sb.gates[:, 3:4], sb.iota
                    gw_loaded = sem("gw_loaded")
                    with nc.Block() as block:
                        @block.sync
                        def _(sp):
                            sp.dma_start(m.gw[:, :, :], a["gate_w"].rearrange("(c p) e -> p c e", p=P)).then_inc(gw_loaded, 16)
                            sp.wait_ge(gw_loaded, 16)
                    layernorm_phase(nc, sem, sb, None, "n3_")
                    gating_phase(nc, sem, sb, m, "g_")
                    wcopy = sem("wcopy")
                    with nc.Block() as block:
                        @block.vector
                        def _(dve):
                            nc.vector.tensor_copy(m.w[:, :, E1 + 1], m.w[:, :, E1]).then_inc(wcopy, 1)
                    expert_phase(nc, sem, sb, m, a, out, "e_")


def loads_phase(nc, sem, sb, w, a, layer, x_loaded, scratch, t):
    L = f"L{layer}_xattn_"
    loaded, ready, ready2 = sem(L + "loaded"), sem(L + "ready"), sem(L + "ready2")
    mask_kept, mask_stored = sem(L + "mask_kept"), sem(L + "mask_stored")
    consts = sem(L + "consts")
    with nc.Block() as block:
        @block.sync
        def _(sp):
            n = 0
            if layer == 0:
                sp.dma_start(sb.rawg[:, 0:2], a["g_xattn"].partition_broadcast(P)).then_inc(loaded, 16)
                sp.dma_start(sb.rawg[:, 2:4], a["g_ffn"].partition_broadcast(P)).then_inc(loaded, 16)
                sp.dma_start(t.m8[:, :], a["keymask"]).then_inc(loaded, 16)
                n += 3
                for g in range(4):
                    sp.dma_start(sb.x[:, 4 * g:4 * g + 4, :], a["x"].rearrange("b (t p) d -> p (b t) d", p=P)[:, 4 * g:4 * g + 4, :]
                                 ).then_inc(x_loaded[g], 16)
            for dst, src in ((w.qk[:, 0, :, :], a[L + "Wq"]), (w.qk[:, 1, :, :], a[L + "Wk"]),
                             (w.v[:, :, :], a[L + "Wv"]), (w.o[:, :, :], a[L + "Wo"])):
                sp.dma_start(dst, src.rearrange("(c p) n -> p c n", p=P)).then_inc(loaded, 16)
            sp.dma_start(w.bqk[:, 0, :], a[L + "bq"]).then_inc(loaded, 16)
            sp.dma_start(w.bqk[:, 1, :], a[L + "bk"]).then_inc(loaded, 16)
            sp.dma_start(w.bv[:, :], a[L + "bv"].partition_broadcast(P)).then_inc(loaded, 16)
            sp.dma_start(w.bo[:, :], a[L + "bo"].partition_broadcast(P)).then_inc(loaded, 16)
            sp.dma_start(sb.cT[:, :, :], a["ctxT"].rearrange("(c p) n -> p c n", p=P)).then_inc(loaded, 16)
            n += 9
            sp.wait_ge(loaded, 16 * n)
            sp.nop().then_inc(ready, 1)
            if layer == 0:
                sp.wait_ge(mask_kept, 1)
                sp.dma_start(scratch.keymask, t.mf[:, :]).then_inc(mask_stored, 16)
                sp.wait_ge(mask_stored, 16)

        @block.vector
        def _(dve):
            dve.wait_ge(ready, 1)
            nc.vector.tensor_scalar(w.bqk[:, 0, :], w.bqk[:, 0, :], SCALE, None, ALU.mult)
            if layer == 0:
                nc.vector.tensor_scalar(t.mf[:, :], t.m8[:, :].bitcast(U8), 1.0, -NEG, ALU.subtract, ALU.mult).then_inc(mask_kept, 1)
                dve.wait_ge(ready2, 1)
                nc.vector.tensor_scalar(sb.gate03[:, :], sb.gates[:, 2:3], 0.3, None, ALU.mult)
            else:
                dve.wait_ge(ready, 1)
            if layer == 0:
                nc.vector.tensor_scalar(w.bo[:, :], w.bo[:, :], sb.gates[:, 0:1], None, ALU.mult)
            else:
                nc.vector.tensor_scalar(w.bo[:, :], w.bo[:, :], sb.gates[:, 1:2], None, ALU.mult)

        @block.scalar
        def _(act):
            if layer == 0:
                act.wait_ge(ready, 1)
                nc.scalar.activation(sb.gates[:, :], sb.rawg[:, :], ACT.Tanh).then_inc(ready2, 1)

        @block.gpsimd
        def _(pool):
            if layer == 0:
                nc.gpsimd.memset(sb.ident[:, :], 0.0).then_inc(consts, 1)
                pool.wait_ge(consts, 1)
                nc.gpsimd.affine_select(out=sb.ident[:, :], in_=sb.ident[:, :], compare_op=ALU.not_equal, fill=1.0,
                                        base=0, pattern=[[-1, P]], channel_multiplier=1).then_inc(consts, 1)
                for e in range(E1):
                    nc.gpsimd.memset(sb.iota[:, e:e + 1], float(e))


def attention_setup(nc, sem, sb, at, a, layer, tag):
    loaded, cleared, onesrow = sem(tag + "loaded"), sem(tag + "cleared"), sem(tag + "onesrow")
    with nc.Block() as block:
        @block.gpsimd
        def _(pool):
            nc.gpsimd.memset(at.vq[:, :, :, :, :], 0.0).then_inc(cleared, 1)
            pool.wait_ge(cleared, 1)
            nc.gpsimd.memset(at.vq[:, :, :, :, DH:DH + 1], 1.0).then_inc(cleared, 1)
            if layer == 0:
                pool.wait_ge(cleared, 2)
                nc.gpsimd.memset(at.qs[KS:KS + 1, :, :, :], 1.0)

        if layer == 1:
            @block.sync
            def _(sp):
                sp.dma_start(at.bias[:, 0, :, :], a["mask"].rearrange("(t p) k -> p t k", p=P)).then_inc(loaded, 16)

            @block.vector
            def _(dve):
                dve.wait_ge(loaded, 16)
                nc.vector.tensor_scalar(at.bias[:, 0, :, :], at.bias[:, 0, :, :], MASK_C, None, ALU.mult)


def routed_loads(nc, sem, sb, f, a):
    loaded, ready = sem("rl_loaded"), sem("rl_ready")
    with nc.Block() as block:
        @block.sync
        def _(sp):
            sp.dma_start(f.wp1[:, :, :], a["L0_ffn_Wp1"].rearrange("(c p) n -> p c n", p=P)).then_inc(loaded, 16)
            sp.dma_start(f.wp2[:, :], a["L0_ffn_Wp2"]).then_inc(loaded, 16)
            sp.dma_start(f.bp1[:, :], a["L0_ffn_bp1"].rearrange("(p a) -> p a", a=1)).then_inc(loaded, 16)
            sp.dma_start(f.bp2[:, :], a["L0_ffn_bp2"].partition_broadcast(B)).then_inc(loaded, 16)
            sp.dma_start(f.wo[:, :, :], a["L0_ffn_Wo"].rearrange("(c p) n -> p c n", p=P)).then_inc(loaded, 16)
            sp.dma_start(f.bo[:, :], a["L0_ffn_bo"].partition_broadcast(P)).then_inc(loaded, 16)
            sp.wait_ge(loaded, 96)
            sp.nop().then_inc(ready, 1)

        @block.vector
        def _(dve):
            dve.wait_ge(ready, 1)
            nc.vector.tensor_scalar(f.bo[:, :], f.bo[:, :], sb.gate03[:, 0:1], None, ALU.mult)


def kernel(**inputs):
    import numpy as _np
    import concourse.bacc as _bacc
    from concourse import mybir as _mybir
    from concourse.bass_utils import run_bass_kernel_spmd as _run

    i = {k: _np.asarray(v) for k, v in inputs.items()}
    gate, up = i["L1_ffn_shared_gate_w"], i["L1_ffn_shared_up_w"]
    down = i["L1_ffn_shared_down_w"]
    gate_up = _np.concatenate([i["L1_ffn_experts_gate_up"]] + [
        _np.concatenate([gate[h * I1:(h + 1) * I1], up[h * I1:(h + 1) * I1]], 0)[None] for h in range(2)], 0)
    downs = _np.concatenate([i["L1_ffn_experts_down"]] + [down[None, :, h * I1:(h + 1) * I1] for h in range(2)], 0)
    laid = {
        "x": i["x"],
        "ctxT": i["ctx_1024"].reshape(N, D).T,
        "keymask": i["mask_BxS2_bk1"].view(_np.uint32),
        "mask": i["mask_SxS2_fk1"],
        "bias": i["L0_xattn_relative_bias"][0],
        "g_xattn": i["g_xattn"], "g_ffn": i["g_ffn"],
        "gate_w": _np.concatenate([i["L1_ffn_gate_w"], i["L1_ffn_shared_expert_gate_w"]], 0).T,
        "gate_up": gate_up.transpose(0, 2, 1),
        "down": downs.transpose(0, 2, 1),
    }
    for n in "qkvo":
        laid[f"L0_xattn_W{n}"] = i[f"L0_xattn_W{n}"].T
        laid[f"L1_xattn_W{n}"] = i[f"L1_xattn_W{n}"]
        for l in range(2):
            laid[f"L{l}_xattn_b{n}"] = i[f"L{l}_xattn_b{n}"]
    for n in ("Wp1", "bp1", "Wp2", "bp2", "W1", "b1", "W2", "b2", "Wo", "bo"):
        laid[f"L0_ffn_{n}"] = i[f"L0_ffn_{n}"]

    for n in ("L0_xattn_bq", "L0_xattn_bk", "L1_xattn_bq", "L1_xattn_bk", "L0_ffn_b1", "L0_ffn_b2"):
        v = laid[n]
        laid[n] = _np.swapaxes(v.reshape(*v.shape[:-1], -1, P), -1, -2)

    nc = _bacc.Bacc("TRN2", target_bir_lowering=False, num_devices=1)
    arrays, args = {}, {}
    for name, v in laid.items():
        v = _np.ascontiguousarray(v)
        arrays[f"in_{name}"] = v
        args[name] = nc.dram_tensor(f"in_{name}", v.shape, _mybir.dt.from_np(v.dtype), kind="ExternalInput").ap()
    out = nc.dram_tensor("out_0", (B, S, D), F32, kind="ExternalOutput").ap()
    build(nc, args, out)
    r = _run(nc, [arrays], core_ids=[0])
    return r.results[0]["out_0"]
```

```python
from contextlib import ExitStack

import concourse.bass as bass
from concourse import mybir

ALU = mybir.AluOpType
ACT = mybir.ActivationFunctionType
F32 = mybir.dt.float32
BF16 = mybir.dt.bfloat16
U32 = mybir.dt.uint32
U8 = mybir.dt.uint8
I32 = mybir.dt.int32

P = 128
B, S, D = 4, 512, 256
H, DH = 16, 16
N = B * S
DC = D // P
TT = N // P
QT = S // P
E0, F0, NAV = 8, 512, 128
E1, I1, SI = 8, 352, 704
HG = 4
VW = 32
SCALE = 1.0 / DH ** 0.5
EPS = 1e-5
NEG = -1.0e30
MASK_C = -1000000000.0
Q_PARTS = [0, 1, 2, 0, 1, 0]
K_PARTS = [0, 0, 0, 1, 1, 2]
KS = DH * len(Q_PARTS)
SLOT_TILES = -(-(2 * TT + E1 - 1) // 4) * 4


def chunks(n):
    return [(a, min(P, n - a)) for a in range(0, n, P)]


def layernorm_phase(nc, sem, sb, x_loaded, tag):
    stats_done, mv_done, var_ready = sem(tag + "stats_done"), sem(tag + "mv_done"), sem(tag + "var_ready")
    std_ready, rstd_ready = sem(tag + "std_ready"), sem(tag + "rstd_ready")
    norm_done, turned, copied = sem(tag + "norm_done"), sem(tag + "turned"), sem(tag + "copied")
    copied_act = sem(tag + "copied_act")
    G = TT // 4

    with nc.Block() as block:
        @block.vector
        def _(dve):
            for t in range(TT):
                if x_loaded is not None and t % 4 == 0:
                    dve.wait_ge(x_loaded[t // 4], 16)
                nc.vector.bn_stats(sb.stats[:, t, :], sb.x[:, t, :]).then_inc(stats_done, 1)
            for t in range(TT):
                dve.wait_ge(stats_done, t + 1)
                nc.vector.bn_aggr(sb.mv[:, t, :], sb.stats[:, t, :]).then_inc(mv_done, 1)
            dve.wait_ge(mv_done, TT)
            nc.vector.tensor_scalar(sb.rstd[:, :], sb.mv[:, :, 1], EPS, None, ALU.add).then_inc(var_ready, 1)
            dve.wait_ge(std_ready, 1)
            nc.vector.reciprocal(sb.rstd[:, :], sb.std[:, :]).then_inc(rstd_ready, 1)
            dve.wait_ge(rstd_ready, 1)
            for t in range(TT):
                nc.vector.tensor_scalar(sb.tok[:, t, :], sb.x[:, t, :], sb.mv[:, t, 0:1], sb.rstd[:, t:t + 1],
                                        ALU.subtract, ALU.mult).then_inc(norm_done, 1)
                if t % 4 == 3:
                    g = t // 4
                    dve.wait_ge(turned, 2 * g + 1)
                    nc.vector.tensor_copy(sb.xT[:, 0, g * S:(g + 1) * S], sb.ps[:, (2 * g) % 8, :]).then_inc(copied, 1)

        @block.scalar
        def _(act):
            act.wait_ge(var_ready, 1)
            nc.scalar.activation(sb.std[:, :], sb.rstd[:, :], ACT.Sqrt).then_inc(std_ready, 1)
            for g in range(G):
                act.wait_ge(turned, 2 * g + 2)
                nc.scalar.activation(sb.xT[:, 1, g * S:(g + 1) * S], sb.ps[:, (2 * g + 1) % 8, :],
                                     ACT.Copy).then_inc(copied_act, 1)

        @block.tensor
        def _(pe):
            for g in range(G):
                for c in range(DC):
                    for i in range(4):
                        t = 4 * g + i
                        pe.wait_ge(norm_done, t + 1)
                        last = nc.tensor.transpose(sb.ps[:, (2 * g + c) % 8, i * P:(i + 1) * P],
                                                   sb.tok[:, t, c * P:(c + 1) * P], sb.ident[:, :])
                    last.then_inc(turned, 1)


def projection_phase(nc, sem, sb, w, dram, tag):
    proj_done, plain_done, head_done = sem(tag + "proj_done"), sem(tag + "plain_done"), sem(tag + "head_done")
    rest_done, mid_done, low_done = sem(tag + "rest_done"), sem(tag + "mid_done"), sem(tag + "low_done")
    stored = [sem(tag + f"stored{i}") for i in range(2)]
    v_done, v_copied = sem(tag + "v_done"), sem(tag + "v_copied")
    NT = 2 * DC * B

    def place(n):
        return n // (DC * B), n // B % DC, n % B

    with nc.Block() as block:
        @block.tensor
        def _(pe):
            for n in range(NT):
                which, mo, b = place(n)
                src = sb.cT if which else sb.xT
                if n >= 4:
                    pe.wait_ge(plain_done, n - 3)
                for c in range(DC):
                    last = nc.tensor.matmul(sb.ps[:, n % 4, :], w.qk[:, which, c, mo * P:(mo + 1) * P],
                                            src[:, c, b * S:(b + 1) * S], start=(c == 0), stop=(c == DC - 1))
                last.then_inc(proj_done, 1)
            for v in range(TT // 2):
                if v >= 4:
                    pe.wait_ge(v_copied, v - 3)
                for i in range(2):
                    t = 2 * v + i
                    for c in range(DC):
                        last = nc.tensor.matmul(sb.ps[:, 4 + v % 4, i * D:(i + 1) * D],
                                                sb.cT[:, c, t * P:(t + 1) * P], w.v[:, c, :],
                                                start=(c == 0), stop=(c == DC - 1))
                last.then_inc(v_done, 1)

        @block.scalar
        def _(act):
            for n in range(NT):
                which, mo, b = place(n)
                act.wait_ge(proj_done, n + 1)
                if n >= 2:
                    act.wait_ge(rest_done, n - 1)
                nc.scalar.activation(sb.plain[:, n % 2, :], sb.ps[:, n % 4, :], ACT.Identity,
                                     bias=w.bqk[:, which, mo:mo + 1],
                                     scale=1.0 if which else SCALE).then_inc(plain_done, 1)

        @block.vector
        def _(dve):
            for n in range(NT):
                dve.wait_ge(plain_done, n + 1)
                if n >= 2:
                    dve.wait_ge(stored[n % 2], 16 * (n // 2))
                nc.vector.tensor_copy(sb.parts[:, n % 2, 0, :], sb.plain[:, n % 2, :]).then_inc(head_done, 1)
                dve.wait_ge(head_done, n + 1)
                if n >= 2:
                    dve.wait_ge(low_done, n - 1)
                nc.vector.tensor_tensor(sb.rest[:, n % 2, :], sb.plain[:, n % 2, :], sb.parts[:, n % 2, 0, :],
                                        ALU.subtract).then_inc(rest_done, 1)
                dve.wait_ge(rest_done, n + 1)
                nc.vector.tensor_copy(sb.parts[:, n % 2, 1, :], sb.rest[:, n % 2, :]).then_inc(mid_done, 1)
            for v in range(TT // 2):
                dve.wait_ge(v_done, v + 1)
                nc.vector.tensor_tensor(
                    sb.v[:, 2 * v:2 * v + 2, :], sb.ps[:, 4 + v % 4, :].rearrange("p (a d) -> p a d", a=2),
                    w.bv[:, :].unsqueeze(1).to_broadcast([P, 2, D]), ALU.add).then_inc(v_copied, 1)

        @block.gpsimd
        def _(pool):
            for n in range(NT):
                pool.wait_ge(mid_done, n + 1)
                nc.gpsimd.tensor_tensor(sb.parts[:, n % 2, 2, :], sb.rest[:, n % 2, :], sb.parts[:, n % 2, 1, :],
                                        ALU.subtract).then_inc(low_done, 1)

        @block.sync
        def _(sp):
            for n in range(NT):
                which, mo, b = place(n)
                sp.wait_ge(low_done, n + 1)
                sp.dma_start(dram.qk[which, :, mo * P:(mo + 1) * P, b * S:(b + 1) * S].rearrange("s p t -> p s t"),
                             sb.parts[:, n % 2, :, :]).then_inc(stored[n % 2], 16)
            for i in range(2):
                sp.wait_ge(stored[i], 16 * (NT // 2))


def attention_phase(nc, sem, sb, at, dram, bias_dram, tag):
    per_head_bias = bias_dram is not None
    K = KS + 1 if per_head_bias else KS
    LOADS = 2 * len(Q_PARTS) + (1 if per_head_bias else 0)
    qk_loaded = [sem(tag + f"qk_loaded{i}") for i in range(2)]
    bias_loaded = [sem(tag + f"bias_loaded{j}") for j in range(HG)]
    scores_done = sem(tag + "scores_done")
    biased = sem(tag + "biased")
    exp_done = sem(tag + "exp_done")
    turned = sem(tag + "turned")
    kept0, kept1 = sem(tag + "kept0"), sem(tag + "kept1")
    v_ready = sem(tag + "v_ready")
    av_done = sem(tag + "av_done")
    out_kept = sem(tag + "out_kept")
    out_turned = sem(tag + "out_turned")
    sums_ready = sem(tag + "sums_ready")
    out_done = sem(tag + "out_done")
    granted = sem(tag + "granted")
    GROUPS = H // HG
    M = HG * B

    def groups(eng, body):
        body(0, True, False)
        with eng.Fori(1, GROUPS - 1) as hg:
            body(hg, False, False)
        body(GROUPS - 1, False, True)

    def before(hg, b):
        return (hg, b - 1) if b else (hg - 1, B - 1)

    def slot(b, j):
        return j + HG * (b % 2) if j < 2 else j

    with nc.Block() as block:
        @block.sync
        def _(sp):
            def load_qk(hg, b):
                sp.wait_ge(scores_done, (hg * 4 + b) * 16 + 16)
                for s in range(len(Q_PARTS)):
                    for which, part, dst in ((0, Q_PARTS[s], at.qs), (1, K_PARTS[s], at.ks)):
                        src = dram.qk[which, part, :, b * S:(b + 1) * S].rearrange("(g j d) t -> g d j t", j=HG, d=DH)
                        sp.dma_start(dst[s * DH:(s + 1) * DH, b % 2, :, :],
                                     src[bass.ds(hg, 1), :, :, :].rearrange("g d j t -> (g d) j t")
                                     ).then_inc(qk_loaded[b % 2], 16)
                if per_head_bias:
                    sp.dma_start(at.ks[KS:KS + 1, b % 2, :, :],
                                 dram.keymask[b:b + 1, :].unsqueeze(1).to_broadcast([1, HG, S])
                                 ).then_inc(qk_loaded[b % 2], 16)

            def load_bias(hg, j):
                src = bias_dram.rearrange("(g j) (t p) k -> g j p t k", j=HG, p=P)
                sp.dma_start(at.bias[:, j, :, :], src[bass.ds(hg, 1), j, :, :, :].rearrange("g p t k -> (g p) t k")
                             ).then_inc(bias_loaded[j], 16)

            load_qk(0, 0)
            if per_head_bias:
                for j in range(HG):
                    load_bias(0, j)

            def body(hg, first, last):
                for b in range(1, B):
                    load_qk(hg, b)
                if not last:
                    load_qk(hg + 1, 0)
                    for j in range(HG if per_head_bias else 0):
                        sp.wait_ge(biased, hg * 64 + 4 * (M - HG + j) + 4 + 2)
                        load_bias(hg + 1, j)
            groups(sp, body)

        @block.tensor
        def _(pe):
            pe.nop().then_inc(scores_done, 32)

            def scores(hg, m, qts):
                b, j = m % M // HG, m % HG
                for qt in qts:
                    if j == 0 and qt == 0:
                        pe.wait_ge(qk_loaded[b % 2], (hg * 2 + (m // HG) // 2 + 1) * (16 * LOADS))
                    pe.wait_ge(biased, hg * 64 + 4 * m + qt + 1)
                    nc.tensor.matmul(sb.ps[:, qt % 2, :], at.qs[0:K, b % 2, j, qt * P:(qt + 1) * P],
                                     at.ks[0:K, b % 2, j, :], start=True, stop=True).then_inc(scores_done, 1)

            def turn(hg, m, kt):
                if kt == 0:
                    pe.wait_ge(exp_done, hg * 64 + 4 * m + 4 + 4)
                if kt % 2 == 0:
                    pe.wait_ge(kept1 if kt else kept0, hg * M + m + 1)
                for qt in range(QT):
                    last = nc.tensor.transpose(sb.ps[:, 2 + kt, qt * P:(qt + 1) * P],
                                               at.p[m % 4][:, qt, kt * P:(kt + 1) * P], sb.ident[:, :])
                if kt % 2 == 1:
                    last.then_inc(turned, 1)

            def values(hg, b, kt):
                pe.wait_ge(kept1 if kt >= 2 else kept0, hg * M + HG * b + HG + 1)
                if kt == 0:
                    pe.wait_ge(v_ready, hg * B + b + 1)
                    pe.wait_ge(out_kept, hg * B + b + 1)
                for j in range(HG):
                    last = nc.tensor.matmul(sb.ps[VW * j:VW * (j + 1), 6, :], at.vq[:, b % 2, kt, j, :],
                                            at.pT[:, slot(b, j), kt, :], start=(kt == 0), stop=(kt == QT - 1))
                if kt == QT - 1:
                    last.then_inc(av_done, 1)

            def turn_out(hg, b):
                pe.wait_ge(out_kept, hg * B + b + 2)
                pe.wait_ge(out_done, hg * B + b + 1)
                for qt in range(QT):
                    last = nc.tensor.transpose(sb.ps[:, 7, qt * P:(qt + 1) * P], at.oT[:, qt * P:(qt + 1) * P],
                                               sb.ident[:, :])
                last.then_inc(out_turned, 1)

            scores(0, 0, range(QT))
            scores(0, 1, (0, 1))

            def body(hg, first, last):
                for m in range(M):
                    b, j = m // HG, m % HG
                    earlier = not (first and b == 0)
                    next1, next2 = not (last and m + 1 >= M), not (last and m + 2 >= M)
                    if next1:
                        scores(hg, m + 1, (2,))
                    if earlier and j < 3:
                        values(*before(hg, b), (0, 2, 3)[j])
                    turn(hg, m, 0)
                    if next1:
                        scores(hg, m + 1, (3,))
                    turn(hg, m, 1)
                    if next2:
                        scores(hg, m + 2, (0,))
                    if earlier and j == 0:
                        values(*before(hg, b), 1)
                    if earlier and j == 3:
                        turn_out(*before(hg, b))
                    turn(hg, m, 2)
                    if next2:
                        scores(hg, m + 2, (1,))
                    turn(hg, m, 3)
                if last:
                    for kt in range(QT):
                        values(hg, B - 1, kt)
                    turn_out(hg, B - 1)
            groups(pe, body)

        @block.vector
        def _(dve):
            dve.nop().then_inc(biased, 2)
            dve.nop().then_inc(kept1, 1)
            dve.nop().then_inc(out_done, 1)

            def add_bias(hg, m, qts):
                b, j = m % M // HG, m % HG
                for qt in qts:
                    u = 4 * m + qt + 1
                    if per_head_bias and b == 0 and qt == 0:
                        dve.wait_ge(bias_loaded[j], (hg + (m // M + 1)) * 16)
                    dve.wait_ge(scores_done, hg * 64 + (u + 32))
                    dve.wait_ge(exp_done, hg * 64 + u)
                    dve.sem_inc(granted, 1)
                    nc.vector.tensor_tensor_reduce(
                        at.s[:, qt, :], sb.ps[:, qt % 2, :], at.bias[:, j if per_head_bias else 0, qt, :],
                        -1.0, 3.0e38, ALU.add, ALU.min, at.nmax[:, m % 4, qt:qt + 1]).then_inc(biased, 1)

            def keep(hg, m):
                dve.wait_ge(turned, (hg * M + m) * 2 + 2 + 8)
                nc.vector.tensor_copy(at.pT[:, slot(m // HG, m % HG), 2:4, :], sb.ps[:, 4:6, :]).then_inc(kept1, 1)

            def normalise(hg, b):
                dve.wait_ge(out_turned, hg * B + b + 2)
                o = sb.ps[:, 7, :].rearrange("p (t j w) -> p t j w", t=QT, j=HG)
                nc.vector.reciprocal(at.rsum[:, :, :], o[:, :, :, DH]).then_inc(sums_ready, 1)
                dve.wait_ge(sums_ready, hg * B + b + 1)
                dst = sb.tok[:, b * QT:(b + 1) * QT, :].rearrange("p t (g f) -> p g t f", g=GROUPS)
                nc.vector.tensor_tensor(
                    dst[:, bass.ds(hg, 1), :, :].rearrange("p g t (j d) -> p (g t) j d", j=HG),
                    o[:, :, :, 0:DH], at.rsum[:, :, :].unsqueeze(3).to_broadcast([P, QT, HG, DH]),
                    ALU.mult).then_inc(out_done, 1)

            add_bias(0, 0, range(QT))
            add_bias(0, 1, (0, 1))

            def body(hg, first, last):
                for m in range(M):
                    b, j = m // HG, m % HG
                    if not (last and m + 1 >= M):
                        add_bias(hg, m + 1, (2,))
                    if not (first and m == 0):
                        keep(hg, m - 1)
                    if not (last and m + 1 >= M):
                        add_bias(hg, m + 1, (3,))
                    if not (last and m + 2 >= M):
                        add_bias(hg, m + 2, (0, 1))
                    if j == 3 and not (first and b == 0):
                        normalise(*before(hg, b))
                if last:
                    keep(hg, M - 1)
                    normalise(hg, B - 1)
            groups(dve, body)

        @block.scalar
        def _(act):
            act.nop().then_inc(exp_done, 4)
            act.nop().then_inc(kept0, 1)
            act.nop().then_inc(out_kept, 1)

            def exps(hg, m, qts):
                for qt in qts:
                    if qt == 0:
                        act.wait_ge(turned, (hg * M + m) * 2 + 2)
                    act.wait_ge(biased, hg * 64 + 4 * m + qt + 1 + 2)
                    nc.scalar.activation(at.p[m % 4][:, qt, :], at.s[:, qt, :], ACT.Exp,
                                         bias=at.nmax[:, m % 4, qt:qt + 1], scale=-1.0).then_inc(exp_done, 1)

            def keep(hg, m):
                act.wait_ge(turned, (hg * M + m) * 2 + 1 + 8)
                nc.scalar.activation(at.pT[:, slot(m // HG, m % HG), 0:2, :], sb.ps[:, 2:4, :], ACT.Copy).then_inc(kept0, 1)

            def keep_out(hg, b):
                act.wait_ge(av_done, hg * B + b + 1 + 2)
                act.wait_ge(out_turned, hg * B + b + 1)
                nc.scalar.activation(at.oT[:, :], sb.ps[:, 6, :], ACT.Copy).then_inc(out_kept, 1)

            exps(0, 0, range(QT))
            exps(0, 1, (0, 1))

            def body(hg, first, last):
                for m in range(M):
                    b, j = m // HG, m % HG
                    if not (last and m + 1 >= M):
                        exps(hg, m + 1, (2, 3))
                    keep(hg, m)
                    if j == 2 and not (first and b == 0):
                        keep_out(*before(hg, b))
                    if not (last and m + 2 >= M):
                        exps(hg, m + 2, (0, 1))
                if last:
                    keep_out(hg, B - 1)
            groups(act, body)

        @block.gpsimd
        def _(pool):
            pool.nop().then_inc(turned, 8)
            pool.nop().then_inc(av_done, 2)
            pool.nop().then_inc(out_turned, 1)

            def body(hg, first, last):
                for b in range(B):
                    pool.wait_ge(av_done, hg * B + b + 1)
                    src = sb.v[:, b * QT:(b + 1) * QT, :].rearrange("p t (g f) -> p g t f", g=GROUPS)
                    nc.gpsimd.tensor_copy(
                        at.vq[:, b % 2, :, :, 0:DH],
                        src[:, bass.ds(hg, 1), :, :].rearrange("p g t (j d) -> p (g t) j d", j=HG)).then_inc(v_ready, 1)
            groups(pool, body)


def output_phase(nc, sem, sb, w, tag):
    turned, copied, copied_act = sem(tag + "turned"), sem(tag + "copied"), sem(tag + "copied_act")
    bias_added, proj_done, added = sem(tag + "bias_added"), sem(tag + "proj_done"), sem(tag + "added")
    G = TT // 4

    with nc.Block() as block:
        @block.tensor
        def _(pe):
            for g in range(G):
                for c in range(DC):
                    if g >= 2:
                        pe.wait_ge(copied_act if c else copied, g - 1)
                    for i in range(4):
                        last = nc.tensor.transpose(sb.ps[:, 2 * (g % 2) + c, i * P:(i + 1) * P],
                                                   sb.tok[:, 4 * g + i, c * P:(c + 1) * P], sb.ident[:, :])
                    last.then_inc(turned, 1)
            for v in range(TT // 2):
                if v % 2 == 0:
                    pe.wait_ge(copied, v // 2 + 1)
                    pe.wait_ge(copied_act, v // 2 + 1)
                if v >= 4:
                    pe.wait_ge(added, v - 3)
                for i in range(2):
                    t = 2 * v + i
                    for c in range(DC):
                        last = nc.tensor.matmul(sb.ps[:, 4 + v % 4, i * D:(i + 1) * D],
                                                sb.xT[:, c, t * P:(t + 1) * P], w.o[:, c, :],
                                                start=(c == 0), stop=(c == DC - 1))
                last.then_inc(proj_done, 1)

        @block.scalar
        def _(act):
            for g in range(G):
                act.wait_ge(turned, 2 * g + 2)
                nc.scalar.activation(sb.xT[:, 1, g * S:(g + 1) * S], sb.ps[:, 2 * (g % 2) + 1, :],
                                     ACT.Copy).then_inc(copied_act, 1)

        @block.gpsimd
        def _(pool):
            for v in range(TT // 2):
                nc.gpsimd.tensor_tensor(sb.x[:, 2 * v:2 * v + 2, :], sb.x[:, 2 * v:2 * v + 2, :],
                                        w.bo[:, :].unsqueeze(1).to_broadcast([P, 2, D]),
                                        ALU.add).then_inc(bias_added, 1)

        @block.vector
        def _(dve):
            for g in range(G):
                dve.wait_ge(turned, 2 * g + 1)
                nc.vector.tensor_copy(sb.xT[:, 0, g * S:(g + 1) * S], sb.ps[:, 2 * (g % 2), :]).then_inc(copied, 1)
            for v in range(TT // 2):
                dve.wait_ge(bias_added, v + 1)
                dve.wait_ge(proj_done, v + 1)
                xs = sb.x[:, 2 * v:2 * v + 2, :].rearrange("p a d -> p (a d)")
                nc.vector.scalar_tensor_tensor(xs, sb.ps[:, 4 + v % 4, :], w.gate, xs,
                                               ALU.mult, ALU.add).then_inc(added, 1)


def routed_ffn_phase(nc, sem, sb, f, args, tag):
    r1_done, r1_kept, r2_done = sem(tag + "r1_done"), sem(tag + "r1_kept"), sem(tag + "r2_done")
    logits_kept, top_done, idx_done = sem(tag + "logits_kept"), sem(tag + "top_done"), sem(tag + "idx_done")
    loaded = [sem(tag + f"loaded{i}") for i in range(2)]
    up_done, gelu_done, down_done = sem(tag + "up_done"), sem(tag + "gelu_done"), sem(tag + "down_done")
    down_kept, out_done, added = sem(tag + "down_kept"), sem(tag + "out_done"), sem(tag + "added")
    hid_added = sem(tag + "hid_added")
    FC = F0 // P

    with nc.Block() as block:
        @block.tensor
        def _(pe):
            last_tokens = sb.xT[:, :, :].rearrange("p c (b s) -> p c b s", b=B)[:, :, :, S - 1]
            for c in range(DC):
                last = nc.tensor.matmul(sb.ps[:, 0, 0:B], f.wp1[:, c, :], last_tokens[:, c, :],
                                        start=(c == 0), stop=(c == DC - 1))
            last.then_inc(r1_done, 1)
            pe.wait_ge(r1_kept, 1)
            nc.tensor.matmul(sb.ps[0:B, 1, 0:E0], f.r1[:, :], f.wp2[:, :], start=True, stop=True).then_inc(r2_done, 1)
            for b in range(B):
                pe.wait_ge(loaded[b % 2], 64 * (b // 2 + 1))
                for mo in range(FC):
                    n = b * FC + mo
                    if n >= 4:
                        pe.wait_ge(gelu_done, n - 3)
                    elif n < 2:
                        pe.wait_ge(logits_kept, 1)
                    for c in range(DC):
                        last = nc.tensor.matmul(sb.ps[:, n % 4, :], f.w1[:, b % 2, c, mo * P:(mo + 1) * P],
                                                sb.xT[:, c, b * S:(b + 1) * S], start=(c == 0), stop=(c == DC - 1))
                    last.then_inc(up_done, 1)
                pe.wait_ge(gelu_done, FC * (b + 1))
                for mo in range(DC):
                    if b >= 1:
                        pe.wait_ge(down_kept, DC * (b - 1) + mo + 1)
                    for c in range(FC):
                        last = nc.tensor.matmul(sb.ps[:, 4 + mo, :], f.w2[:, b % 2, c, mo * P:(mo + 1) * P],
                                                f.h[:, b % 2, c, :], start=(c == 0), stop=(c == FC - 1))
                    last.then_inc(down_done, 1)
                pe.wait_ge(down_kept, DC * (b + 1))
                for v in range(2):
                    if b >= 1:
                        pe.wait_ge(added, 2 * (b - 1) + v + 1)
                    for i in range(2):
                        t = 2 * v + i
                        for c in range(DC):
                            last = nc.tensor.matmul(sb.ps[:, 6 + v, i * D:(i + 1) * D],
                                                    f.rT[:, c, t * P:(t + 1) * P], f.wo[:, c, :],
                                                    start=(c == 0), stop=(c == DC - 1))
                    last.then_inc(out_done, 1)

        @block.scalar
        def _(act):
            act.wait_ge(r1_done, 1)
            nc.scalar.activation(f.r1[:, :], sb.ps[:, 0, 0:B], ACT.Gelu, bias=f.bp1[:, 0:1]).then_inc(r1_kept, 1)
            for b in range(B):
                act.wait_ge(loaded[b % 2], 64 * (b // 2 + 1))
                for mo in range(FC):
                    n = b * FC + mo
                    act.wait_ge(up_done, n + 1)
                    if b >= 2 and mo == 0:
                        act.wait_ge(down_done, DC * (b - 1))
                    nc.scalar.activation(f.h[:, b % 2, mo, :], sb.ps[:, n % 4, :], ACT.Gelu,
                                         bias=f.b1[:, b % 2, mo:mo + 1]).then_inc(gelu_done, 1)

        @block.vector
        def _(dve):
            dve.wait_ge(r2_done, 1)
            nc.vector.tensor_tensor(f.logits[:, :], sb.ps[0:B, 1, 0:E0], f.bp2[:, :], ALU.add).then_inc(logits_kept, 1)
            dve.wait_ge(logits_kept, 1)
            nc.vector.max(f.top[:, :], f.logits[:, :]).then_inc(top_done, 1)
            dve.wait_ge(top_done, 1)
            nc.vector.max_index(f.idx[:, :], f.top[:, :], f.logits[:, :]).then_inc(idx_done, 1)
            for b in range(B):
                for mo in range(DC):
                    dve.wait_ge(down_done, DC * b + mo + 1)
                    if b >= 1 and mo == 0:
                        dve.wait_ge(out_done, 2 * b)
                    nc.vector.tensor_scalar(f.rT[:, mo, :], sb.ps[:, 4 + mo, :], f.b2[:, b % 2, mo:mo + 1], None,
                                            ALU.add).then_inc(down_kept, 1)
                for v in range(2):
                    t = QT * b + 2 * v
                    dve.wait_ge(out_done, 2 * b + v + 1)
                    dve.wait_ge(hid_added, 2 * (2 * b + v + 1))
                    xs = sb.x[:, t:t + 2, :].rearrange("p a d -> p (a d)")
                    nc.vector.scalar_tensor_tensor(xs, sb.ps[:, 6 + v, :], f.gate03, xs,
                                                   ALU.mult, ALU.add).then_inc(added, 1)

        @block.gpsimd
        def _(pool):
            for v in range(TT // 2):
                xs, hs = sb.x[:, 2 * v:2 * v + 2, :], f.gh[:, v % 2, :, :]
                nc.gpsimd.tensor_tensor(xs, xs, f.bo[:, :].unsqueeze(1).to_broadcast([P, 2, D]),
                                        ALU.add).then_inc(hid_added, 1)
                if v >= 2:
                    pool.wait_ge(hid_added, 2 * (v - 1))
                nc.gpsimd.tensor_scalar(hs, sb.tok[:, 2 * v:2 * v + 2, :], f.gate, None, ALU.mult).then_inc(f.scaled, 1)
                pool.wait_ge(f.scaled, v + 1)
                pool.wait_ge(hid_added, 2 * v + 1)
                nc.gpsimd.tensor_tensor(xs, xs, hs, ALU.add).then_inc(hid_added, 1)

        @block.sync
        def _(sp):
            sp.wait_ge(idx_done, 1)
            for b in range(B):
                e = sp.value_load(f.idx[b:b + 1, 0:1], min_val=0, max_val=E0 - 1)
                if b >= 2:
                    sp.wait_ge(down_done, DC * (b - 1))
                    sp.wait_ge(down_kept, DC * (b - 1))
                s = loaded[b % 2]
                sp.dma_start(f.w1[:, b % 2, :, :], args["L0_ffn_W1"][bass.ds(e, 1), :, :].rearrange(
                    "e (c p) f -> (e p) c f", p=P)).then_inc(s, 16)
                sp.dma_start(f.w2[:, b % 2, :, :], args["L0_ffn_W2"][bass.ds(e, 1), :, :].rearrange(
                    "e (c p) f -> (e p) c f", p=P)).then_inc(s, 16)
                sp.dma_start(f.b1[:, b % 2, :], args["L0_ffn_b1"][bass.ds(e, 1), :, :].rearrange(
                    "e p c -> (e p) c")).then_inc(s, 16)
                sp.dma_start(f.b2[:, b % 2, :], args["L0_ffn_b2"][bass.ds(e, 1), :, :].rearrange(
                    "e p c -> (e p) c")).then_inc(s, 16)


def mixture_phase(nc, sem, sb, m, args, scr, zeroed, out):
    E, IC, ST = E1, chunks(I1), SLOT_TILES
    UP = B * len(IC)
    logits_done, logits_kept, exp_done = sem("logits_done"), sem("logits_kept"), sem("scores_exp")
    shared_gate, hot_ready, ranks_done = sem("shared_gate"), sem("hot_ready"), sem("ranks_done")
    slots_ready, scattered = sem("slots_ready"), sem("scattered")
    chain = sem("route_chain")
    half_loaded = [sem(f"half_loaded{i}") for i in range(2)]
    experts_loaded = sem("experts_loaded")
    s_up, s_silu, s_prod = sem("shared_up"), sem("shared_silu"), sem("shared_prod")
    s_down, x_added = sem("shared_down"), sem("x_added")
    padded = sem("padded")
    xg_loaded = [sem(f"xg_loaded{i}") for i in range(4)]
    x_turned = sem("x_turned")
    xT_kept = sem("xT_kept")
    up_done = sem("up_done")
    silu_done = sem("silu_done")
    prod_done = sem("prod_done")
    h_turned = sem("h_turned")
    hT_kept = sem("hT_kept")
    down_done = sem("down_done")
    y_kept = sem("y_kept")
    y_stored = [sem(f"y_stored{i}") for i in range(4)]
    y_gathered = [sem(f"y_gathered{i}") for i in range(4)]
    y_added = sem("y_added")
    out_done = sem("out_done")

    def shared_tile(half, b, i):
        return half * UP + b * len(IC) + i

    def tiles(eng, body):
        body(0, True, False)
        with eng.Fori(1, ST // 4 - 1) as it:
            body(it, False, False)
        body(ST // 4 - 1, False, True)

    with nc.Block() as block:
        @block.sync
        def _(sp):
            for u in range(4):
                sp.nop().then_inc(y_stored[u], 16)
            for half in range(2):
                sp.dma_start(m.sgu[:, half, :, :], args["gate_up"][E + half].rearrange("(c p) f -> p c f", p=P)
                             ).then_inc(half_loaded[half], 16)
                for i, (a, n) in enumerate(IC):
                    sp.dma_start(m.sdn[0:n, half, i, :], args["down"][E + half, a:a + n, :]
                                 ).then_inc(half_loaded[half], 16)
            for e in range(E):
                sp.dma_start(m.gu[:, e, :, :], args["gate_up"][e].rearrange("(c p) f -> p c f", p=P)
                             ).then_inc(experts_loaded, 16)
            for i, (a, n) in enumerate(IC):
                sp.dma_start(m.dn[0:n, :, i, :], args["down"][0:E, a:a + n, :].rearrange("e p f -> p e f")
                             ).then_inc(experts_loaded, 16)
            sp.wait_ge(scattered, 16 * 2 * TT)

            def slot_tile(buf, it, u):
                return buf.rearrange("(i u p) d -> i u p d", u=4, p=P)[
                    bass.ds(it, 1), u, :, :].rearrange("i p d -> (i p) d")

            def store(it, u):
                sp.wait_ge(y_kept, it * 4 + (u + 1 + 2))
                sp.dma_start(slot_tile(scr.ys, it, u), m.y[:, u, :]).then_inc(y_stored[u], 16)

            def body(it, first, last):
                for u in range(4):
                    sp.wait_ge(x_turned, it * 4 + (u + 1))
                    sp.dma_start(m.xg[:, u, :], slot_tile(scr.xs, it, u)).then_inc(xg_loaded[u], 16)
                    if not first:
                        store(it - 1, u)
                for u in range(4 if last else 0):
                    store(it, u)
            tiles(sp, body)
            for b in range(B):
                sp.wait_ge(y_added, 2 * QT * (b + 1))
                sp.dma_start(out[b].rearrange("(t p) d -> p t d", p=P), sb.x[:, b * QT:(b + 1) * QT, :]
                             ).then_inc(out_done, 16)
            sp.wait_ge(out_done, 16 * B)

        @block.gpsimd
        def _(pool):
            nc.gpsimd.memset(m.tri[:, 0, :], 1.0).then_inc(padded, 1)
            pool.wait_ge(padded, 1)
            nc.gpsimd.memset(m.tri[:, 1, :], 1.0).then_inc(padded, 1)
            pool.wait_ge(padded, 2)
            nc.gpsimd.affine_select(out=m.tri[:, 0, :], in_=m.tri[:, 0, :], compare_op=ALU.is_gt, fill=0.0,
                                    base=0, pattern=[[1, P]], channel_multiplier=-1).then_inc(padded, 1)
            pool.wait_ge(padded, 3)
            nc.gpsimd.iota(m.count_i[:, :], pattern=[[1, ST]], base=0, channel_multiplier=0).then_inc(padded, 1)
            pool.wait_ge(padded, 4)
            nc.gpsimd.tensor_copy(m.count[:, :], m.count_i[:, :]).then_inc(padded, 1)
            pool.wait_ge(padded, 5)
            nc.gpsimd.memset(m.hs[:, :, I1:len(IC) * P], 0.0).then_inc(padded, 1)
            pool.nop().then_inc(x_turned, 4)
            pool.wait_ge(zeroed, 16)
            pool.wait_ge(slots_ready, 1)
            for t in range(TT):
                for c in range(2):
                    pool.indirect_dma_start(
                        out=scr.xs, out_offset=bass.IndirectOffsetOnAxis(ap=m.slot[:, c, t:t + 1], axis=0),
                        in_=sb.tok[:, t, :], in_offset=None).then_inc(scattered, 16)
            for u in range(4):
                pool.wait_ge(y_stored[u], 16 * (ST // 4 + 1))
            for t in range(TT):
                for c in range(2):
                    n = 2 * t + c
                    if n >= 4:
                        pool.wait_ge(y_added, n - 3)
                    pool.indirect_dma_start(
                        out=m.yg[:, n % 4, :], out_offset=None, in_=scr.ys,
                        in_offset=bass.IndirectOffsetOnAxis(ap=m.slot[:, c, t:t + 1], axis=0)
                    ).then_inc(y_gathered[n % 4], 16)

        @block.tensor
        def _(pe):
            pe.nop().then_inc(up_done, 2)
            pe.nop().then_inc(h_turned, 2)
            pe.nop().then_inc(down_done, 2)

            def shared_up(half, b):
                for i, (a, n) in enumerate(IC):
                    k = shared_tile(half, b, i)
                    if k >= 2:
                        pe.wait_ge(s_prod, k - 1)
                    for g in range(2):
                        for c in range(DC):
                            last = nc.tensor.matmul(sb.ps[0:n, 2 * (k % 2) + g, :],
                                                    m.sgu[:, half, c, g * I1 + a:g * I1 + a + n],
                                                    sb.xT[:, c, b * S:(b + 1) * S], start=(c == 0), stop=(c == DC - 1))
                    last.then_inc(s_up, 1)

            def shared_down(half, b):
                pe.wait_ge(s_prod, half * UP + (b + 1) * len(IC))
                for q in range(QT):
                    d = half * TT + b * QT + q
                    if d >= 2:
                        pe.wait_ge(x_added, d - 1)
                    for i, (a, n) in enumerate(IC):
                        last = nc.tensor.matmul(sb.ps[:, 4 + q % 2, 0:D], m.h[0:n, b % 2, i, q * P:(q + 1) * P],
                                                m.sdn[0:n, half, i, :], start=(i == 0), stop=(i == len(IC) - 1))
                    last.then_inc(s_down, 1)

            for t in range(TT):
                for c in range(DC):
                    last = nc.tensor.matmul(sb.ps[:, 7, t * 16:t * 16 + E + 1], sb.xT[:, c, t * P:(t + 1) * P],
                                            m.gw[:, c, :], start=(c == 0), stop=(c == DC - 1))
            last.then_inc(logits_done, 1)
            pe.wait_ge(half_loaded[0], 16 * (1 + len(IC)))
            shared_up(0, 0)
            shared_up(0, 1)
            shared_down(0, 0)
            pe.wait_ge(hot_ready, 1)
            pe.wait_ge(padded, 3)
            hot = m.hot[:, 2, :, :].rearrange("p t e -> p (t e)")
            nc.tensor.matmul(sb.ps[:, 6, 0:TT * E], m.tri[:, 0, :], hot, start=True, stop=True)
            nc.tensor.matmul(sb.ps[:, 7, 0:TT * E], m.tri[:, 1, :], hot, start=True, stop=True).then_inc(ranks_done, 1)
            for b in range(2, B):
                shared_up(0, b)
                shared_down(0, b - 1)
            shared_down(0, B - 1)

            def turn_x(it, u):
                pe.wait_ge(xg_loaded[u % 4], (it + (u // 4 + 1)) * 16)
                pe.wait_ge(xT_kept, it * 4 + (u + 1))
                for c in range(DC):
                    last = nc.tensor.transpose(sb.ps[:, 4, c * P:(c + 1) * P], m.xg[:, u % 4, c * P:(c + 1) * P],
                                               sb.ident[:, :])
                last.then_inc(x_turned, 1)

            def up(it, u, e):
                pe.wait_ge(xT_kept, it * 4 + (u + 2))
                pe.wait_ge(prod_done, it * 4 + (u + 1))
                for g in range(2):
                    for c in range(DC):
                        last = nc.tensor.matmul(
                            sb.ps[:, 2 * (u % 2) + g, 0:I1], m.xgT[:, u % 2, c, :],
                            m.gu[:, bass.ds(e, 1), c, g * I1:(g + 1) * I1].rearrange("p e f -> p (e f)"),
                            start=(c == 0), stop=(c == DC - 1))
                last.then_inc(up_done, 1)

            def turn_h(it, u):
                pe.wait_ge(prod_done, it * 4 + (u + 3))
                pe.wait_ge(hT_kept, it * 4 + (u + 1))
                for i in range(len(IC)):
                    last = nc.tensor.transpose(sb.ps[:, 5, i * P:(i + 1) * P], m.hs[:, u % 2, i * P:(i + 1) * P],
                                               sb.ident[:, :])
                last.then_inc(h_turned, 1)

            def down(it, u, e):
                pe.wait_ge(hT_kept, it * 4 + (u + 2))
                pe.wait_ge(y_kept, it * 4 + (u + 1))
                for i, (a, n) in enumerate(IC):
                    last = nc.tensor.matmul(sb.ps[:, 6 + u % 2, 0:D], m.hT[0:n, u % 2, i, :],
                                            m.dn[0:n, bass.ds(e, 1), i, :].rearrange("p e f -> p (e f)"),
                                            start=(i == 0), stop=(i == len(IC) - 1))
                last.then_inc(down_done, 1)

            def expert_of(it, u):
                col = m.tile_expert[0:1, :].rearrange("p (i u) -> p i u", u=4)[:, bass.ds(it, 1), u]
                return pe.value_load(col, min_val=0, max_val=E - 1)

            pe.wait_ge(experts_loaded, 16 * (E + len(IC)))
            pe.wait_ge(slots_ready, 1)
            pe.wait_ge(padded, 6)
            pe.wait_ge(s_prod, UP)
            pe.wait_ge(x_added, TT)
            turn_x(0, 0)

            def body(it, first, last):
                for u in range(4):
                    if not (first and u == 0):
                        turn_h(it, u - 1)
                    up(it, u, expert_of(it, u))
                    if not (last and u == 3):
                        turn_x(it, u + 1)
                    if not (first and u == 0):
                        before = (it, u - 1) if u else (it - 1, 3)
                        down(it, u - 1, expert_of(*before))
                if last:
                    turn_h(it, 3)
                    down(it, 3, expert_of(it, 3))
            tiles(pe, body)

            pe.wait_ge(prod_done, ST + 2)
            pe.wait_ge(hT_kept, ST + 1)
            pe.wait_ge(half_loaded[1], 16 * (1 + len(IC)))
            shared_up(1, 0)
            for b in range(1, B):
                shared_up(1, b)
                shared_down(1, b - 1)
            shared_down(1, B - 1)

        @block.scalar
        def _(act):
            act.nop().then_inc(xT_kept, 1)
            act.nop().then_inc(hT_kept, 1)
            act.wait_ge(chain, 1)
            nc.scalar.activation(m.e[:, :, :], m.e[:, :, :], ACT.Exp).then_inc(exp_done, 1)
            nc.scalar.activation(m.sw[:, :], m.lg[:, :, E], ACT.Sigmoid).then_inc(shared_gate, 1)

            def shared_silu(half):
                for b in range(B):
                    for i, (a, n) in enumerate(IC):
                        k = shared_tile(half, b, i)
                        act.wait_ge(s_up, k + 1)
                        if k >= 2:
                            act.wait_ge(s_prod, k - 1)
                        nc.scalar.activation(m.g[0:n, k % 2, :], sb.ps[0:n, 2 * (k % 2), :],
                                             ACT.Silu).then_inc(s_silu, 1)

            def keep_x(it, u):
                act.wait_ge(x_turned, it * 4 + (u + 1 + 4))
                act.wait_ge(up_done, it * 4 + (u + 1))
                nc.scalar.activation(m.xgT[:, u % 2, :, :].rearrange("p c s -> p (c s)"), sb.ps[:, 4, 0:D],
                                     ACT.Copy).then_inc(xT_kept, 1)

            def silu(it, u):
                act.wait_ge(up_done, it * 4 + (u + 1 + 2))
                nc.scalar.activation(m.gs[:, u % 2, :], sb.ps[:, 2 * (u % 2), 0:I1], ACT.Silu).then_inc(silu_done, 1)

            def keep_h(it, u):
                act.wait_ge(h_turned, it * 4 + (u + 1 + 2))
                act.wait_ge(down_done, it * 4 + (u + 1))
                nc.scalar.activation(m.hT[:, u % 2, :, :].rearrange("p i s -> p (i s)"),
                                     sb.ps[:, 5, 0:len(IC) * P], ACT.Copy).then_inc(hT_kept, 1)

            shared_silu(0)
            keep_x(0, 0)

            def body(it, first, last):
                for u in range(4):
                    if not (first and u == 0):
                        keep_h(it, u - 1)
                    silu(it, u)
                    if not (last and u == 3):
                        keep_x(it, u + 1)
                if last:
                    keep_h(it, 3)
            tiles(act, body)
            shared_silu(1)

        @block.vector
        def _(dve):
            dve.nop().then_inc(prod_done, 2)
            dve.nop().then_inc(y_kept, 2)
            steps, adds = [0], [0]

            def link(ins):
                steps[0] += 1
                ins.then_inc(chain, 1)
                dve.wait_ge(chain, steps[0])

            def by_expert(col):
                return col.to_broadcast([P, TT, E])

            def gating():
                lg = sb.ps[:, 7, 0:TT * 16].rearrange("p (t w) -> p t w", w=16)
                dve.wait_ge(logits_done, 1)
                nc.vector.tensor_copy(m.lg[:, :, :], lg[:, :, 0:E + 1]).then_inc(logits_kept, 1)
                dve.wait_ge(logits_kept, 1)
                for t in range(TT):
                    last = nc.vector.max(m.top[:, t, :], m.lg[:, t, 0:E])
                last.then_inc(logits_kept, 1)
                dve.wait_ge(logits_kept, 2)
                link(nc.vector.tensor_tensor(m.e[:, :, :], m.lg[:, :, 0:E], by_expert(m.top[:, :, 0:1]), ALU.subtract))
                dve.wait_ge(exp_done, 1)
                link(nc.vector.tensor_reduce(m.sum[:, :], m.e[:, :, :], mybir.AxisListType.X, ALU.add))
                link(nc.vector.reciprocal(m.rsum[:, :], m.sum[:, :]))
                link(nc.vector.tensor_tensor(m.e[:, :, :], m.e[:, :, :], by_expert(m.rsum[:, :].unsqueeze(2)), ALU.mult))
                for t in range(TT):
                    last = nc.vector.max(m.top[:, t, :], m.e[:, t, :])
                link(last)
                for t in range(TT):
                    last = nc.vector.max_index(m.idx[:, t, :], m.top[:, t, :], m.e[:, t, :])
                link(last)
                link(nc.vector.tensor_copy(m.idxf[:, :, :], m.idx[:, :, :]))
                iota = m.count[:, 0:E].unsqueeze(1).to_broadcast([P, TT, E])
                dve.wait_ge(padded, 5)
                for c in range(2):
                    link(nc.vector.tensor_tensor(m.hot[:, c, :, :], iota, by_expert(m.idxf[:, :, c:c + 1]), ALU.is_equal))
                nc.vector.tensor_tensor(m.hot[:, 2, :, :], m.hot[:, 0, :, :], m.hot[:, 1, :, :], ALU.add).then_inc(hot_ready, 1)
                for c in range(2):
                    link(nc.vector.tensor_tensor(m.sel[:, :, :], m.hot[:, c, :, :], m.e[:, :, :], ALU.mult))
                    link(nc.vector.tensor_reduce(m.w[:, c, :], m.sel[:, :, :], mybir.AxisListType.X, ALU.add))
                dve.wait_ge(shared_gate, 1)
                link(nc.vector.tensor_copy(m.w[:, 2, :], m.sw[:, :]))
                link(nc.vector.tensor_scalar(m.w[:, :, :], m.w[:, :, :], m.gate, None, ALU.mult))

            def slots():
                dve.wait_ge(ranks_done, 1)
                tile = [P, TT, E]
                before = sb.ps[:, 6, 0:TT * E].rearrange("p (t e) -> p t e", e=E)
                link(nc.vector.tensor_copy(m.total[:, :, :], sb.ps[:, 7, 0:TT * E].rearrange("p (t e) -> p t e", e=E)))
                for e in range(E):
                    last = nc.vector.tensor_tensor_scan(m.upto[:, :, e], m.tri[:, 1, 0:TT], m.total[:, :, e], 0.0,
                                                        ALU.mult, ALU.add)
                link(last)
                link(nc.vector.tensor_scalar(m.edge[:, :], m.count[:, 0:TT], float(P), None, ALU.mult))
                link(nc.vector.tensor_tensor(m.above[:, :, :], m.upto[:, TT - 1, :].unsqueeze(2).to_broadcast([P, E, TT]),
                                             m.edge[:, :].unsqueeze(1).to_broadcast([P, E, TT]), ALU.is_gt))
                link(nc.vector.tensor_reduce(m.tiles[:, :], m.above[:, :, :], mybir.AxisListType.X, ALU.add))
                link(nc.vector.tensor_tensor_scan(m.ends[:, :], m.tri[:, 1, 0:E], m.tiles[:, :], 0.0, ALU.mult, ALU.add))
                link(nc.vector.tensor_tensor(m.starts[:, :], m.ends[:, :], m.tiles[:, :], ALU.subtract))
                link(nc.vector.tensor_scalar(m.starts[:, :], m.starts[:, :], float(P), None, ALU.mult))
                link(nc.vector.tensor_tensor(m.upto[:, :, :], m.upto[:, :, :], m.total[:, :, :], ALU.subtract))
                link(nc.vector.tensor_tensor(m.upto[:, :, :], m.upto[:, :, :], before, ALU.add))
                link(nc.vector.tensor_tensor(m.upto[:, :, :], m.upto[:, :, :],
                                             m.starts[:, :].unsqueeze(1).to_broadcast(tile), ALU.add))
                for c in range(2):
                    link(nc.vector.tensor_tensor(m.sel[:, :, :], m.hot[:, c, :, :], m.upto[:, :, :], ALU.mult))
                    link(nc.vector.tensor_reduce(m.slotf[:, c, :], m.sel[:, :, :], mybir.AxisListType.X, ALU.add))
                link(nc.vector.tensor_copy(m.slot[:, :, :], m.slotf[:, :, :]))
                link(nc.vector.tensor_tensor(m.past[:, :, :], m.count[:, :].unsqueeze(2).to_broadcast([P, ST, E]),
                                             m.ends[:, :].unsqueeze(1).to_broadcast([P, ST, E]), ALU.is_ge))
                link(nc.vector.tensor_reduce(m.tile_f[:, :], m.past[:, :, :], mybir.AxisListType.X, ALU.add))
                link(nc.vector.tensor_scalar(m.tile_f[:, :], m.tile_f[:, :], float(E - 1), None, ALU.min))
                nc.vector.tensor_copy(m.tile_expert[:, :], m.tile_f[:, :]).then_inc(slots_ready, 1)

            def shared_prod(half, b):
                for i, (a, n) in enumerate(IC):
                    k, g = shared_tile(half, b, i), half * B + b
                    dve.wait_ge(s_silu, k + 1)
                    if i == 0 and g >= 2:
                        dve.wait_ge(s_down, QT * (g - 1))
                    nc.vector.tensor_tensor(m.h[0:n, b % 2, i, :], m.g[0:n, k % 2, :],
                                            sb.ps[0:n, 2 * (k % 2) + 1, :], ALU.mult).then_inc(s_prod, 1)

            def shared_add(half, b):
                for q in range(QT):
                    t = b * QT + q
                    dve.wait_ge(s_down, half * TT + t + 1)
                    nc.vector.scalar_tensor_tensor(sb.x[:, t, :], sb.ps[:, 4 + q % 2, 0:D], m.w[:, 2, t:t + 1],
                                                   sb.x[:, t, :], ALU.mult, ALU.add).then_inc(x_added, 1)

            def expert_add(b):
                dve.wait_ge(x_added, TT + (b + 1) * QT)
                for t in range(b * QT, (b + 1) * QT):
                    for c in range(2):
                        n = 2 * t + c
                        if c == 1:
                            dve.wait_ge(y_added, n)
                        dve.wait_ge(y_gathered[n % 4], 16 * (n // 4 + 1))
                        nc.vector.scalar_tensor_tensor(sb.x[:, t, :], m.yg[:, n % 4, :], m.w[:, c, t:t + 1],
                                                       sb.x[:, t, :], ALU.mult, ALU.add).then_inc(y_added, 1)

            gating()
            shared_prod(0, 0)
            shared_prod(0, 1)
            shared_add(0, 0)
            slots()
            for b in range(2, B):
                shared_prod(0, b)
                shared_add(0, b - 1)
            shared_add(0, B - 1)

            def prod(it, u):
                dve.wait_ge(silu_done, it * 4 + (u + 1))
                dve.wait_ge(h_turned, it * 4 + (u + 1))
                nc.vector.tensor_tensor(m.hs[:, u % 2, 0:I1], m.gs[:, u % 2, :], sb.ps[:, 2 * (u % 2) + 1, 0:I1],
                                        ALU.mult).then_inc(prod_done, 1)

            def keep_y(it, u):
                dve.wait_ge(down_done, it * 4 + (u + 1 + 2))
                dve.wait_ge(y_stored[u], (it + 1) * 16)
                nc.vector.tensor_copy(m.y[:, u, :], sb.ps[:, 6 + u % 2, 0:D]).then_inc(y_kept, 1)

            def body(it, first, last):
                for u in range(4):
                    prod(it, u)
                    if u:
                        keep_y(it, u - 1)
                    elif not first:
                        keep_y(it - 1, 3)
                if last:
                    keep_y(it, 3)
            tiles(dve, body)
            shared_prod(1, 0)
            for b in range(1, B):
                shared_prod(1, b)
                shared_add(1, b - 1)
                expert_add(b - 1)
            shared_add(1, B - 1)
            expert_add(B - 1)


class Names:
    pass


def build(nc, a, out):
    ctx = ExitStack()
    with ctx:
        names = [0]
        layer_sems, used = [ctx.enter_context(ExitStack())], []

        def sem(name):
            used.append(layer_sems[0].enter_context(nc.semaphore(name)))
            return used[-1]

        def buffers(stack):
            def made(name, shape, dt):
                names[0] += 1
                return stack.enter_context(nc.sbuf_tensor(f"{name}_{names[0]}", shape, dt))
            return made

        def dram(name, shape, dt):
            return nc.dram_tensor(name, shape, dt, kind="Internal").ap()

        sb, buf = Names(), buffers(ctx)
        sb.x = buf("x", [P, TT, D], F32)
        sb.tok = buf("tok", [P, TT, D], F32)
        sb.xT = buf("xT", [P, DC, N], F32)
        sb.ident = buf("ident", [P, P], F32)
        sb.stats = buf("stats", [P, TT, 6], F32)
        sb.mv = buf("mv", [P, TT, 2], F32)
        sb.std = buf("std", [P, TT], F32)
        sb.rstd = buf("rstd", [P, TT], F32)
        sb.gates = buf("gates", [P, 4], F32)
        sb.rawg = buf("rawg", [P, 4], F32)
        sb.gate03 = buf("gate03", [P, 1], F32)
        sb.zeros = buf("zeros", [P, D], F32)
        sb.ps = ctx.enter_context(nc.psum_tensor("ps", [P, 8, 512], F32))
        x_loaded = [sem(f"x_loaded{i}") for i in range(4)]
        scratch = Names()
        scratch.keymask = dram("keymask_scratch", [B, S], BF16)
        scratch.xs = dram("slots_in", [SLOT_TILES * P, D], F32)
        scratch.ys = dram("slots_out", [SLOT_TILES * P, D], F32)
        scratch.qk = [dram(f"qk_scratch{i}", [2, 3, D, N], BF16) for i in range(2)]

        for layer in range(2):
            L = f"L{layer}_"
            with ExitStack() as mem:
                aw, buf = Names(), buffers(mem)
                aw.o = buf("o", [P, DC, D], F32)
                aw.bo = buf("bo", [P, D], F32)
                sb.v = buf("v", [P, TT, D], F32)
                with ExitStack() as pm:
                    t, buf = Names(), buffers(pm)
                    aw.qk = buf("qk", [P, 2, DC, D], F32)
                    aw.v = buf("v", [P, DC, D], F32)
                    aw.bqk = buf("bqk", [P, 2, DC], F32)
                    aw.bv = buf("bv", [P, D], F32)
                    t.cT = buf("cT", [P, DC, N], F32)
                    t.plain = buf("plain", [P, 2, S], F32)
                    t.rest = buf("rest", [P, 2, S], F32)
                    t.parts = buf("parts", [P, 2, 3, S], BF16)
                    t.m8 = buf("m8", [B, S // 4], U32)
                    t.mf = buf("mf", [B, S], BF16)
                    sb.cT, sb.plain, sb.rest, sb.parts = t.cT, t.plain, t.rest, t.parts
                    loads_phase(nc, sem, sb, aw, a, layer, x_loaded, scratch, t)
                    layernorm_phase(nc, sem, sb, x_loaded if layer == 0 else None, f"n{layer}_")
                    s2 = Names()
                    s2.qk = scratch.qk[layer]
                    projection_phase(nc, sem, sb, aw, s2, f"p{layer}_")
                with ExitStack() as am:
                    t, buf = Names(), buffers(am)
                    t.bias = buf("bias", [P, HG if layer == 0 else 1, QT, S], F32)
                    t.qs = buf("qs", [P, 2, HG, S], BF16)
                    t.ks = buf("ks", [P, 2, HG, S], BF16)
                    t.s = buf("s", [P, QT, S], F32)
                    p01 = buf("p", [P, 2, QT, S], F32)
                    t.p = [p01[:, i, :, :] for i in range(2)] + [
                        sb.xT[:, i, :].rearrange("p (t k) -> p t k", t=QT) for i in range(2)]
                    t.pT = buf("pT", [P, HG + 2, QT, S], F32)
                    t.vq = buf("vq", [P, 2, QT, HG, VW], F32)
                    t.oT = buf("oT", [P, S], F32)
                    t.nmax = buf("nmax", [P, 4, QT], F32)
                    t.rsum = buf("rsum", [P, QT, HG], F32)
                    s2.keymask = scratch.keymask
                    attention_setup(nc, sem, sb, t, a, layer, f"s{layer}_")
                    if layer == 1:
                        zeroed, cleared0 = sem("zeroed"), sem("zeros_ready")
                        with nc.Block() as block:
                            @block.gpsimd
                            def _(pool):
                                nc.gpsimd.memset(sb.zeros[:, :], 0.0).then_inc(cleared0, 1)
                                pool.wait_ge(cleared0, 1)
                                pool.dma_start(scratch.xs.rearrange("(r p) d -> p r d", p=P),
                                               sb.zeros[:, :].unsqueeze(1).to_broadcast([P, SLOT_TILES, D])
                                               ).then_inc(zeroed, 16)
                    attention_phase(nc, sem, sb, t, s2, a["bias"] if layer == 0 else None, f"a{layer}_")
                aw.gate = sb.gates[:, layer:layer + 1]
                output_phase(nc, sem, sb, aw, f"o{layer}_")
            with ExitStack() as fm:
                if layer == 0:
                    f, buf = Names(), buffers(fm)
                    f.wp1 = buf("wp1", [P, DC, NAV], F32)
                    f.wp2 = buf("wp2", [P, E0], F32)
                    f.bp1 = buf("bp1", [P, 1], F32)
                    f.bp2 = buf("bp2", [B, E0], F32)
                    f.wo = buf("wo", [P, DC, D], F32)
                    f.bo = buf("bo", [P, D], F32)
                    f.r1 = buf("r1", [P, B], F32)
                    f.logits = buf("logits", [B, E0], F32)
                    f.top = buf("top", [B, E0], F32)
                    f.idx = buf("idx", [B, E0], U32)
                    f.w1 = buf("w1", [P, 2, DC, F0], F32)
                    f.w2 = buf("w2", [P, 2, F0 // P, D], F32)
                    f.b1 = buf("b1", [P, 2, F0 // P], F32)
                    f.b2 = buf("b2", [P, 2, DC], F32)
                    f.h = buf("h", [P, 2, F0 // P, S], F32)
                    f.rT = buf("rT", [P, DC, S], F32)
                    f.gh = buf("gh", [P, 2, 2, D], F32)
                    f.gate, f.gate03, f.scaled = sb.gates[:, 2:3], sb.gate03[:, 0:1], sem("hid_scaled")
                    routed_loads(nc, sem, sb, f, a)
                    layernorm_phase(nc, sem, sb, None, "n2_")
                    routed_ffn_phase(nc, sem, sb, f, a, "f_")
                    with nc.Block() as block:
                        @block.sync
                        def _(sp):
                            for s in used:
                                sp.sem_clear(s)
                    layer_sems[0].close()
                    layer_sems[0] = ctx.enter_context(ExitStack())
                else:
                    m, buf = Names(), buffers(fm)
                    m.gw = buf("gw", [P, DC, E1 + 1], F32)
                    m.lg = buf("lg", [P, TT, E1 + 1], F32)
                    m.top = buf("top", [P, TT, 8], F32)
                    m.e = buf("e", [P, TT, E1], F32)
                    m.sum = buf("sum", [P, TT], F32)
                    m.rsum = buf("rsum", [P, TT], F32)
                    m.idx = buf("idx", [P, TT, 8], U32)
                    m.idxf = buf("idxf", [P, TT, 8], F32)
                    m.hot = buf("hot", [P, 3, TT, E1], F32)
                    m.sel = buf("sel", [P, TT, E1], F32)
                    m.w = buf("w", [P, 3, TT], F32)
                    m.sw = buf("sw", [P, TT], F32)
                    m.tri = buf("tri", [P, 2, P], F32)
                    m.count_i = buf("count_i", [P, SLOT_TILES], I32)
                    m.count = buf("count", [P, SLOT_TILES], F32)
                    m.total = buf("total", [P, TT, E1], F32)
                    m.upto = buf("upto", [P, TT, E1], F32)
                    m.edge = buf("edge", [P, TT], F32)
                    m.above = buf("above", [P, E1, TT], F32)
                    m.tiles = buf("tiles", [P, E1], F32)
                    m.ends = buf("ends", [P, E1], F32)
                    m.starts = buf("starts", [P, E1], F32)
                    m.slotf = buf("slotf", [P, 2, TT], F32)
                    m.slot = buf("slot", [P, 2, TT], U32)
                    m.past = buf("past", [P, SLOT_TILES, E1], F32)
                    m.tile_f = buf("tile_f", [P, SLOT_TILES], F32)
                    m.tile_expert = buf("tile_expert", [P, SLOT_TILES], I32)
                    m.sgu = buf("sgu", [P, 2, DC, 2 * I1], F32)
                    m.sdn = buf("sdn", [P, 2, 3, D], F32)
                    m.gu = buf("gu", [P, E1, DC, 2 * I1], F32)
                    m.dn = buf("dn", [P, E1, 3, D], F32)
                    m.g = buf("g", [P, 2, S], F32)
                    m.h = buf("h", [P, 2, 3, S], F32)
                    m.xg = buf("xg", [P, 4, D], F32)
                    m.xgT = buf("xgT", [P, 2, DC, P], F32)
                    m.gs = buf("gs", [P, 2, I1], F32)
                    m.hs = buf("hs", [P, 2, 3 * P], F32)
                    m.hT = buf("hT", [P, 2, 3, P], F32)
                    m.y = buf("y", [P, 4, D], F32)
                    m.yg = buf("yg", [P, 4, D], F32)
                    m.gate = sb.gates[:, 3:4]
                    gw_loaded = sem("gw_loaded")
                    with nc.Block() as block:
                        @block.sync
                        def _(sp):
                            sp.dma_start(m.gw[:, :, :], a["gate_w"].rearrange("(c p) e -> p c e", p=P)).then_inc(gw_loaded, 16)
                            sp.wait_ge(gw_loaded, 16)
                    layernorm_phase(nc, sem, sb, None, "n3_")
                    mixture_phase(nc, sem, sb, m, a, scratch, zeroed, out)


def loads_phase(nc, sem, sb, w, a, layer, x_loaded, scratch, t):
    L = f"L{layer}_xattn_"
    loaded, ready, ready2 = sem(L + "loaded"), sem(L + "ready"), sem(L + "ready2")
    mask_kept, mask_stored = sem(L + "mask_kept"), sem(L + "mask_stored")
    consts = sem(L + "consts")
    with nc.Block() as block:
        @block.sync
        def _(sp):
            n = 0
            if layer == 0:
                sp.dma_start(sb.rawg[:, 0:2], a["g_xattn"].partition_broadcast(P)).then_inc(loaded, 16)
                sp.dma_start(sb.rawg[:, 2:4], a["g_ffn"].partition_broadcast(P)).then_inc(loaded, 16)
                sp.dma_start(t.m8[:, :], a["keymask"]).then_inc(loaded, 16)
                n += 3
                for g in range(4):
                    sp.dma_start(sb.x[:, 4 * g:4 * g + 4, :], a["x"].rearrange("b (t p) d -> p (b t) d", p=P)[:, 4 * g:4 * g + 4, :]
                                 ).then_inc(x_loaded[g], 16)
            for dst, src in ((w.qk[:, 0, :, :], a[L + "Wq"]), (w.qk[:, 1, :, :], a[L + "Wk"]),
                             (w.v[:, :, :], a[L + "Wv"]), (w.o[:, :, :], a[L + "Wo"])):
                sp.dma_start(dst, src.rearrange("(c p) n -> p c n", p=P)).then_inc(loaded, 16)
            sp.dma_start(w.bqk[:, 0, :], a[L + "bq"]).then_inc(loaded, 16)
            sp.dma_start(w.bqk[:, 1, :], a[L + "bk"]).then_inc(loaded, 16)
            sp.dma_start(w.bv[:, :], a[L + "bv"].partition_broadcast(P)).then_inc(loaded, 16)
            sp.dma_start(w.bo[:, :], a[L + "bo"].partition_broadcast(P)).then_inc(loaded, 16)
            sp.dma_start(sb.cT[:, :, :], a["ctxT"].rearrange("(c p) n -> p c n", p=P)).then_inc(loaded, 16)
            n += 9
            sp.wait_ge(loaded, 16 * n)
            sp.nop().then_inc(ready, 1)
            if layer == 0:
                sp.wait_ge(mask_kept, 1)
                sp.dma_start(scratch.keymask, t.mf[:, :]).then_inc(mask_stored, 16)
                sp.wait_ge(mask_stored, 16)

        @block.vector
        def _(dve):
            dve.wait_ge(ready, 1)
            nc.vector.tensor_scalar(w.bqk[:, 0, :], w.bqk[:, 0, :], SCALE, None, ALU.mult)
            if layer == 0:
                nc.vector.tensor_scalar(t.mf[:, :], t.m8[:, :].bitcast(U8), 1.0, -NEG, ALU.subtract, ALU.mult).then_inc(mask_kept, 1)
                dve.wait_ge(ready2, 1)
                nc.vector.tensor_scalar(sb.gate03[:, :], sb.gates[:, 2:3], 0.3, None, ALU.mult)
            else:
                dve.wait_ge(ready, 1)
            if layer == 0:
                nc.vector.tensor_scalar(w.bo[:, :], w.bo[:, :], sb.gates[:, 0:1], None, ALU.mult)
            else:
                nc.vector.tensor_scalar(w.bo[:, :], w.bo[:, :], sb.gates[:, 1:2], None, ALU.mult)

        @block.scalar
        def _(act):
            if layer == 0:
                act.wait_ge(ready, 1)
                nc.scalar.activation(sb.gates[:, :], sb.rawg[:, :], ACT.Tanh).then_inc(ready2, 1)

        @block.gpsimd
        def _(pool):
            if layer == 0:
                nc.gpsimd.memset(sb.ident[:, :], 0.0).then_inc(consts, 1)
                pool.wait_ge(consts, 1)
                nc.gpsimd.affine_select(out=sb.ident[:, :], in_=sb.ident[:, :], compare_op=ALU.not_equal, fill=1.0,
                                        base=0, pattern=[[-1, P]], channel_multiplier=1).then_inc(consts, 1)


def attention_setup(nc, sem, sb, at, a, layer, tag):
    loaded, cleared, onesrow = sem(tag + "loaded"), sem(tag + "cleared"), sem(tag + "onesrow")
    with nc.Block() as block:
        @block.gpsimd
        def _(pool):
            nc.gpsimd.memset(at.vq[:, :, :, :, :], 0.0).then_inc(cleared, 1)
            pool.wait_ge(cleared, 1)
            nc.gpsimd.memset(at.vq[:, :, :, :, DH:DH + 1], 1.0).then_inc(cleared, 1)
            if layer == 0:
                pool.wait_ge(cleared, 2)
                nc.gpsimd.memset(at.qs[KS:KS + 1, :, :, :], 1.0)

        if layer == 1:
            @block.sync
            def _(sp):
                sp.dma_start(at.bias[:, 0, :, :], a["mask"].rearrange("(t p) k -> p t k", p=P)).then_inc(loaded, 16)

            @block.vector
            def _(dve):
                dve.wait_ge(loaded, 16)
                nc.vector.tensor_scalar(at.bias[:, 0, :, :], at.bias[:, 0, :, :], MASK_C, None, ALU.mult)


def routed_loads(nc, sem, sb, f, a):
    loaded, ready = sem("rl_loaded"), sem("rl_ready")
    with nc.Block() as block:
        @block.sync
        def _(sp):
            sp.dma_start(f.wp1[:, :, :], a["L0_ffn_Wp1"].rearrange("(c p) n -> p c n", p=P)).then_inc(loaded, 16)
            sp.dma_start(f.wp2[:, :], a["L0_ffn_Wp2"]).then_inc(loaded, 16)
            sp.dma_start(f.bp1[:, :], a["L0_ffn_bp1"].rearrange("(p a) -> p a", a=1)).then_inc(loaded, 16)
            sp.dma_start(f.bp2[:, :], a["L0_ffn_bp2"].partition_broadcast(B)).then_inc(loaded, 16)
            sp.dma_start(f.wo[:, :, :], a["L0_ffn_Wo"].rearrange("(c p) n -> p c n", p=P)).then_inc(loaded, 16)
            sp.dma_start(f.bo[:, :], a["L0_ffn_bo"].partition_broadcast(P)).then_inc(loaded, 16)
            sp.wait_ge(loaded, 96)
            sp.nop().then_inc(ready, 1)

        @block.vector
        def _(dve):
            dve.wait_ge(ready, 1)
            nc.vector.tensor_scalar(f.bo[:, :], f.bo[:, :], sb.gate03[:, 0:1], None, ALU.mult)


def kernel(**inputs):
    import numpy as _np
    import concourse.bacc as _bacc
    from concourse import mybir as _mybir
    from concourse.bass_utils import run_bass_kernel_spmd as _run

    i = {k: _np.asarray(v) for k, v in inputs.items()}
    gate, up = i["L1_ffn_shared_gate_w"], i["L1_ffn_shared_up_w"]
    down = i["L1_ffn_shared_down_w"]
    gate_up = _np.concatenate([i["L1_ffn_experts_gate_up"]] + [
        _np.concatenate([gate[h * I1:(h + 1) * I1], up[h * I1:(h + 1) * I1]], 0)[None] for h in range(2)], 0)
    downs = _np.concatenate([i["L1_ffn_experts_down"]] + [down[None, :, h * I1:(h + 1) * I1] for h in range(2)], 0)
    laid = {
        "x": i["x"],
        "ctxT": i["ctx_1024"].reshape(N, D).T,
        "keymask": i["mask_BxS2_bk1"].view(_np.uint32),
        "mask": i["mask_SxS2_fk1"],
        "bias": i["L0_xattn_relative_bias"][0],
        "g_xattn": i["g_xattn"], "g_ffn": i["g_ffn"],
        "gate_w": _np.concatenate([i["L1_ffn_gate_w"], i["L1_ffn_shared_expert_gate_w"]], 0).T,
        "gate_up": gate_up.transpose(0, 2, 1),
        "down": downs.transpose(0, 2, 1),
    }
    for n in "qkvo":
        laid[f"L0_xattn_W{n}"] = i[f"L0_xattn_W{n}"].T
        laid[f"L1_xattn_W{n}"] = i[f"L1_xattn_W{n}"]
        for l in range(2):
            laid[f"L{l}_xattn_b{n}"] = i[f"L{l}_xattn_b{n}"]
    for n in ("Wp1", "bp1", "Wp2", "bp2", "W1", "b1", "W2", "b2", "Wo", "bo"):
        laid[f"L0_ffn_{n}"] = i[f"L0_ffn_{n}"]

    for n in ("L0_xattn_bq", "L0_xattn_bk", "L1_xattn_bq", "L1_xattn_bk", "L0_ffn_b1", "L0_ffn_b2"):
        v = laid[n]
        laid[n] = _np.swapaxes(v.reshape(*v.shape[:-1], -1, P), -1, -2)

    nc = _bacc.Bacc("TRN2", target_bir_lowering=False, num_devices=1)
    arrays, args = {}, {}
    for name, v in laid.items():
        v = _np.ascontiguousarray(v)
        arrays[f"in_{name}"] = v
        args[name] = nc.dram_tensor(f"in_{name}", v.shape, _mybir.dt.from_np(v.dtype), kind="ExternalInput").ap()
    out = nc.dram_tensor("out_0", (B, S, D), F32, kind="ExternalOutput").ap()
    build(nc, args, out)
    r = _run(nc, [arrays], core_ids=[0])
    return r.results[0]["out_0"]
```

```python
from contextlib import ExitStack

import concourse.bass as bass
from concourse import mybir

ALU = mybir.AluOpType
ACT = mybir.ActivationFunctionType
F32 = mybir.dt.float32
BF16 = mybir.dt.bfloat16
U32 = mybir.dt.uint32
U8 = mybir.dt.uint8
I32 = mybir.dt.int32

P = 128
B, S, D = 4, 512, 256
H, DH = 16, 16
N = B * S
DC = D // P
TT = N // P
QT = S // P
E0, F0, NAV = 8, 512, 128
E1, I1, SI = 8, 352, 704
HG = 4
VW = 32
SCALE = 1.0 / DH ** 0.5
EPS = 1e-5
NEG = -1.0e30
MASK_C = -1000000000.0
Q_PARTS = [0, 1, 2, 0, 1, 0]
K_PARTS = [0, 0, 0, 1, 1, 2]
KS = DH * len(Q_PARTS)
EARLY = 1
SLOT_TILES = -(-(2 * TT + E1 - 1) // 4) * 4
USED_TILES = 2 * TT + E1 - 1
LAST_STEP = USED_TILES - (SLOT_TILES - 4)


def chunks(n):
    return [(a, min(P, n - a)) for a in range(0, n, P)]


def load_context(eng, w, a, layer, ld):
    L = f"L{layer}_xattn_"
    eng.dma_start(w.qk[:, 1, :, :], a[L + "Wk"].rearrange("(c p) n -> p c n", p=P)).then_inc(ld.k, 16)
    eng.dma_start(w.bqk[:, 1, :], a[L + "bk"]).then_inc(ld.k, 16)
    for b in range(B):
        eng.dma_start(w.cT[:, :, b * S:(b + 1) * S],
                      a["ctxT"].rearrange("(c p) n -> p c n", p=P)[:, :, b * S:(b + 1) * S]).then_inc(ld.ctx[b], 16)


def load_rest(eng, sb, w, at, a, layer, ld):
    L = f"L{layer}_xattn_"
    if layer == 0:
        eng.dma_start(w.m8[:, :], a["keymask"]).then_inc(ld.mask, 16)
        eng.dma_start(sb.rawg[:, 0:2], a["g_xattn"].partition_broadcast(P)).then_inc(ld.gates, 16)
        eng.dma_start(sb.rawg[:, 2:4], a["g_ffn"].partition_broadcast(P)).then_inc(ld.gates, 16)
    eng.dma_start(w.bqk[:, 0, :], a[L + "bq"]).then_inc(ld.q, 16)
    eng.dma_start(w.bv[:, :], a[L + "bv"].partition_broadcast(P)).then_inc(ld.v, 16)
    if layer == 0:
        for b in range(B):
            eng.dma_start(sb.x[:, QT * b:QT * (b + 1), :], a["x"][b].rearrange("(t p) d -> p t d", p=P)
                          ).then_inc(ld.x[b], 16)
    eng.dma_start(w.v[:, :, :], a[L + "Wv"].rearrange("(c p) n -> p c n", p=P)).then_inc(ld.v, 16)
    eng.dma_start(w.qk[:, 0, :, :], a[L + "Wq"].rearrange("(c p) n -> p c n", p=P)).then_inc(ld.q, 16)
    eng.dma_start(w.bo[:, :], a[L + "bo"].partition_broadcast(P)).then_inc(ld.o, 16)
    eng.dma_start(w.o[:, :, :], a[L + "Wo"].rearrange("(c p) n -> p c n", p=P)).then_inc(ld.o, 16)
    if layer == 0:
        for j in range(2):
            load_bias(eng, at, a["bias"], 0, j)
    else:
        eng.dma_start(at.bias[:, 0, :, :], a["mask"].rearrange("(t p) k -> p t k", p=P)).then_inc(ld.mask, 16)


def load_bias(eng, at, bias_dram, hg, j):
    src = bias_dram.rearrange("(g j) (t p) k -> g j p t k", j=HG, p=P)
    eng.dma_start(at.bias[:, j, :, :], src[bass.ds(hg, 1), j, :, :, :].rearrange("g p t k -> (g p) t k")
                  ).then_inc(at.bias_loaded[j], 16)


def load_qk(eng, at, dram, per_head_bias, hg, b):
    for s in range(len(Q_PARTS)):
        for which, part, dst in ((0, Q_PARTS[s], at.qs), (1, K_PARTS[s], at.ks)):
            src = dram.qk[which, part, :, b * S:(b + 1) * S].rearrange("(g j d) t -> g d j t", j=HG, d=DH)
            eng.dma_start(dst[s * DH:(s + 1) * DH, b % 2, :, :],
                          src[bass.ds(hg, 1), :, :, :].rearrange("g d j t -> (g d) j t")
                          ).then_inc(at.qk_loaded[b % 2], 16)
    if per_head_bias:
        eng.dma_start(at.ks[KS:KS + 1, b % 2, :, :],
                      dram.keymask[b:b + 1, :].unsqueeze(1).to_broadcast([1, HG, S])
                      ).then_inc(at.qk_loaded[b % 2], 16)


def projection_phase(nc, sem, sb, w, at, a, dram, layer, ld, tag):
    mask_kept, mask_stored = sem(tag + "mask_kept"), sem(tag + "mask_stored")
    consts, gates_ready, bq_scaled = sem(tag + "consts"), sem(tag + "gates_ready"), sem(tag + "bq_scaled")
    stats_done, mv_done, var_ready = sem(tag + "stats_done"), sem(tag + "mv_done"), sem(tag + "var_ready")
    std_ready, rstd_ready = sem(tag + "std_ready"), sem(tag + "rstd_ready")
    norm_done, turned, xT_kept = sem(tag + "norm_done"), sem(tag + "turned"), sem(tag + "xT_kept")
    proj_done, plain_done, head_done = sem(tag + "proj_done"), sem(tag + "plain_done"), sem(tag + "head_done")
    rest_done, mid_done, low_done = sem(tag + "rest_done"), sem(tag + "mid_done"), sem(tag + "low_done")
    stored = [sem(tag + f"stored{i}") for i in range(4)]
    v_done, v_copied = sem(tag + "v_done"), sem(tag + "v_copied")
    NK = DC * B
    NT = 2 * NK
    NV = TT // 2

    def place(n):
        return 1 - n // NK, n % DC, n // DC % B

    with nc.Block() as block:
        @block.sync
        def _(sp):
            if layer == 0:
                load_rest(sp, sb, w, at, a, layer, ld)
                sp.wait_ge(mask_kept, 1)
                sp.dma_start(dram.keymask, w.mf[:, :]).then_inc(mask_stored, 16)
            for n in range(NT):
                which, mo, b = place(n)
                sp.wait_ge(low_done, n + 1)
                sp.dma_start(dram.qk[which, :, mo * P:(mo + 1) * P, b * S:(b + 1) * S].rearrange("s p t -> p s t"),
                             sb.parts[:, n % 4, :, :]).then_inc(stored[n % 4], 16)
            for i in range(4):
                sp.wait_ge(stored[i], 16 * (NT // 4))
            sp.wait_ge(ld.o, 32)

        @block.gpsimd
        def _(pool):
            if layer == 0:
                nc.gpsimd.memset(sb.ident[:, :], 0.0).then_inc(consts, 1)
                pool.wait_ge(consts, 1)
                nc.gpsimd.affine_select(out=sb.ident[:, :], in_=sb.ident[:, :], compare_op=ALU.not_equal, fill=1.0,
                                        base=0, pattern=[[-1, P]], channel_multiplier=1).then_inc(consts, 1)
                pool.wait_ge(consts, 2)
                nc.gpsimd.memset(at.qs[KS:KS + 1, :, :, :], 1.0).then_inc(consts, 1)
                pool.wait_ge(consts, 3)
            else:
                pool.nop().then_inc(consts, 3)
            nc.gpsimd.memset(at.vq[:, :, :, :, :], 0.0).then_inc(consts, 1)
            pool.wait_ge(consts, 4)
            nc.gpsimd.memset(at.vq[:, :, :, :, DH:DH + 1], 1.0).then_inc(consts, 1)
            pool.wait_ge(consts, 5)
            for n in range(NT):
                pool.wait_ge(mid_done, n + 1)
                nc.gpsimd.tensor_tensor(sb.parts[:, n % 4, 2, :], sb.rest[:, n % 4, :], sb.parts[:, n % 4, 1, :],
                                        ALU.subtract).then_inc(low_done, 1)

        @block.tensor
        def _(pe):
            def project_v(v):
                if v == 0:
                    pe.wait_ge(ld.v, 32)
                if v < 4:
                    pe.wait_ge(xT_kept, 3 + v // 2)
                else:
                    pe.wait_ge(v_copied, v - 3)
                for i in range(2):
                    t = 2 * v + i
                    for c in range(DC):
                        last = nc.tensor.matmul(sb.ps[:, 4 + v % 4, i * D:(i + 1) * D],
                                                w.cT[:, c, t * P:(t + 1) * P], w.v[:, c, :],
                                                start=(c == 0), stop=(c == DC - 1))
                last.then_inc(v_done, 1)

            def turn(g):
                if g >= 2:
                    pe.wait_ge(xT_kept, g - 1)
                for c in range(DC):
                    for i in range(QT):
                        t = QT * g + i
                        if c == 0:
                            pe.wait_ge(norm_done, t + 1)
                        last = nc.tensor.transpose(sb.ps[:, 4 + 2 * (g % 2) + c, i * P:(i + 1) * P],
                                                   sb.tok[:, t, c * P:(c + 1) * P], sb.ident[:, :])
                last.then_inc(turned, 1)

            def project(n):
                which, mo, b = place(n)
                if which == 0:
                    pe.wait_ge(xT_kept, b + 1)
                else:
                    pe.wait_ge(ld.ctx[b], 16)
                if n >= 4:
                    pe.wait_ge(plain_done, n - 3)
                src = w.cT if which else sb.xT
                for c in range(DC):
                    last = nc.tensor.matmul(sb.ps[:, n % 4, :], w.qk[:, which, c, mo * P:(mo + 1) * P],
                                            src[:, c, b * S:(b + 1) * S], start=(c == 0), stop=(c == DC - 1))
                last.then_inc(proj_done, 1)

            pe.wait_ge(ld.k, 32)
            for n in range(NK):
                project(n)
            pe.wait_ge(consts, 2)
            for g in range(B):
                turn(g)
            for v in range(NV // 2):
                project_v(v)
            pe.wait_ge(ld.q, 32)
            for n in range(NK, NT):
                project(n)
            for v in range(NV // 2, NV):
                project_v(v)

        @block.scalar
        def _(act):
            if layer == 0:
                load_context(act, w, a, layer, ld)
                act.wait_ge(ld.gates, 32)
                nc.scalar.activation(sb.gates[:, :], sb.rawg[:, :], ACT.Tanh).then_inc(gates_ready, 1)

            def plain(n):
                which, mo, b = place(n)
                act.wait_ge(proj_done, n + 1)
                if n >= 4:
                    act.wait_ge(rest_done, n - 3)
                nc.scalar.activation(sb.plain[:, n % 4, :], sb.ps[:, n % 4, :], ACT.Identity,
                                     bias=w.bqk[:, which, mo:mo + 1],
                                     scale=1.0 if which else SCALE).then_inc(plain_done, 1)

            act.wait_ge(ld.k, 32)
            for n in range(4):
                plain(n)
            act.wait_ge(var_ready, 1)
            nc.scalar.activation(sb.std[:, :], sb.rstd[:, :], ACT.Sqrt).then_inc(std_ready, 1)
            for g in range(B):
                act.wait_ge(turned, g + 1)
                nc.scalar.activation(sb.xT[:, :, g * S:(g + 1) * S],
                                     sb.ps[:, 4 + 2 * (g % 2):6 + 2 * (g % 2), :], ACT.Copy).then_inc(xT_kept, 1)
            for n in range(4, NK):
                plain(n)
            act.wait_ge(bq_scaled, 1)
            for n in range(NK, NT):
                plain(n)
            act.wait_ge(stored[0], 16 * (NK // 4 + 1))
            if layer == 0:
                act.wait_ge(mask_stored, 16)
                act.wait_ge(consts, 3)
            load_qk(act, at, dram, layer == 0, 0, 0)

        @block.vector
        def _(dve):
            def cut_parts(n):
                dve.wait_ge(plain_done, n + 1)
                if n >= 4:
                    dve.wait_ge(stored[n % 4], 16 * (n // 4))
                nc.vector.tensor_copy(sb.parts[:, n % 4, 0, :], sb.plain[:, n % 4, :]).then_inc(head_done, 1)
                dve.wait_ge(head_done, n + 1)
                if n >= 4:
                    dve.wait_ge(low_done, n - 3)
                nc.vector.tensor_tensor(sb.rest[:, n % 4, :], sb.plain[:, n % 4, :], sb.parts[:, n % 4, 0, :],
                                        ALU.subtract).then_inc(rest_done, 1)
                dve.wait_ge(rest_done, n + 1)
                nc.vector.tensor_copy(sb.parts[:, n % 4, 1, :], sb.rest[:, n % 4, :]).then_inc(mid_done, 1)

            def keep_v(v):
                dve.wait_ge(v_done, v + 1)
                nc.vector.tensor_tensor(
                    sb.v[:, 2 * v:2 * v + 2, :], sb.ps[:, 4 + v % 4, :].rearrange("p (a d) -> p a d", a=2),
                    w.bv[:, :].unsqueeze(1).to_broadcast([P, 2, D]), ALU.add).then_inc(v_copied, 1)

            for t in range(TT):
                if layer == 0 and t % QT == 0:
                    dve.wait_ge(ld.x[t // QT], 16)
                nc.vector.bn_stats(sb.stats[:, t, :], sb.x[:, t, :]).then_inc(stats_done, 1)
            for t in range(TT):
                dve.wait_ge(stats_done, t + 1)
                nc.vector.bn_aggr(sb.mv[:, t, :], sb.stats[:, t, :]).then_inc(mv_done, 1)
            dve.wait_ge(mv_done, TT)
            nc.vector.tensor_scalar(sb.rstd[:, :], sb.mv[:, :, 1], EPS, None, ALU.add).then_inc(var_ready, 1)
            if layer == 0:
                dve.wait_ge(ld.mask, 16)
                nc.vector.tensor_scalar(w.mf[:, :], w.m8[:, :].bitcast(U8), 1.0, -NEG, ALU.subtract, ALU.mult).then_inc(mask_kept, 1)
                dve.wait_ge(gates_ready, 1)
                nc.vector.tensor_scalar(sb.gate03[:, :], sb.gates[:, 2:3], 0.3, None, ALU.mult)
            dve.wait_ge(std_ready, 1)
            nc.vector.reciprocal(sb.rstd[:, :], sb.std[:, :]).then_inc(rstd_ready, 1)
            dve.wait_ge(rstd_ready, 1)
            for t in range(TT):
                nc.vector.tensor_scalar(sb.tok[:, t, :], sb.x[:, t, :], sb.mv[:, t, 0:1], sb.rstd[:, t:t + 1],
                                        ALU.subtract, ALU.mult).then_inc(norm_done, 1)
            dve.wait_ge(ld.q, 32)
            nc.vector.tensor_scalar(w.bqk[:, 0, :], w.bqk[:, 0, :], SCALE, None, ALU.mult).then_inc(bq_scaled, 1)
            for n in range(NT):
                cut_parts(n)
                if NK - 3 <= n < NK + 1:
                    keep_v(n - NK + 3)
            if layer == 1:
                dve.wait_ge(ld.mask, 16)
                nc.vector.tensor_scalar(at.bias[:, 0, :, :], at.bias[:, 0, :, :], MASK_C, None, ALU.mult)
            dve.wait_ge(ld.o, 32)
            nc.vector.tensor_scalar(w.bo[:, :], w.bo[:, :], sb.gates[:, layer:layer + 1], None, ALU.mult)
            for v in range(NV // 2, NV):
                keep_v(v)


def attention_phase(nc, sem, sb, at, dram, bias_dram, zeroed, tag):
    per_head_bias = bias_dram is not None
    K = KS + 1 if per_head_bias else KS
    LOADS = 2 * len(Q_PARTS) + (1 if per_head_bias else 0)
    qk_loaded, bias_loaded = at.qk_loaded, at.bias_loaded
    scores_done = sem(tag + "scores_done")
    biased = sem(tag + "biased")
    exp_done = sem(tag + "exp_done")
    turned = sem(tag + "turned")
    kept0, kept1 = sem(tag + "kept0"), sem(tag + "kept1")
    v_ready = sem(tag + "v_ready")
    av_done = sem(tag + "av_done")
    out_kept = sem(tag + "out_kept")
    out_turned = sem(tag + "out_turned")
    sums_ready = sem(tag + "sums_ready")
    out_done = sem(tag + "out_done")
    granted = sem(tag + "granted")
    zeros_ready = sem(tag + "zeros_ready")
    GROUPS = H // HG
    M = HG * B

    def groups(eng, body):
        body(0, True, False)
        with eng.Fori(1, GROUPS - 1) as hg:
            body(hg, False, False)
        body(GROUPS - 1, False, True)

    def before(hg, b):
        return (hg, b - 1) if b else (hg - 1, B - 1)

    def slot(b, j):
        return j + HG * (b % 2) if j < HG - 1 else j

    with nc.Block() as block:
        @block.sync
        def _(sp):
            def body(hg, first, last):
                for j in range(2, HG) if first and per_head_bias else ():
                    load_bias(sp, at, bias_dram, 0, j)
                for b in range(1, B):
                    sp.wait_ge(scores_done, (hg * 4 + b) * 16 + 16)
                    load_qk(sp, at, dram, per_head_bias, hg, b)
                if not last:
                    sp.wait_ge(scores_done, (hg * 4 + 4) * 16 + 16)
                    load_qk(sp, at, dram, per_head_bias, hg + 1, 0)
                    for j in range(HG if per_head_bias else 0):
                        sp.wait_ge(biased, hg * 64 + 4 * (M - HG + j) + 4 + 2)
                        load_bias(sp, at, bias_dram, hg + 1, j)
            groups(sp, body)

        @block.tensor
        def _(pe):
            pe.nop().then_inc(scores_done, 32)

            def scores(hg, m, qts):
                b, j = m % M // HG, m % HG
                for qt in qts:
                    if j == 0 and qt == 0:
                        pe.wait_ge(qk_loaded[b % 2], (hg * 2 + (m // HG) // 2 + 1) * (16 * LOADS))
                    pe.wait_ge(biased, hg * 64 + 4 * m + qt + 1)
                    nc.tensor.matmul(sb.ps[:, qt % 2, :], at.qs[0:K, b % 2, j, qt * P:(qt + 1) * P],
                                     at.ks[0:K, b % 2, j, :], start=True, stop=True).then_inc(scores_done, 1)

            def turn(hg, m, kt):
                if kt == 0:
                    pe.wait_ge(exp_done, hg * 64 + 4 * m + 4 + 4)
                if kt % 2 == 0:
                    pe.wait_ge(kept1 if kt else kept0, hg * M + m + 1)
                for qt in range(QT):
                    last = nc.tensor.transpose(sb.ps[:, 2 + kt, qt * P:(qt + 1) * P],
                                               at.p[m % 4][:, qt, kt * P:(kt + 1) * P], sb.ident[:, :])
                if kt % 2 == 1:
                    last.then_inc(turned, 1)

            def values(hg, b, kt):
                pe.wait_ge(kept1 if kt >= 2 else kept0, hg * M + HG * b + HG + 1)
                if kt == 0:
                    pe.wait_ge(v_ready, hg * B + b + 1)
                    pe.wait_ge(out_kept, hg * B + b + 1)
                for j in range(HG):
                    last = nc.tensor.matmul(sb.ps[VW * j:VW * (j + 1), 6, :], at.vq[:, b % 2, kt, j, :],
                                            at.pT[:, slot(b, j), kt, :], start=(kt == 0), stop=(kt == QT - 1))
                if kt == QT - 1:
                    last.then_inc(av_done, 1)

            def turn_out(hg, b):
                pe.wait_ge(out_kept, hg * B + b + 2)
                pe.wait_ge(out_done, hg * B + b + 1)
                for qt in range(QT):
                    last = nc.tensor.transpose(sb.ps[:, 7, qt * P:(qt + 1) * P], at.oT[:, qt * P:(qt + 1) * P],
                                               sb.ident[:, :])
                last.then_inc(out_turned, 1)

            scores(0, 0, range(QT))
            scores(0, 1, (0, 1))

            def body(hg, first, last):
                for m in range(M):
                    b, j = m // HG, m % HG
                    earlier = not (first and b == 0)
                    next1, next2 = not (last and m + 1 >= M), not (last and m + 2 >= M)
                    if next1:
                        scores(hg, m + 1, (2,))
                    if j == 0 and not (first and b < 2):
                        turn_out(*before(*before(hg, b)))
                        if next1:
                            scores(hg, m + 1, (3,))
                    if earlier:
                        values(*before(hg, b), j)
                    turn(hg, m, 0)
                    if next1 and (j > 0 or (first and b < 2)):
                        scores(hg, m + 1, (3,))
                    turn(hg, m, 1)
                    if next2:
                        scores(hg, m + 2, (0,))
                    turn(hg, m, 2)
                    if next2:
                        scores(hg, m + 2, (1,))
                    turn(hg, m, 3)
                if last:
                    turn_out(hg, B - 2)
                    for kt in range(QT):
                        values(hg, B - 1, kt)
                    turn_out(hg, B - 1)
            groups(pe, body)

        @block.vector
        def _(dve):
            dve.nop().then_inc(biased, 2)
            dve.nop().then_inc(kept1, 1)
            dve.nop().then_inc(out_done, 1)

            def add_bias(hg, m, qts):
                b, j = m % M // HG, m % HG
                for qt in qts:
                    u = 4 * m + qt + 1
                    if per_head_bias and b == 0 and qt == 0:
                        dve.wait_ge(bias_loaded[j], (hg + (m // M + 1)) * 16)
                    dve.wait_ge(scores_done, hg * 64 + (u + 32))
                    dve.wait_ge(exp_done, hg * 64 + u)
                    dve.sem_inc(granted, 1)
                    nc.vector.tensor_tensor_reduce(
                        at.s[:, qt, :], sb.ps[:, qt % 2, :], at.bias[:, j if per_head_bias else 0, qt, :],
                        -1.0, 3.0e38, ALU.add, ALU.min, at.nmax[:, m % 4, qt:qt + 1]).then_inc(biased, 1)

            def keep(hg, m):
                dve.wait_ge(turned, (hg * M + m) * 2 + 2 + 8)
                nc.vector.tensor_copy(at.pT[:, slot(m // HG, m % HG), 2:4, :], sb.ps[:, 4:6, :]).then_inc(kept1, 1)

            def turned_out():
                return sb.ps[:, 7, :].rearrange("p (t j w) -> p t j w", t=QT, j=HG)

            def invert_sums(hg, b):
                dve.wait_ge(out_turned, hg * B + b + 2)
                nc.vector.reciprocal(at.rsum[:, :, :], turned_out()[:, :, :, DH]).then_inc(sums_ready, 1)

            def normalise(hg, b):
                dve.wait_ge(sums_ready, hg * B + b + 1)
                dst = sb.tok[:, b * QT:(b + 1) * QT, :].rearrange("p t (g f) -> p g t f", g=GROUPS)
                nc.vector.tensor_tensor(
                    dst[:, bass.ds(hg, 1), :, :].rearrange("p g t (j d) -> p (g t) j d", j=HG),
                    turned_out()[:, :, :, 0:DH], at.rsum[:, :, :].unsqueeze(3).to_broadcast([P, QT, HG, DH]),
                    ALU.mult).then_inc(out_done, 1)

            add_bias(0, 0, range(QT))
            add_bias(0, 1, (0, 1))

            def body(hg, first, last):
                for m in range(M):
                    b, j = m // HG, m % HG
                    if not (last and m + 1 >= M):
                        add_bias(hg, m + 1, (2,))
                    out_due = j == 0 and not (first and b < 2)
                    if out_due:
                        invert_sums(*before(*before(hg, b)))
                    if not (first and m == 0):
                        keep(hg, m - 1)
                    if out_due:
                        normalise(*before(*before(hg, b)))
                    if not (last and m + 1 >= M):
                        add_bias(hg, m + 1, (3,))
                    if not (last and m + 2 >= M):
                        add_bias(hg, m + 2, (0, 1))
                if last:
                    invert_sums(hg, B - 2)
                    keep(hg, M - 1)
                    normalise(hg, B - 2)
                    invert_sums(hg, B - 1)
                    normalise(hg, B - 1)
            groups(dve, body)

        @block.scalar
        def _(act):
            act.nop().then_inc(exp_done, 4)
            act.nop().then_inc(kept0, 1)
            act.nop().then_inc(out_kept, 1)

            def exps(hg, m, qts):
                for qt in qts:
                    if qt == 0:
                        act.wait_ge(turned, (hg * M + m) * 2 + 2)
                    act.wait_ge(biased, hg * 64 + 4 * m + qt + 1 + 2)
                    nc.scalar.activation(at.p[m % 4][:, qt, :], at.s[:, qt, :], ACT.Exp,
                                         bias=at.nmax[:, m % 4, qt:qt + 1], scale=-1.0).then_inc(exp_done, 1)

            def keep(hg, m):
                act.wait_ge(turned, (hg * M + m) * 2 + 1 + 8)
                nc.scalar.activation(at.pT[:, slot(m // HG, m % HG), 0:2, :], sb.ps[:, 2:4, :], ACT.Copy).then_inc(kept0, 1)

            def keep_out(hg, b):
                act.wait_ge(av_done, hg * B + b + 1 + 2)
                act.wait_ge(out_turned, hg * B + b + 1)
                nc.scalar.activation(at.oT[:, :], sb.ps[:, 6, :], ACT.Copy).then_inc(out_kept, 1)

            exps(0, 0, range(QT))
            exps(0, 1, (0, 1))

            def body(hg, first, last):
                for m in range(M):
                    b, j = m // HG, m % HG
                    if j == 3 and not (first and b == 0):
                        keep_out(*before(hg, b))
                    if not (last and m + 1 >= M):
                        exps(hg, m + 1, (2, 3))
                    keep(hg, m)
                    if not (last and m + 2 >= M):
                        exps(hg, m + 2, (0, 1))
                if last:
                    keep_out(hg, B - 1)
            groups(act, body)

        @block.gpsimd
        def _(pool):
            pool.nop().then_inc(turned, 8)
            pool.nop().then_inc(av_done, 2)
            pool.nop().then_inc(out_turned, 1)
            if zeroed is not None:
                nc.gpsimd.memset(sb.zeros[:, :], 0.0).then_inc(zeros_ready, 1)
                pool.wait_ge(zeros_ready, 1)

            def body(hg, first, last):
                if zeroed is not None:
                    pool.dma_start(dram.xs.rearrange("(g r p) d -> g p r d", g=GROUPS, p=P)[
                        bass.ds(hg, 1), :, :, :].rearrange("g p r d -> (g p) r d"),
                        sb.zeros[:, :].unsqueeze(1).to_broadcast([P, SLOT_TILES // GROUPS, D])).then_inc(zeroed, 16)
                for b in range(B):
                    pool.wait_ge(av_done, hg * B + b + 1)
                    src = sb.v[:, b * QT:(b + 1) * QT, :].rearrange("p t (g f) -> p g t f", g=GROUPS)
                    nc.gpsimd.tensor_copy(
                        at.vq[:, b % 2, :, :, 0:DH],
                        src[:, bass.ds(hg, 1), :, :].rearrange("p g t (j d) -> p (g t) j d", j=HG)).then_inc(v_ready, 1)
            groups(pool, body)


def output_phase(nc, sem, sb, w, tag, load, f, m):
    tok_turned, tok_kept = sem(tag + "tok_turned"), sem(tag + "tok_kept")
    bias_added, proj_done, added = sem(tag + "bias_added"), sem(tag + "proj_done"), sem(tag + "added")
    stats_done, mv_done, var_ready = sem(tag + "stats_done"), sem(tag + "mv_done"), sem(tag + "var_ready")
    std_ready, rstd_ready = sem(tag + "std_ready"), sem(tag + "rstd_ready")
    norm_done, turned, xT_kept = sem(tag + "norm_done"), sem(tag + "turned"), sem(tag + "xT_kept")
    r1_done, r1_kept, r2_done = sem(tag + "r1_done"), sem(tag + "r1_kept"), sem(tag + "r2_done")
    logits_kept, top_done, router_loaded = sem(tag + "logits_kept"), sem(tag + "top_done"), sem(tag + "router_loaded")

    def tile_of(buf, g):
        return buf.rearrange("p (b q) d -> p b q d", q=QT)[:, :, QT - 1 - g, :]

    def turned_tile_of(g):
        return sb.xT[:, :, :].rearrange("p c (b q s) -> p c b q s", b=B, q=QT)[:, :, :, QT - 1 - g, :]

    with nc.Block() as block:
        @block.sync
        def _(sp):
            load(sp, router_loaded)

        @block.tensor
        def _(pe):
            def turn(g, bank):
                for c in range(DC):
                    for b in range(B):
                        last = nc.tensor.transpose(sb.ps[:, bank + c, b * P:(b + 1) * P],
                                                   tile_of(sb.tok, g)[:, b, c * P:(c + 1) * P], sb.ident[:, :])
                return last

            def turn_attention(g):
                if g >= 2:
                    pe.wait_ge(tok_kept, g - 1)
                turn(g, 2 * (g % 2)).then_inc(tok_turned, 1)

            def turn_normed(g):
                pe.wait_ge(norm_done, B * (g + 1))
                if g >= 2:
                    pe.wait_ge(xT_kept, g - 1)
                else:
                    pe.wait_ge(tok_kept, g + 3)
                turn(g, 2 * (g % 2)).then_inc(turned, 1)

            def project(g):
                pe.wait_ge(tok_kept, g + 1)
                for v in range(2):
                    if g >= 2:
                        pe.wait_ge(added, 2 * (g - 2) + v + 1)
                    for i in range(2):
                        for c in range(DC):
                            last = nc.tensor.matmul(sb.ps[:, 4 + 2 * (g % 2) + v, i * D:(i + 1) * D],
                                                    turned_tile_of(g)[:, c, 2 * v + i, :], w.o[:, c, :],
                                                    start=(c == 0), stop=(c == DC - 1))
                    last.then_inc(proj_done, 1)

            def route_hidden():
                pe.wait_ge(xT_kept, 1)
                pe.wait_ge(router_loaded, 64)
                pe.wait_ge(added, 6)
                for c in range(DC):
                    last = nc.tensor.matmul(sb.ps[:, 4, 0:B], f.wp1[:, c, :], turned_tile_of(0)[:, c, :, P - 1],
                                            start=(c == 0), stop=(c == DC - 1))
                last.then_inc(r1_done, 1)

            def gate_logits(g):
                pe.wait_ge(xT_kept, g + 1)
                if g == 0:
                    pe.wait_ge(router_loaded, 16)
                    pe.wait_ge(added, 6)
                for b in range(B):
                    t = QT * b + QT - 1 - g
                    for c in range(DC):
                        last = nc.tensor.matmul(sb.ps[:, 4, t * 16:t * 16 + E1 + 1], turned_tile_of(g)[:, c, b, :],
                                                m.gw[:, c, :], start=(c == 0), stop=(c == DC - 1))
                if g == QT - 1:
                    last.then_inc(m.logits_done, 1)

            turn_attention(0)
            turn_attention(1)
            project(0)
            turn_attention(2)
            project(1)
            turn_attention(3)
            project(2)
            turn_normed(0)
            project(3)
            if f is not None:
                route_hidden()
            turn_normed(1)
            if m is not None:
                gate_logits(0)
            turn_normed(2)
            if m is not None:
                gate_logits(1)
            if f is not None:
                pe.wait_ge(r1_kept, 1)
                nc.tensor.matmul(sb.ps[0:B, 5, 0:E0], f.r1[:, :], f.wp2[:, :], start=True, stop=True).then_inc(r2_done, 1)
            turn_normed(3)
            if m is not None:
                gate_logits(2)
                gate_logits(3)

        @block.gpsimd
        def _(pool):
            for g in range(QT):
                xs = tile_of(sb.x, g)
                nc.gpsimd.tensor_tensor(xs, xs, w.bo[:, :].unsqueeze(1).to_broadcast([P, B, D]),
                                        ALU.add).then_inc(bias_added, 1)

        @block.scalar
        def _(act):
            def banks(g):
                return sb.ps[:, 2 * (g % 2):2 * (g % 2) + 2, :].rearrange("p c (b s) -> p c b s", b=B)

            def keep_attention(g):
                act.wait_ge(tok_turned, g + 1)
                nc.scalar.activation(turned_tile_of(g), banks(g), ACT.Copy).then_inc(tok_kept, 1)

            def root(g):
                act.wait_ge(var_ready, g + 1)
                nc.scalar.activation(sb.std[:, B * g:B * (g + 1)], sb.rstd[:, B * g:B * (g + 1)],
                                     ACT.Sqrt).then_inc(std_ready, 1)

            def keep_normed(g):
                act.wait_ge(turned, g + 1)
                nc.scalar.activation(turned_tile_of(g), banks(g), ACT.Copy).then_inc(xT_kept, 1)

            keep_attention(0)
            keep_attention(1)
            keep_attention(2)
            root(0)
            keep_attention(3)
            root(1)
            keep_normed(0)
            root(2)
            if f is not None:
                act.wait_ge(r1_done, 1)
                nc.scalar.activation(f.r1[:, :], sb.ps[:, 4, 0:B], ACT.Gelu, bias=f.bp1[:, 0:1]).then_inc(r1_kept, 1)
            keep_normed(1)
            root(3)
            keep_normed(2)
            keep_normed(3)

        @block.vector
        def _(dve):
            def add(g):
                dve.wait_ge(bias_added, g + 1)
                for v in range(2):
                    dve.wait_ge(proj_done, 2 * g + v + 1)
                    xs = tile_of(sb.x, g)[:, 2 * v:2 * v + 2, :]
                    nc.vector.scalar_tensor_tensor(xs, sb.ps[:, 4 + 2 * (g % 2) + v, :].rearrange("p (a d) -> p a d", a=2), w.gate, xs,
                                                   ALU.mult, ALU.add).then_inc(added, 1)

            def statistics(g):
                for b in range(B):
                    if b % 2 == 0:
                        dve.wait_ge(added, 2 * g + b // 2 + 1)
                    nc.vector.bn_stats(sb.stats[:, B * g + b, :], tile_of(sb.x, g)[:, b, :]).then_inc(stats_done, 1)
                for b in range(B):
                    dve.wait_ge(stats_done, B * g + b + 1)
                    nc.vector.bn_aggr(sb.mv[:, B * g + b, :], sb.stats[:, B * g + b, :]).then_inc(mv_done, 1)
                dve.wait_ge(mv_done, B * (g + 1))
                nc.vector.tensor_scalar(sb.rstd[:, B * g:B * (g + 1)], sb.mv[:, B * g:B * (g + 1), 1], EPS, None,
                                        ALU.add).then_inc(var_ready, 1)

            def normalise(g):
                dve.wait_ge(std_ready, g + 1)
                nc.vector.reciprocal(sb.rstd[:, B * g:B * (g + 1)], sb.std[:, B * g:B * (g + 1)]).then_inc(rstd_ready, 1)
                dve.wait_ge(rstd_ready, g + 1)
                dve.wait_ge(tok_turned, g + 1)
                for b in range(B):
                    k = B * g + b
                    nc.vector.tensor_scalar(tile_of(sb.tok, g)[:, b, :], tile_of(sb.x, g)[:, b, :], sb.mv[:, k, 0:1],
                                            sb.rstd[:, k:k + 1], ALU.subtract, ALU.mult).then_inc(norm_done, 1)

            for g in range(QT):
                add(g)
                statistics(g)
                if g >= 1:
                    normalise(g - 1)
            normalise(QT - 1)
            if f is not None:
                dve.wait_ge(r2_done, 1)
                nc.vector.tensor_tensor(f.logits[:, :], sb.ps[0:B, 5, 0:E0], f.bp2[:, :], ALU.add).then_inc(logits_kept, 1)
                dve.wait_ge(logits_kept, 1)
                nc.vector.max(f.top[:, :], f.logits[:, :]).then_inc(top_done, 1)
                dve.wait_ge(top_done, 1)
                nc.vector.max_index(f.idx[:, :], f.top[:, :], f.logits[:, :]).then_inc(f.idx_done, 1)
                dve.wait_ge(f.rest_loaded, 32)
                nc.vector.tensor_scalar(f.bo[:, :], f.bo[:, :], sb.gate03[:, 0:1], None, ALU.mult)


def routed_ffn_phase(nc, sem, sb, f, args, prefetch, tag):
    up_done, gelu_done, down_done = sem(tag + "up_done"), sem(tag + "gelu_done"), sem(tag + "down_done")
    down_kept, out_done, added = sem(tag + "down_kept"), sem(tag + "out_done"), sem(tag + "added")
    hid_added = sem(tag + "hid_added")
    FC = F0 // P

    with nc.Block() as block:
        @block.tensor
        def _(pe):
            def up(b, mo):
                n = b * FC + mo
                if mo == 0:
                    pe.wait_ge(f.loaded[b % 2], 64 * (b // 2 + 1))
                if n >= 4:
                    pe.wait_ge(gelu_done, n - 3)
                for c in range(DC):
                    last = nc.tensor.matmul(sb.ps[:, n % 4, :], f.w1[:, b % 2, c, mo * P:(mo + 1) * P],
                                            sb.xT[:, c, b * S:(b + 1) * S], start=(c == 0), stop=(c == DC - 1))
                last.then_inc(up_done, 1)

            def down(b):
                pe.wait_ge(gelu_done, FC * (b + 1))
                for mo in range(DC):
                    if b >= 1:
                        pe.wait_ge(down_kept, DC * (b - 1) + mo + 1)
                    for c in range(FC):
                        last = nc.tensor.matmul(sb.ps[:, 4 + mo, :], f.w2[:, b % 2, c, mo * P:(mo + 1) * P],
                                                f.h[:, b % 2, c, :], start=(c == 0), stop=(c == FC - 1))
                    last.then_inc(down_done, 1)

            def project(b):
                pe.wait_ge(down_kept, DC * (b + 1))
                for v in range(2):
                    if b >= 1:
                        pe.wait_ge(added, 2 * (b - 1) + v + 1)
                    for i in range(2):
                        t = 2 * v + i
                        for c in range(DC):
                            last = nc.tensor.matmul(sb.ps[:, 6 + v, i * D:(i + 1) * D],
                                                    f.rT[:, c, t * P:(t + 1) * P], f.wo[:, c, :],
                                                    start=(c == 0), stop=(c == DC - 1))
                    last.then_inc(out_done, 1)

            for mo in range(FC):
                up(0, mo)
            for b in range(B):
                if b < B - 1:
                    up(b + 1, 0)
                down(b)
                if b < B - 1:
                    up(b + 1, 1)
                project(b)
                for mo in range(2, FC) if b < B - 1 else ():
                    up(b + 1, mo)

        @block.scalar
        def _(act):
            for b in range(B):
                act.wait_ge(f.loaded[b % 2], 64 * (b // 2 + 1))
                for mo in range(FC):
                    n = b * FC + mo
                    act.wait_ge(up_done, n + 1)
                    if b >= 2 and mo == 0:
                        act.wait_ge(down_done, DC * (b - 1))
                    nc.scalar.activation(f.h[:, b % 2, mo, :], sb.ps[:, n % 4, :], ACT.Gelu,
                                         bias=f.b1[:, b % 2, mo:mo + 1]).then_inc(gelu_done, 1)

        @block.vector
        def _(dve):
            for b in range(B):
                for mo in range(DC):
                    dve.wait_ge(down_done, DC * b + mo + 1)
                    if b >= 1 and mo == 0:
                        dve.wait_ge(out_done, 2 * b)
                    nc.vector.tensor_scalar(f.rT[:, mo, :], sb.ps[:, 4 + mo, :], f.b2[:, b % 2, mo:mo + 1], None,
                                            ALU.add).then_inc(down_kept, 1)
                for v in range(2):
                    t = QT * b + 2 * v
                    dve.wait_ge(out_done, 2 * b + v + 1)
                    dve.wait_ge(hid_added, 2 * (2 * b + v + 1))
                    xs = sb.x[:, t:t + 2, :].rearrange("p a d -> p (a d)")
                    nc.vector.scalar_tensor_tensor(xs, sb.ps[:, 6 + v, :], f.gate03, xs,
                                                   ALU.mult, ALU.add).then_inc(added, 1)

        @block.gpsimd
        def _(pool):
            for v in range(TT // 2):
                xs, hs = sb.x[:, 2 * v:2 * v + 2, :], f.gh[:, v % 2, :, :]
                nc.gpsimd.tensor_tensor(xs, xs, f.bo[:, :].unsqueeze(1).to_broadcast([P, 2, D]),
                                        ALU.add).then_inc(hid_added, 1)
                if v >= 2:
                    pool.wait_ge(hid_added, 2 * (v - 1))
                nc.gpsimd.tensor_scalar(hs, sb.tok[:, 2 * v:2 * v + 2, :], f.gate, None, ALU.mult).then_inc(f.scaled, 1)
                pool.wait_ge(f.scaled, v + 1)
                pool.wait_ge(hid_added, 2 * v + 1)
                nc.gpsimd.tensor_tensor(xs, xs, hs, ALU.add).then_inc(hid_added, 1)

        @block.sync
        def _(sp):
            for b in range(2, B):
                sp.wait_ge(down_done, DC * (b - 1))
                sp.wait_ge(down_kept, DC * (b - 1))
                load_routed(sp, f, args, b)
            prefetch(sp)


def load_routed(sp, f, args, b):
    e = sp.value_load(f.idx[b:b + 1, 0:1], min_val=0, max_val=E0 - 1)
    for dst, src in ((f.w1, args["L0_ffn_W1"]), (f.w2, args["L0_ffn_W2"])):
        sp.dma_start(dst[:, b % 2, :, :], src[bass.ds(e, 1), :, :].rearrange("e (c p) f -> (e p) c f", p=P)
                     ).then_inc(f.loaded[b % 2], 16)
    for dst, src in ((f.b1, args["L0_ffn_b1"]), (f.b2, args["L0_ffn_b2"])):
        sp.dma_start(dst[:, b % 2, :], src[bass.ds(e, 1), :, :].rearrange("e p c -> (e p) c")
                     ).then_inc(f.loaded[b % 2], 16)


def mixture_phase(nc, sem, sb, m, args, scr, zeroed, out):
    E, IC, ST = E1, chunks(I1), SLOT_TILES
    UP = B * len(IC)
    logits_kept, exp_done = sem("logits_kept"), sem("scores_exp")
    shared_gate, hot_ready, ranks_done = sem("shared_gate"), sem("hot_ready"), sem("ranks_done")
    slots_ready, scattered = sem("slots_ready"), sem("scattered")
    chain = sem("route_chain")
    half_loaded = m.half_loaded
    experts_loaded = sem("experts_loaded")
    s_up, s_silu, s_prod = sem("shared_up"), sem("shared_silu"), sem("shared_prod")
    s_down, x_added = sem("shared_down"), sem("x_added")
    padded = sem("padded")
    xg_loaded = [sem(f"xg_loaded{i}") for i in range(4)]
    x_turned = sem("x_turned")
    xT_kept = sem("xT_kept")
    up_done = sem("up_done")
    silu_done = sem("silu_done")
    prod_done = sem("prod_done")
    h_turned = sem("h_turned")
    hT_kept = sem("hT_kept")
    down_done = sem("down_done")
    y_kept = sem("y_kept")
    y_stored = [sem(f"y_stored{i}") for i in range(4)]
    y_gathered = [sem(f"y_gathered{b}") for b in range(B)]
    y_added = sem("y_added")
    out_done = sem("out_done")

    def shared_tile(half, b, i):
        return half * UP + b * len(IC) + i

    early_blocks = [(0, b) for b in range(B)] + [(1, b) for b in range(EARLY)]
    late_blocks = [(1, b) for b in range(EARLY, B)]

    def down_bank(half, b, q):
        return 4 + (q if (half, b) in late_blocks else q % 2)

    def tiles(eng, body):
        body(0, True, False)
        with eng.Fori(1, ST // 4 - 1) as it:
            body(it, False, False)
        body(ST // 4 - 1, False, True)

    def step_tiles(last):
        return LAST_STEP if last else 4

    with nc.Block() as block:
        @block.sync
        def _(sp):
            for u in range(4):
                sp.nop().then_inc(y_stored[u], 16)
            for e in range(E):
                sp.dma_start(m.gu[:, e, :, :], args["gate_up"][e].rearrange("(c p) f -> p c f", p=P)
                             ).then_inc(experts_loaded, 16)
            for i, (a, n) in enumerate(IC):
                sp.dma_start(m.dn[0:n, :, i, :], args["down"][0:E, a:a + n, :].rearrange("e p f -> p e f")
                             ).then_inc(experts_loaded, 16)
            sp.wait_ge(scattered, 16 * 2 * TT)

            def slot_tile(buf, it, u):
                return buf.rearrange("(i u p) d -> i u p d", u=4, p=P)[
                    bass.ds(it, 1), u, :, :].rearrange("i p d -> (i p) d")

            def store(it, u):
                sp.wait_ge(y_kept, it * 4 + (u + 1 + 2))
                sp.dma_start(slot_tile(scr.ys, it, u), m.y[:, u, :]).then_inc(y_stored[u], 16)

            def body(it, first, last):
                for u in range(4):
                    if u < step_tiles(last):
                        sp.wait_ge(x_turned, it * 4 + (u + 1))
                        sp.dma_start(m.xg[:, u, :], slot_tile(scr.xs, it, u)).then_inc(xg_loaded[u], 16)
                    if not first:
                        store(it - 1, u)
                for u in range(step_tiles(last) if last else 0):
                    store(it, u)
            tiles(sp, body)
            for b in range(B):
                sp.wait_ge(y_added, 2 * QT * (b + 1))
                sp.wait_ge(x_added, TT + QT * (b + 1))
                sp.dma_start(out[b].rearrange("(t p) d -> p t d", p=P), sb.x[:, b * QT:(b + 1) * QT, :]
                             ).then_inc(out_done, 16)
            sp.wait_ge(out_done, 16 * B)

        @block.gpsimd
        def _(pool):
            nc.gpsimd.memset(m.tri[:, 0, :], 1.0).then_inc(padded, 1)
            pool.wait_ge(padded, 1)
            nc.gpsimd.memset(m.tri[:, 1, :], 1.0).then_inc(padded, 1)
            pool.wait_ge(padded, 2)
            nc.gpsimd.affine_select(out=m.tri[:, 0, :], in_=m.tri[:, 0, :], compare_op=ALU.is_gt, fill=0.0,
                                    base=0, pattern=[[1, P]], channel_multiplier=-1).then_inc(padded, 1)
            pool.wait_ge(padded, 3)
            nc.gpsimd.iota(m.count_i[:, :], pattern=[[1, ST]], base=0, channel_multiplier=0).then_inc(padded, 1)
            pool.wait_ge(padded, 4)
            nc.gpsimd.tensor_copy(m.count[:, :], m.count_i[:, :]).then_inc(padded, 1)
            pool.wait_ge(padded, 5)
            nc.gpsimd.memset(m.hs[:, :, I1:len(IC) * P], 0.0).then_inc(padded, 1)
            pool.nop().then_inc(x_turned, 4)
            pool.wait_ge(zeroed, 16 * (H // HG))
            pool.wait_ge(slots_ready, 1)
            for t in range(TT):
                for c in range(2):
                    pool.indirect_dma_start(
                        out=scr.xs, out_offset=bass.IndirectOffsetOnAxis(ap=m.slot[:, c, t:t + 1], axis=0),
                        in_=sb.tok[:, t, :], in_offset=None).then_inc(scattered, 16)
            for u in range(4):
                pool.wait_ge(y_stored[u], 16 * (1 + ST // 4 - (0 if u < LAST_STEP else 1)))
            for t in range(TT):
                for c in range(2):
                    pool.indirect_dma_start(
                        out=m.yg[c][:, t, :], out_offset=None, in_=scr.ys[0:USED_TILES * P, :],
                        in_offset=bass.IndirectOffsetOnAxis(ap=m.slot[:, c, t:t + 1], axis=0)
                    ).then_inc(y_gathered[t // QT], 16)

        @block.tensor
        def _(pe):
            pe.nop().then_inc(up_done, 2)
            pe.nop().then_inc(h_turned, 2)
            pe.nop().then_inc(down_done, 2)

            def shared_up(half, b):
                for i, (a, n) in enumerate(IC):
                    k = shared_tile(half, b, i)
                    if k >= 2:
                        pe.wait_ge(s_prod, k - 1)
                    for g in range(2):
                        for c in range(DC):
                            last = nc.tensor.matmul(sb.ps[0:n, 2 * (k % 2) + g, :],
                                                    m.sgu[:, half, c, g * I1 + a:g * I1 + a + n],
                                                    sb.xT[:, c, b * S:(b + 1) * S], start=(c == 0), stop=(c == DC - 1))
                    last.then_inc(s_up, 1)

            def shared_down(half, b):
                pe.wait_ge(s_prod, half * UP + (b + 1) * len(IC))
                for q in range(QT):
                    d = half * TT + b * QT + q
                    if (half, b) in late_blocks:
                        pe.wait_ge(x_added, d - 3)
                    elif d >= 2:
                        pe.wait_ge(x_added, d - 1)
                    for i, (a, n) in enumerate(IC):
                        last = nc.tensor.matmul(sb.ps[:, down_bank(half, b, q), 0:D], m.h[0:n, b % 2, i, q * P:(q + 1) * P],
                                                m.sdn[0:n, half, i, :], start=(i == 0), stop=(i == len(IC) - 1))
                    last.then_inc(s_down, 1)

            pe.wait_ge(half_loaded[0], 16 * (1 + len(IC)))
            shared_up(0, 0)
            shared_up(0, 1)
            pe.wait_ge(logits_kept, 1)
            shared_down(0, 0)
            pe.wait_ge(hot_ready, 1)
            pe.wait_ge(padded, 3)
            hot = m.hot[:, 2, :, :].rearrange("p t e -> p (t e)")
            nc.tensor.matmul(sb.ps[:, 6, 0:TT * E], m.tri[:, 0, :], hot, start=True, stop=True)
            nc.tensor.matmul(sb.ps[:, 7, 0:TT * E], m.tri[:, 1, :], hot, start=True, stop=True).then_inc(ranks_done, 1)
            pe.wait_ge(half_loaded[1], 16 * (1 + len(IC)))
            for n in range(2, len(early_blocks)):
                shared_up(*early_blocks[n])
                shared_down(*early_blocks[n - 1])
            shared_down(*early_blocks[-1])

            def turn_x(it, u):
                pe.wait_ge(xg_loaded[u % 4], (it + (u // 4 + 1)) * 16)
                pe.wait_ge(xT_kept, it * 4 + (u + 1))
                for c in range(DC):
                    last = nc.tensor.transpose(sb.ps[:, 4, c * P:(c + 1) * P], m.xg[:, u % 4, c * P:(c + 1) * P],
                                               sb.ident[:, :])
                last.then_inc(x_turned, 1)

            def up(it, u, e):
                pe.wait_ge(xT_kept, it * 4 + (u + 2))
                pe.wait_ge(prod_done, it * 4 + (u + 1))
                for g in range(2):
                    for c in range(DC):
                        last = nc.tensor.matmul(
                            sb.ps[:, 2 * (u % 2) + g, 0:I1], m.xgT[:, u % 2, c, :],
                            m.gu[:, bass.ds(e, 1), c, g * I1:(g + 1) * I1].rearrange("p e f -> p (e f)"),
                            start=(c == 0), stop=(c == DC - 1))
                last.then_inc(up_done, 1)

            def turn_h(it, u):
                pe.wait_ge(prod_done, it * 4 + (u + 3))
                pe.wait_ge(hT_kept, it * 4 + (u + 1))
                for i in range(len(IC)):
                    last = nc.tensor.transpose(sb.ps[:, 5, i * P:(i + 1) * P], m.hs[:, u % 2, i * P:(i + 1) * P],
                                               sb.ident[:, :])
                last.then_inc(h_turned, 1)

            def down(it, u, e):
                pe.wait_ge(hT_kept, it * 4 + (u + 2))
                pe.wait_ge(y_kept, it * 4 + (u + 1))
                for i, (a, n) in enumerate(IC):
                    last = nc.tensor.matmul(sb.ps[:, 6 + u % 2, 0:D], m.hT[0:n, u % 2, i, :],
                                            m.dn[0:n, bass.ds(e, 1), i, :].rearrange("p e f -> p (e f)"),
                                            start=(i == 0), stop=(i == len(IC) - 1))
                last.then_inc(down_done, 1)

            def expert_of(it, u):
                col = m.tile_expert[0:1, :].rearrange("p (i u) -> p i u", u=4)[:, bass.ds(it, 1), u]
                return pe.value_load(col, min_val=0, max_val=E - 1)

            pe.wait_ge(experts_loaded, 16 * (E + len(IC)))
            pe.wait_ge(slots_ready, 1)
            pe.wait_ge(padded, 6)
            pe.wait_ge(s_prod, len(early_blocks) * len(IC))
            pe.wait_ge(x_added, len(early_blocks) * QT)
            turn_x(0, 0)

            def body(it, first, last):
                earlier = None if first else expert_of(it - 1, 3)
                for u in range(step_tiles(last)):
                    expert = expert_of(it, u)
                    if not (first and u == 0):
                        turn_h(it, u - 1)
                    up(it, u, expert)
                    if not (last and u == LAST_STEP - 1):
                        turn_x(it, u + 1)
                    if not (first and u == 0):
                        down(it, u - 1, earlier)
                    earlier = expert
                if last:
                    turn_h(it, LAST_STEP - 1)
                    down(it, LAST_STEP - 1, earlier)
            tiles(pe, body)

            pe.wait_ge(prod_done, USED_TILES + 2)
            pe.wait_ge(hT_kept, USED_TILES + 1)
            shared_up(*late_blocks[0])
            pe.wait_ge(y_kept, USED_TILES + 2)
            for n in range(1, len(late_blocks)):
                shared_up(*late_blocks[n])
                shared_down(*late_blocks[n - 1])
            shared_down(*late_blocks[-1])

        @block.scalar
        def _(act):
            act.nop().then_inc(xT_kept, 1)
            act.nop().then_inc(hT_kept, 1)
            act.wait_ge(chain, 1)
            nc.scalar.activation(m.e[:, :, :], m.e[:, :, :], ACT.Exp).then_inc(exp_done, 1)
            nc.scalar.activation(m.sw[:, :], m.lg[:, :, E], ACT.Sigmoid).then_inc(shared_gate, 1)

            def shared_silu(blocks):
                for half, b in blocks:
                    for i, (a, n) in enumerate(IC):
                        k = shared_tile(half, b, i)
                        act.wait_ge(s_up, k + 1)
                        if k >= 2:
                            act.wait_ge(s_prod, k - 1)
                        nc.scalar.activation(m.g[0:n, k % 2, :], sb.ps[0:n, 2 * (k % 2), :],
                                             ACT.Silu).then_inc(s_silu, 1)

            def keep_x(it, u):
                act.wait_ge(x_turned, it * 4 + (u + 1 + 4))
                act.wait_ge(up_done, it * 4 + (u + 1))
                nc.scalar.activation(m.xgT[:, u % 2, :, :].rearrange("p c s -> p (c s)"), sb.ps[:, 4, 0:D],
                                     ACT.Copy).then_inc(xT_kept, 1)

            def silu(it, u):
                act.wait_ge(up_done, it * 4 + (u + 1 + 2))
                nc.scalar.activation(m.gs[:, u % 2, :], sb.ps[:, 2 * (u % 2), 0:I1], ACT.Silu).then_inc(silu_done, 1)

            def keep_h(it, u):
                act.wait_ge(h_turned, it * 4 + (u + 1 + 2))
                act.wait_ge(down_done, it * 4 + (u + 1))
                nc.scalar.activation(m.hT[:, u % 2, :, :].rearrange("p i s -> p (i s)"),
                                     sb.ps[:, 5, 0:len(IC) * P], ACT.Copy).then_inc(hT_kept, 1)

            shared_silu(early_blocks)
            keep_x(0, 0)

            def body(it, first, last):
                for u in range(step_tiles(last)):
                    if not (first and u == 0):
                        keep_h(it, u - 1)
                    silu(it, u)
                    if not (last and u == LAST_STEP - 1):
                        keep_x(it, u + 1)
                if last:
                    keep_h(it, LAST_STEP - 1)
            tiles(act, body)
            shared_silu(late_blocks)

        @block.vector
        def _(dve):
            dve.nop().then_inc(prod_done, 2)
            dve.nop().then_inc(y_kept, 2)
            steps, adds = [0], [0]

            def link(ins):
                steps[0] += 1
                ins.then_inc(chain, 1)
                dve.wait_ge(chain, steps[0])

            def by_expert(col):
                return col.to_broadcast([P, TT, E])

            def gating():
                lg = sb.ps[:, 4, 0:TT * 16].rearrange("p (t w) -> p t w", w=16)
                dve.wait_ge(m.logits_done, 1)
                nc.vector.tensor_copy(m.lg[:, :, :], lg[:, :, 0:E + 1]).then_inc(logits_kept, 1)
                dve.wait_ge(logits_kept, 1)
                for t in range(TT):
                    last = nc.vector.max(m.top[:, t, :], m.lg[:, t, 0:E])
                last.then_inc(logits_kept, 1)
                dve.wait_ge(logits_kept, 2)
                link(nc.vector.tensor_tensor(m.e[:, :, :], m.lg[:, :, 0:E], by_expert(m.top[:, :, 0:1]), ALU.subtract))
                dve.wait_ge(exp_done, 1)
                link(nc.vector.tensor_reduce(m.sum[:, :], m.e[:, :, :], mybir.AxisListType.X, ALU.add))
                link(nc.vector.reciprocal(m.rsum[:, :], m.sum[:, :]))
                link(nc.vector.tensor_tensor(m.e[:, :, :], m.e[:, :, :], by_expert(m.rsum[:, :].unsqueeze(2)), ALU.mult))
                for t in range(TT):
                    last = nc.vector.max(m.top[:, t, :], m.e[:, t, :])
                link(last)
                for t in range(TT):
                    last = nc.vector.max_index(m.idx[:, t, :], m.top[:, t, :], m.e[:, t, :])
                link(last)
                link(nc.vector.tensor_copy(m.idxf[:, :, :], m.idx[:, :, :]))
                iota = m.count[:, 0:E].unsqueeze(1).to_broadcast([P, TT, E])
                dve.wait_ge(padded, 5)
                for c in range(2):
                    link(nc.vector.tensor_tensor(m.hot[:, c, :, :], iota, by_expert(m.idxf[:, :, c:c + 1]), ALU.is_equal))
                nc.vector.tensor_tensor(m.hot[:, 2, :, :], m.hot[:, 0, :, :], m.hot[:, 1, :, :], ALU.add).then_inc(hot_ready, 1)
                for c in range(2):
                    link(nc.vector.tensor_tensor(m.sel[:, :, :], m.hot[:, c, :, :], m.e[:, :, :], ALU.mult))
                    link(nc.vector.tensor_reduce(m.w[:, c, :], m.sel[:, :, :], mybir.AxisListType.X, ALU.add))
                dve.wait_ge(shared_gate, 1)
                link(nc.vector.tensor_copy(m.w[:, 2, :], m.sw[:, :]))
                link(nc.vector.tensor_scalar(m.w[:, :, :], m.w[:, :, :], m.gate, None, ALU.mult))

            def slots():
                dve.wait_ge(ranks_done, 1)
                tile = [P, TT, E]
                before = sb.ps[:, 6, 0:TT * E].rearrange("p (t e) -> p t e", e=E)
                link(nc.vector.tensor_copy(m.total[:, :, :], sb.ps[:, 7, 0:TT * E].rearrange("p (t e) -> p t e", e=E)))
                for e in range(E):
                    last = nc.vector.tensor_tensor_scan(m.upto[:, :, e], m.tri[:, 1, 0:TT], m.total[:, :, e], 0.0,
                                                        ALU.mult, ALU.add)
                link(last)
                link(nc.vector.tensor_scalar(m.edge[:, :], m.count[:, 0:TT], float(P), None, ALU.mult))
                link(nc.vector.tensor_tensor(m.above[:, :, :], m.upto[:, TT - 1, :].unsqueeze(2).to_broadcast([P, E, TT]),
                                             m.edge[:, :].unsqueeze(1).to_broadcast([P, E, TT]), ALU.is_gt))
                link(nc.vector.tensor_reduce(m.tiles[:, :], m.above[:, :, :], mybir.AxisListType.X, ALU.add))
                link(nc.vector.tensor_tensor_scan(m.ends[:, :], m.tri[:, 1, 0:E], m.tiles[:, :], 0.0, ALU.mult, ALU.add))
                link(nc.vector.tensor_tensor(m.starts[:, :], m.ends[:, :], m.tiles[:, :], ALU.subtract))
                link(nc.vector.tensor_scalar(m.starts[:, :], m.starts[:, :], float(P), None, ALU.mult))
                link(nc.vector.tensor_tensor(m.upto[:, :, :], m.upto[:, :, :], m.total[:, :, :], ALU.subtract))
                link(nc.vector.tensor_tensor(m.upto[:, :, :], m.upto[:, :, :], before, ALU.add))
                link(nc.vector.tensor_tensor(m.upto[:, :, :], m.upto[:, :, :],
                                             m.starts[:, :].unsqueeze(1).to_broadcast(tile), ALU.add))
                for c in range(2):
                    link(nc.vector.tensor_tensor(m.sel[:, :, :], m.hot[:, c, :, :], m.upto[:, :, :], ALU.mult))
                    link(nc.vector.tensor_reduce(m.slotf[:, c, :], m.sel[:, :, :], mybir.AxisListType.X, ALU.add))
                link(nc.vector.tensor_copy(m.slot[:, :, :], m.slotf[:, :, :]))
                link(nc.vector.tensor_tensor(m.past[:, :, :], m.count[:, :].unsqueeze(2).to_broadcast([P, ST, E]),
                                             m.ends[:, :].unsqueeze(1).to_broadcast([P, ST, E]), ALU.is_ge))
                link(nc.vector.tensor_reduce(m.tile_f[:, :], m.past[:, :, :], mybir.AxisListType.X, ALU.add))
                link(nc.vector.tensor_scalar(m.tile_f[:, :], m.tile_f[:, :], float(E - 1), None, ALU.min))
                nc.vector.tensor_copy(m.tile_expert[:, :], m.tile_f[:, :]).then_inc(slots_ready, 1)

            def shared_prod(half, b):
                for i, (a, n) in enumerate(IC):
                    k, g = shared_tile(half, b, i), half * B + b
                    dve.wait_ge(s_silu, k + 1)
                    if i == 0 and g >= 2:
                        dve.wait_ge(s_down, QT * (g - 1))
                    nc.vector.tensor_tensor(m.h[0:n, b % 2, i, :], m.g[0:n, k % 2, :],
                                            sb.ps[0:n, 2 * (k % 2) + 1, :], ALU.mult).then_inc(s_prod, 1)

            def shared_add(half, b):
                for q in range(QT):
                    t = b * QT + q
                    dve.wait_ge(s_down, half * TT + t + 1)
                    nc.vector.scalar_tensor_tensor(sb.x[:, t, :], sb.ps[:, down_bank(half, b, q), 0:D], m.w[:, 2, t:t + 1],
                                                   sb.x[:, t, :], ALU.mult, ALU.add).then_inc(x_added, 1)

            def expert_add(b):
                dve.wait_ge(x_added, b * QT + QT)
                dve.wait_ge(y_gathered[b], 16 * 2 * QT)
                for c in range(2):
                    for q in range(QT):
                        t = b * QT + q
                        if c == 1:
                            dve.wait_ge(y_added, 2 * QT * b + q + 1)
                        nc.vector.scalar_tensor_tensor(sb.x[:, t, :], m.yg[c][:, t, :], m.w[:, c, t:t + 1],
                                                       sb.x[:, t, :], ALU.mult, ALU.add).then_inc(y_added, 1)

            gating()
            shared_prod(0, 0)
            shared_prod(0, 1)
            shared_add(0, 0)
            slots()
            for n in range(2, len(early_blocks)):
                shared_prod(*early_blocks[n])
                shared_add(*early_blocks[n - 1])
            shared_add(*early_blocks[-1])

            def prod(it, u):
                dve.wait_ge(silu_done, it * 4 + (u + 1))
                dve.wait_ge(h_turned, it * 4 + (u + 1))
                nc.vector.tensor_tensor(m.hs[:, u % 2, 0:I1], m.gs[:, u % 2, :], sb.ps[:, 2 * (u % 2) + 1, 0:I1],
                                        ALU.mult).then_inc(prod_done, 1)

            def keep_y(it, u):
                dve.wait_ge(down_done, it * 4 + (u + 1 + 2))
                dve.wait_ge(y_stored[u], (it + 1) * 16)
                nc.vector.tensor_copy(m.y[:, u, :], sb.ps[:, 6 + u % 2, 0:D]).then_inc(y_kept, 1)

            def body(it, first, last):
                for u in range(step_tiles(last)):
                    prod(it, u)
                    if u:
                        keep_y(it, u - 1)
                    elif not first:
                        keep_y(it - 1, 3)
                if last:
                    keep_y(it, LAST_STEP - 1)
            tiles(dve, body)
            shared_prod(*late_blocks[0])
            for n in range(1, len(late_blocks)):
                shared_prod(*late_blocks[n])
                shared_add(*late_blocks[n - 1])
                if n == 1:
                    for b in range(EARLY):
                        expert_add(b)
                dve.wait_ge(x_added, TT + (EARLY + n) * QT)
                expert_add(EARLY + n - 1)
            expert_add(B - 1)
            dve.wait_ge(y_added, 2 * TT)
            shared_add(*late_blocks[-1])


class Names:
    pass


def build(nc, a, out):
    ctx = ExitStack()
    with ctx:
        names = [0]
        layer_sems, used = [ctx.enter_context(ExitStack())], []

        def sem(name):
            used.append(layer_sems[0].enter_context(nc.semaphore(name)))
            return used[-1]

        def buffers(stack):
            def made(name, shape, dt):
                names[0] += 1
                return stack.enter_context(nc.sbuf_tensor(f"{name}_{names[0]}", shape, dt))
            return made

        def dram(name, shape, dt):
            return nc.dram_tensor(name, shape, dt, kind="Internal").ap()

        sb, buf = Names(), buffers(ctx)
        sb.x = buf("x", [P, TT, D], F32)
        sb.tok = buf("tok", [P, TT, D], F32)
        sb.xT = buf("xT", [P, DC, N], F32)
        sb.ident = buf("ident", [P, P], F32)
        sb.stats = buf("stats", [P, TT, 6], F32)
        sb.mv = buf("mv", [P, TT, 2], F32)
        sb.std = buf("std", [P, TT], F32)
        sb.rstd = buf("rstd", [P, TT], F32)
        sb.gates = buf("gates", [P, 4], F32)
        sb.rawg = buf("rawg", [P, 4], F32)
        sb.gate03 = buf("gate03", [P, 1], F32)
        sb.zeros = buf("zeros", [P, D], F32)
        sb.ps = ctx.enter_context(nc.psum_tensor("ps", [P, 8, 512], F32))
        aw = Names()
        aw.o = buf("o", [P, DC, D], F32)
        aw.bo = buf("bo", [P, D], F32)
        scratch = Names()
        scratch.keymask = dram("keymask_scratch", [B, S], BF16)
        scratch.xs = dram("slots_in", [SLOT_TILES * P, D], F32)
        scratch.ys = dram("slots_out", [SLOT_TILES * P, D], F32)
        scratch.qk = [dram(f"qk_scratch{i}", [2, 3, D, N], BF16) for i in range(2)]

        def input_loads(layer):
            ld, made = Names(), lambda name: ctx.enter_context(nc.semaphore(f"L{layer}_{name}_loaded"))
            ld.k, ld.v, ld.q, ld.o, ld.mask, ld.gates = [made(s) for s in ("k", "v", "q", "o", "mask", "gates")]
            ld.x, ld.ctx = [made(f"x{b}") for b in range(B)], [made(f"ctx{b}") for b in range(B)]
            return ld

        def attention_buffers(layer, at, made):
            sb.v = made("v", [P, TT, D], F32)
            at.bias = made("bias", [P, HG if layer == 0 else 1, QT, S], F32)
            at.qs = made("qs", [P, 2, HG, S], BF16)
            at.ks = made("ks", [P, 2, HG, S], BF16)
            at.vq = made("vq", [P, 2, QT, HG, VW], F32)

        def projection_buffers(made):
            aw.qk = made("qk", [P, 2, DC, D], F32)
            aw.v = made("v", [P, DC, D], F32)
            aw.bqk = made("bqk", [P, 2, DC], F32)
            aw.bv = made("bv", [P, D], F32)
            aw.cT = made("cT", [P, DC, N], F32)
            sb.plain = made("plain", [P, 4, S], F32)
            sb.rest = made("rest", [P, 4, S], F32)
            sb.parts = made("parts", [P, 4, 3, S], BF16)
            aw.m8 = made("m8", [B, S // 4], U32)
            aw.mf = made("mf", [B, S], BF16)

        mem, pm, at = ExitStack(), ExitStack(), Names()
        attention_buffers(0, at, buffers(mem))
        projection_buffers(buffers(pm))
        ld = input_loads(0)
        for layer in range(2):
            at.qk_loaded = [sem(f"qk_loaded{i}") for i in range(2)]
            at.bias_loaded = [sem(f"bias_loaded{j}") for j in range(HG)]
            dr = Names()
            dr.qk, dr.keymask, dr.xs = scratch.qk[layer], scratch.keymask, scratch.xs
            projection_phase(nc, sem, sb, aw, at, a, dr, layer, ld, f"p{layer}_")
            pm.close()
            with ExitStack() as am:
                buf = buffers(am)
                at.s = buf("s", [P, QT, S], F32)
                p01 = buf("p", [P, 2, QT, S], F32)
                at.p = [p01[:, i, :, :] for i in range(2)] + [
                    sb.xT[:, i, :].rearrange("p (t k) -> p t k", t=QT) for i in range(2)]
                at.pT = buf("pT", [P, 2 * HG - 1, QT, S], F32)
                at.oT = buf("oT", [P, S], F32)
                at.nmax = buf("nmax", [P, 4, QT], F32)
                at.rsum = buf("rsum", [P, QT, HG], F32)
                zeroed = sem("zeroed") if layer == 1 else None
                attention_phase(nc, sem, sb, at, dr, a["bias"] if layer == 0 else None, zeroed, f"a{layer}_")
            mem.close()
            if layer == 0:
                mem, pm = ExitStack(), ExitStack()
                attention_buffers(1, at, buffers(mem))
                projection_buffers(buffers(pm))
                ld = input_loads(1)
            aw.gate = sb.gates[:, layer:layer + 1]
            with ExitStack() as fm:
                if layer == 0:
                    f, buf = Names(), buffers(fm)
                    f.wp1 = buf("wp1", [P, DC, NAV], F32)
                    f.wp2 = buf("wp2", [P, E0], F32)
                    f.bp1 = buf("bp1", [P, 1], F32)
                    f.bp2 = buf("bp2", [B, E0], F32)
                    f.wo = buf("wo", [P, DC, D], F32)
                    f.bo = buf("bo", [P, D], F32)
                    f.r1 = buf("r1", [P, B], F32)
                    f.logits = buf("logits", [B, E0], F32)
                    f.top = buf("top", [B, E0], F32)
                    f.idx = buf("idx", [B, E0], U32)
                    f.w1 = buf("w1", [P, 2, DC, F0], F32)
                    f.w2 = buf("w2", [P, 2, F0 // P, D], F32)
                    f.b1 = buf("b1", [P, 2, F0 // P], F32)
                    f.b2 = buf("b2", [P, 2, DC], F32)
                    f.h = buf("h", [P, 2, F0 // P, S], F32)
                    f.rT = buf("rT", [P, DC, S], F32)
                    f.gh = buf("gh", [P, 2, 2, D], F32)
                    f.gate, f.gate03, f.scaled = sb.gates[:, 2:3], sb.gate03[:, 0:1], sem("hid_scaled")
                    f.idx_done, f.rest_loaded = sem("idx_done"), sem("rest_loaded")
                    f.loaded = [sem(f"routed_loaded{i}") for i in range(2)]
                    output_phase(nc, sem, sb, aw, "o0_", lambda sp, s: load_router(sp, f, a, s), f, None)

                    def prefetch(sp):
                        load_context(sp, aw, a, 1, ld)
                        load_rest(sp, sb, aw, at, a, 1, ld)
                    routed_ffn_phase(nc, sem, sb, f, a, prefetch, "f_")
                    with nc.Block() as block:
                        @block.sync
                        def _(sp):
                            for s in used[0::4]:
                                sp.sem_clear(s)

                        @block.gpsimd
                        def _(pool):
                            for s in used[1::4]:
                                pool.sem_clear(s)

                        @block.scalar
                        def _(act):
                            for s in used[2::4]:
                                act.sem_clear(s)

                        @block.vector
                        def _(dve):
                            for s in used[3::4]:
                                dve.sem_clear(s)
                    layer_sems[0].close()
                    layer_sems[0] = ctx.enter_context(ExitStack())
                else:
                    m, buf = Names(), buffers(fm)
                    m.gw = buf("gw", [P, DC, E1 + 1], F32)
                    m.lg = buf("lg", [P, TT, E1 + 1], F32)
                    m.top = buf("top", [P, TT, 8], F32)
                    m.e = buf("e", [P, TT, E1], F32)
                    m.sum = buf("sum", [P, TT], F32)
                    m.rsum = buf("rsum", [P, TT], F32)
                    m.idx = buf("idx", [P, TT, 8], U32)
                    m.idxf = buf("idxf", [P, TT, 8], F32)
                    m.hot = buf("hot", [P, 3, TT, E1], F32)
                    m.sel = buf("sel", [P, TT, E1], F32)
                    m.w = buf("w", [P, 3, TT], F32)
                    m.sw = buf("sw", [P, TT], F32)
                    m.tri = buf("tri", [P, 2, P], F32)
                    m.count_i = buf("count_i", [P, SLOT_TILES], I32)
                    m.count = buf("count", [P, SLOT_TILES], F32)
                    m.total = buf("total", [P, TT, E1], F32)
                    m.upto = buf("upto", [P, TT, E1], F32)
                    m.edge = buf("edge", [P, TT], F32)
                    m.above = buf("above", [P, E1, TT], F32)
                    m.tiles = buf("tiles", [P, E1], F32)
                    m.ends = buf("ends", [P, E1], F32)
                    m.starts = buf("starts", [P, E1], F32)
                    m.slotf = buf("slotf", [P, 2, TT], F32)
                    m.slot = buf("slot", [P, 2, TT], U32)
                    m.past = buf("past", [P, SLOT_TILES, E1], F32)
                    m.tile_f = buf("tile_f", [P, SLOT_TILES], F32)
                    m.tile_expert = buf("tile_expert", [P, SLOT_TILES], I32)
                    m.sgu = buf("sgu", [P, 2, DC, 2 * I1], F32)
                    m.sdn = buf("sdn", [P, 2, 3, D], F32)
                    m.gu = buf("gu", [P, E1, DC, 2 * I1], F32)
                    m.dn = buf("dn", [P, E1, 3, D], F32)
                    m.g = buf("g", [P, 2, S], F32)
                    m.h = buf("h", [P, 2, 3, S], F32)
                    m.xg = buf("xg", [P, 4, D], F32)
                    m.xgT = buf("xgT", [P, 2, DC, P], F32)
                    m.gs = buf("gs", [P, 2, I1], F32)
                    m.hs = buf("hs", [P, 2, 3 * P], F32)
                    m.hT = buf("hT", [P, 2, 3, P], F32)
                    m.y = buf("y", [P, 4, D], F32)
                    m.yg = [sb.tok, buf("yg", [P, TT, D], F32)]
                    m.gate = sb.gates[:, 3:4]
                    m.half_loaded = [sem(f"half_loaded{i}") for i in range(2)]
                    m.logits_done = sem("logits_done")
                    output_phase(nc, sem, sb, aw, "o1_", lambda sp, s: load_gate(sp, m, a, s), None, m)
                    mixture_phase(nc, sem, sb, m, a, scratch, zeroed, out)


def load_router(sp, f, a, router_loaded):
    sp.dma_start(f.wp1[:, :, :], a["L0_ffn_Wp1"].rearrange("(c p) n -> p c n", p=P)).then_inc(router_loaded, 16)
    sp.dma_start(f.wp2[:, :], a["L0_ffn_Wp2"]).then_inc(router_loaded, 16)
    sp.dma_start(f.bp1[:, :], a["L0_ffn_bp1"].rearrange("(p a) -> p a", a=1)).then_inc(router_loaded, 16)
    sp.dma_start(f.bp2[:, :], a["L0_ffn_bp2"].partition_broadcast(B)).then_inc(router_loaded, 16)
    sp.dma_start(f.wo[:, :, :], a["L0_ffn_Wo"].rearrange("(c p) n -> p c n", p=P)).then_inc(f.rest_loaded, 16)
    sp.dma_start(f.bo[:, :], a["L0_ffn_bo"].partition_broadcast(P)).then_inc(f.rest_loaded, 16)
    sp.wait_ge(f.idx_done, 1)
    for b in range(2):
        load_routed(sp, f, a, b)


def load_gate(sp, m, a, router_loaded):
    sp.dma_start(m.gw[:, :, :], a["gate_w"].rearrange("(c p) e -> p c e", p=P)).then_inc(router_loaded, 16)
    for half in range(2):
        load_shared(sp, m, a, half)
    sp.wait_ge(router_loaded, 16)


def load_shared(sp, m, a, half):
    sp.dma_start(m.sgu[:, half, :, :], a["gate_up"][E1 + half].rearrange("(c p) f -> p c f", p=P)
                 ).then_inc(m.half_loaded[half], 16)
    for i, (start, n) in enumerate(chunks(I1)):
        sp.dma_start(m.sdn[0:n, half, i, :], a["down"][E1 + half, start:start + n, :]
                     ).then_inc(m.half_loaded[half], 16)


def kernel(**inputs):
    import numpy as _np
    import concourse.bacc as _bacc
    from concourse import mybir as _mybir
    from concourse.bass_utils import run_bass_kernel_spmd as _run

    i = {k: _np.asarray(v) for k, v in inputs.items()}
    gate, up = i["L1_ffn_shared_gate_w"], i["L1_ffn_shared_up_w"]
    down = i["L1_ffn_shared_down_w"]
    gate_up = _np.concatenate([i["L1_ffn_experts_gate_up"]] + [
        _np.concatenate([gate[h * I1:(h + 1) * I1], up[h * I1:(h + 1) * I1]], 0)[None] for h in range(2)], 0)
    downs = _np.concatenate([i["L1_ffn_experts_down"]] + [down[None, :, h * I1:(h + 1) * I1] for h in range(2)], 0)
    laid = {
        "x": i["x"],
        "ctxT": i["ctx_1024"].reshape(N, D).T,
        "keymask": i["mask_BxS2_bk1"].view(_np.uint32),
        "mask": i["mask_SxS2_fk1"],
        "bias": i["L0_xattn_relative_bias"][0],
        "g_xattn": i["g_xattn"], "g_ffn": i["g_ffn"],
        "gate_w": _np.concatenate([i["L1_ffn_gate_w"], i["L1_ffn_shared_expert_gate_w"]], 0).T,
        "gate_up": gate_up.transpose(0, 2, 1),
        "down": downs.transpose(0, 2, 1),
    }
    for n in "qkvo":
        laid[f"L0_xattn_W{n}"] = i[f"L0_xattn_W{n}"].T
        laid[f"L1_xattn_W{n}"] = i[f"L1_xattn_W{n}"]
        for l in range(2):
            laid[f"L{l}_xattn_b{n}"] = i[f"L{l}_xattn_b{n}"]
    for n in ("Wp1", "bp1", "Wp2", "bp2", "W1", "b1", "W2", "b2", "Wo", "bo"):
        laid[f"L0_ffn_{n}"] = i[f"L0_ffn_{n}"]

    for n in ("L0_xattn_bq", "L0_xattn_bk", "L1_xattn_bq", "L1_xattn_bk", "L0_ffn_b1", "L0_ffn_b2"):
        v = laid[n]
        laid[n] = _np.swapaxes(v.reshape(*v.shape[:-1], -1, P), -1, -2)

    nc = _bacc.Bacc("TRN2", target_bir_lowering=False, num_devices=1)
    arrays, args = {}, {}
    for name, v in laid.items():
        v = _np.ascontiguousarray(v)
        arrays[f"in_{name}"] = v
        args[name] = nc.dram_tensor(f"in_{name}", v.shape, _mybir.dt.from_np(v.dtype), kind="ExternalInput").ap()
    out = nc.dram_tensor("out_0", (B, S, D), F32, kind="ExternalOutput").ap()
    build(nc, args, out)
    r = _run(nc, [arrays], core_ids=[0])
    return r.results[0]["out_0"]
```
